# Optimizing a Trainium2 kernel written in Bass

```python
import numpy as np
import jax
import jax.numpy as jnp

def _softmax(x, axis=-1):
    return jax.nn.softmax(x, axis=axis)

def _gelu(x):
    return jax.nn.gelu(x, approximate=True)

def _silu(x):
    return jax.nn.silu(x)

def _sigmoid(x):
    return jax.nn.sigmoid(x)

def _layernorm(x, axis=-1, eps=1e-05):
    m = jnp.mean(x, axis=axis, keepdims=True)
    v = jnp.var(x, axis=axis, keepdims=True)
    return (x - m) / jnp.sqrt(v + eps)

def _scatter_add(tgt, idx, src, axis=0):
    return tgt.at[idx].add(src)

def _segment_sum(src, seg, n):
    return jax.ops.segment_sum(src, seg, n)
kernel_name = 'mk_cond_seq_d2_seqx_r2_f1f0e5'

def setup_inputs(seed: int=0):
    np.random.seed(seed)
    _w = jnp.asarray

    def _rec_inputs():
        import jax
        import jax.numpy as jnp
        _rk = jax.random.key(seed)
        x = 1.648e-05 + 1 * jax.random.normal(jax.random.fold_in(_rk, 1), (4, 1024, 576), jnp.float32)
        _lenS = 1024 - jax.random.randint(jax.random.fold_in(_rk, 7), (4,), 0, max(1, 1024 // 4) + 1, jnp.int32)
        _lenS2 = 1024 - jax.random.randint(jax.random.fold_in(_rk, 8), (4,), 0, max(1, 1024 // 4) + 1, jnp.int32)
        cond_1152 = 0.00914911 + 1.00357 * jax.random.normal(jax.random.fold_in(_rk, 11), (4, 576), jnp.float32)
        return (x, cond_1152)
    x, cond_1152 = _rec_inputs()

    def _L0_cond_setup():
        import jax, jax.numpy as jnp
        import numpy as np
        B, L, C = (8, 512, 576)
        H = 16
        D = C // H
        FF = int(C * 4.0)
        EPS = 1e-06

        def _layernorm(x):
            mu = jnp.mean(x, axis=-1, keepdims=True)
            var = jnp.mean(jnp.square(x - mu), axis=-1, keepdims=True)
            return (x - mu) * jax.lax.rsqrt(var + EPS)

        def _modulate(x, shift, scale):
            return x * (1.0 + scale) + shift

        def _attention(h, W_qkv, b_qkv, W_proj, b_proj):
            b, l, c = h.shape
            qkv = h @ W_qkv + b_qkv
            qkv = qkv.reshape(b, l, 3, H, D)
            q, k, v = (qkv[:, :, 0], qkv[:, :, 1], qkv[:, :, 2])
            scale = D ** (-0.5)
            scores = jnp.einsum('blhd,bmhd->bhlm', q * scale, k)
            attn = jax.nn.softmax(scores, axis=-1)
            o = jnp.einsum('bhlm,bmhd->blhd', attn, v).reshape(b, l, c)
            return o @ W_proj + b_proj
        key = jax.random.key(seed)
        ks = jax.random.split(key, 12)
        s = 0.02
        return {'x': jax.random.normal(ks[0], (B, L, C), jnp.float32), 'c': jax.random.normal(ks[1], (B, 1, C), jnp.float32), 'W_qkv': jax.random.normal(ks[2], (C, 3 * C), jnp.float32) * s, 'b_qkv': jnp.zeros((3 * C,), jnp.float32), 'W_proj': jax.random.normal(ks[3], (C, C), jnp.float32) * s, 'b_proj': jnp.zeros((C,), jnp.float32), 'W_fc1': jax.random.normal(ks[4], (C, FF), jnp.float32) * s, 'b_fc1': jnp.zeros((FF,), jnp.float32), 'W_fc2': jax.random.normal(ks[5], (FF, C), jnp.float32) * s, 'b_fc2': jnp.zeros((C,), jnp.float32), 'W_ada': jax.random.normal(ks[6], (C, 6 * C), jnp.float32) * s, 'b_ada': jnp.zeros((6 * C,), jnp.float32)}
    _L0_cond_all = _L0_cond_setup()
    _L0_cond_in = {k: v for k, v in _L0_cond_all.items() if k in ('W_qkv', 'b_qkv', 'W_proj', 'b_proj', 'W_fc1', 'b_fc1', 'W_fc2', 'b_fc2', 'W_ada', 'b_ada')}
    del _L0_cond_all

    def _L1_cond_setup():
        import jax, jax.numpy as jnp
        import numpy as np
        from jax.scipy.linalg import expm
        N, D, COND_DIM = (576, 64, 576)
        B, T = (16, 512)

        def _rotation(cond, W, b):
            v = jax.nn.silu(cond) @ W.T + b
            iu, ju = jnp.triu_indices(D, k=1)
            A = jnp.zeros((cond.shape[0], D, D), dtype=v.dtype)
            A = A.at[:, iu, ju].set(v).at[:, ju, iu].set(-v)
            return expm(A)
        key = jax.random.key(seed)
        k1, k2, k3, k4, k5 = jax.random.split(key, 5)
        x = jax.random.normal(k1, (B, T, N), dtype=jnp.float32)
        cond = jax.random.normal(k2, (B, COND_DIM), dtype=jnp.float32)
        P = jax.random.normal(k3, (N, D), dtype=jnp.float32)
        n_skew = D * (D - 1) // 2
        bound = 1.0 / np.sqrt(COND_DIM)
        W = jax.random.uniform(k4, (n_skew, COND_DIM), minval=-bound, maxval=bound, dtype=jnp.float32)
        b = jax.random.uniform(k5, (n_skew,), minval=-bound, maxval=bound, dtype=jnp.float32)
        return {'x': x, 'cond': cond, 'P': P, 'W': W, 'b': b}
    _L1_cond_all = _L1_cond_setup()
    _L1_cond_in = {k: v for k, v in _L1_cond_all.items() if k in ('P', 'W', 'b')}
    del _L1_cond_all
    return {'x': x, 'cond_1152': cond_1152, 'L0_cond_W_qkv': _L0_cond_in['W_qkv'], 'L0_cond_b_qkv': _L0_cond_in['b_qkv'], 'L0_cond_W_proj': _L0_cond_in['W_proj'], 'L0_cond_b_proj': _L0_cond_in['b_proj'], 'L0_cond_W_fc1': _L0_cond_in['W_fc1'], 'L0_cond_b_fc1': _L0_cond_in['b_fc1'], 'L0_cond_W_fc2': _L0_cond_in['W_fc2'], 'L0_cond_b_fc2': _L0_cond_in['b_fc2'], 'L0_cond_W_ada': _L0_cond_in['W_ada'], 'L0_cond_b_ada': _L0_cond_in['b_ada'], 'L1_cond_P': _L1_cond_in['P'], 'L1_cond_W': _L1_cond_in['W'], 'L1_cond_b': _L1_cond_in['b']}

def reference(x, cond_1152, L0_cond_W_qkv, L0_cond_b_qkv, L0_cond_W_proj, L0_cond_b_proj, L0_cond_W_fc1, L0_cond_b_fc1, L0_cond_W_fc2, L0_cond_b_fc2, L0_cond_W_ada, L0_cond_b_ada, L1_cond_P, L1_cond_W, L1_cond_b):
    import jax
    import jax.numpy as jnp

    def _L0_cond_ref(x, c, W_qkv, b_qkv, W_proj, b_proj, W_fc1, b_fc1, W_fc2, b_fc2, W_ada, b_ada):
        import jax, jax.numpy as jnp
        import numpy as np
        B, L, C = (8, 512, 576)
        H = 16
        D = C // H
        FF = int(C * 4.0)
        EPS = 1e-06

        def _layernorm(x):
            mu = jnp.mean(x, axis=-1, keepdims=True)
            var = jnp.mean(jnp.square(x - mu), axis=-1, keepdims=True)
            return (x - mu) * jax.lax.rsqrt(var + EPS)

        def _modulate(x, shift, scale):
            return x * (1.0 + scale) + shift

        def _attention(h, W_qkv, b_qkv, W_proj, b_proj):
            b, l, c = h.shape
            qkv = h @ W_qkv + b_qkv
            qkv = qkv.reshape(b, l, 3, H, D)
            q, k, v = (qkv[:, :, 0], qkv[:, :, 1], qkv[:, :, 2])
            scale = D ** (-0.5)
            scores = jnp.einsum('blhd,bmhd->bhlm', q * scale, k)
            attn = jax.nn.softmax(scores, axis=-1)
            o = jnp.einsum('bhlm,bmhd->blhd', attn, v).reshape(b, l, c)
            return o @ W_proj + b_proj
        ada = jax.nn.silu(c) @ W_ada + b_ada
        shift_msa, scale_msa, gate_msa, shift_mlp, scale_mlp, gate_mlp = jnp.split(ada, 6, axis=-1)
        h = _modulate(_layernorm(x), shift_msa, scale_msa)
        x = x + gate_msa * _attention(h, W_qkv, b_qkv, W_proj, b_proj)
        h = _modulate(_layernorm(x), shift_mlp, scale_mlp)
        mlp = jax.nn.gelu(h @ W_fc1 + b_fc1, approximate=True) @ W_fc2 + b_fc2
        x = x + gate_mlp * mlp
        return x

    def _L1_cond_ref(x, cond, P, W, b):
        import jax, jax.numpy as jnp
        import numpy as np
        from jax.scipy.linalg import expm
        N, D, COND_DIM = (576, 64, 576)
        B, T = (16, 512)

        def _rotation(cond, W, b):
            v = jax.nn.silu(cond) @ W.T + b
            iu, ju = jnp.triu_indices(D, k=1)
            A = jnp.zeros((cond.shape[0], D, D), dtype=v.dtype)
            A = A.at[:, iu, ju].set(v).at[:, ju, iu].set(-v)
            return expm(A)
        U, _ = jnp.linalg.qr(P)
        R = _rotation(cond, W, b)
        z = jnp.einsum('btn,nd->btd', x, U)
        z_rot = jnp.einsum('btd,bde->bte', z, R)
        x_rot = x + jnp.einsum('btd,nd->btn', z_rot - z, U)
        return x_rot
    x = _L0_cond_ref(x, cond_1152[:, None, :], L0_cond_W_qkv, L0_cond_b_qkv, L0_cond_W_proj, L0_cond_b_proj, L0_cond_W_fc1, L0_cond_b_fc1, L0_cond_W_fc2, L0_cond_b_fc2, L0_cond_W_ada, L0_cond_b_ada)
    x = _L1_cond_ref(x, cond_1152, L1_cond_P, L1_cond_W, L1_cond_b)
    return x

_drawn_inputs = setup_inputs


def setup_inputs(seed=0):
    import zlib

    import numpy as np

    out = dict(_drawn_inputs(seed))
    spreads = {'L0_cond_b_qkv': (0.0, 0.603),
     'L0_cond_b_proj': (0.0, 0.267),
     'L0_cond_b_fc1': (0.0, 0.437),
     'L0_cond_b_fc2': (0.0, 0.275),
     'L0_cond_b_ada': (0.0, 0.1)}
    factors = {}
    for name, (base, spread) in spreads.items():
        noise = np.random.default_rng([zlib.crc32(name.encode()), seed]).standard_normal(out[name].shape)
        drawn = base * np.exp(spread * noise) if base else spread * noise
        out[name] = jnp.asarray(drawn.astype(out[name].dtype))
    for name, factor in factors.items():
        out[name] = (out[name] * factor).astype(out[name].dtype)
    return out
```

```python
from contextlib import ExitStack

import concourse.bass as bass
from concourse import mybir

F32 = mybir.dt.float32
F32R = mybir.dt.float32r
ALU = mybir.AluOpType
ACT = mybir.ActivationFunctionType
AX = mybir.AxisListType

P = 128
B, L, C = 4, 1024, 576
H = 16
D = C // H
NHEAD = B * H
FF = 4 * C
R = 64
NSKEW = R * (R - 1) // 2
SEC = 6
LN_EPS = 1e-6
FULL = C // P
REM = C - FULL * P
CPAD = (FULL + 1) * P
GT = 512
SUB = GT // P
HALF = C // 2
SHIFT_MSA, SCALE_MSA, GATE_MSA, SHIFT_MLP, SCALE_MLP, GATE_MLP, GB_PROJ, GB_FC2 = range(8)
MOD = (SHIFT_MSA, SCALE_MSA, SHIFT_MLP, SCALE_MLP)

A_TILES = 2 * (FULL + 1)
W_TILES = 2 * FULL + 1
PASSES = [p for k in range(FULL) for p in ((k, k), (FULL + 1 + k, k), (k, FULL + k))]
PASSES += [(FULL, 2 * FULL), (2 * FULL + 1, 2 * FULL)]


def raw(ap):
    return ap.bitcast(F32)


def load_split_weight(eng, dst, src, cols, sem):
    for s in range(2):
        eng.dma_start(raw(dst[:, s * FULL:(s + 1) * FULL, :]),
                      src[s, 0:FULL * P, cols].rearrange("(k p) n -> p k n", p=P)).then_inc(sem, 16)
        eng.dma_start(raw(dst[s * REM:(s + 1) * REM, 2 * FULL, :]), src[s, FULL * P:C, cols]).then_inc(sem, 16)


def wait_alone(eng, sem, value, passed):
    eng.wait_ge(sem, value)
    eng.sem_inc(passed, 1)


def stage_semaphores(nc, ctx, prefix):
    made = []

    def sem(name):
        made.append(ctx.enter_context(nc.semaphore(prefix + name)))
        return made[-1]

    def zero():
        nums = sorted(s.num for s in made)
        starts = [n for n in nums if n - 1 not in nums]
        ends = [n for n in nums if n + 1 not in nums]
        nc.all_engine_barrier()
        for a, z in zip(starts, ends):
            nc.gpsimd.sem_clear(range(a, z + 1))
        nc.all_engine_barrier()

    ctx.callback(zero)
    return sem


def c_slot(half, c):
    return (half * (FULL + 1) + c) % 2


def make_identity(nc, pool, ident, zeroed, made):
    pool.memset(ident[:], 0.0).then_inc(zeroed, 1)
    pool.wait_ge(zeroed, 1)
    pool.affine_select(out=ident[:], in_=ident[:], compare_op=ALU.not_equal, fill=1.0, base=0,
                       pattern=[[-1, P]], channel_multiplier=1).then_inc(made, 1)


def stage_qkv(nc, x, b_qkv, wqkv, mod, q_s, k_s, v_s):
    QKM = 2 * C // P
    QR, VR = 3, 2
    with ExitStack() as ctx:
        sb = lambda n, s, d=F32: ctx.enter_context(nc.sbuf_tensor("q_" + n, s, d))
        ps = lambda n, s: ctx.enter_context(nc.psum_tensor("q_psum_" + n, s, F32))
        sem = stage_semaphores(nc, ctx, "q_")
        passed = sem("passed")
        w = sb("w", [P, W_TILES, 3 * C], F32R)
        bqk = sb("bqk", [P, QKM])
        bv = sb("bv", [P, C])
        ident = sb("ident", [P, P])
        xt = sb("xt", [P, 2, SUB, C])
        xn = sb("xn", [P, 2, SUB, CPAD])
        md = sb("md", [P, 2, len(MOD) * (FULL + 1)])
        stats = sb("stats", [P, SUB, 2, 6])
        mv = sb("mv", [P, 2, SUB, 2])
        small = sb("small", [P, 6, SUB])
        rstd = sb("rstd", [P, 2, SUB])
        shift = sb("shift", [P, 2, SUB])
        ht = sb("ht", [P, 2, A_TILES, GT], F32R)
        hf = sb("hf", [P, FULL + 1, GT])
        qko = sb("qko", [P, QR, 2, GT], F32R)
        vf = sb("vf", [P, VR, C])
        vo = sb("vo", [P, VR, 2, C], F32R)
        pt = ps("pt", [P, 2, GT])
        pqk = ps("pqk", [P, 3, 512])
        pv = ps("pv", [P, 2, 512])

        w_in, zeroed, ident_made = sem("w_in"), sem("zeroed"), sem("ident_made")
        x_in = [sem(f"x_in{i}") for i in range(2)]
        md_in = [sem(f"md_in{i}") for i in range(2)]
        dve_link, var_ready, std_ready, rstd_ready, xn_ready = (
            sem("dve_link"), sem("var_ready"), sem("std_ready"), sem("rstd_ready"), sem("xn_ready"))
        t_ready, hi_ready, full_ready, lo_ready = (
            sem("t_ready"), sem("hi_ready"), sem("full_ready"), sem("lo_ready"))
        qk_ready, qk_hi = sem("qk_ready"), sem("qk_hi")
        qk_lo = [sem(f"qk_lo{i}") for i in range(QR)]
        qk_out = [sem(f"qk_out{i}") for i in range(QR)]
        v_ready, v_hi = sem("v_ready"), sem("v_hi")
        v_full = [sem(f"v_full{i}") for i in range(2)]
        v_lo = [sem(f"v_lo{i}") for i in range(VR)]
        v_out = [sem(f"v_out{i}") for i in range(VR)]
        NK = FULL + 1

        def groups(eng, body):
            with eng.Fori(0, B - 1) as b:
                body(b, 0, False)
                body(b, 1, False)
            body(B - 1, 0, True)
            body(B - 1, 1, True)

        SPLIT = C // P

        def out_count(slot, g):
            return (QKM // QR + (1 if SPLIT % QR == slot else 0)) * g

        with nc.Block() as block:
            @block.sync
            def _(sp):
                def load(b, half):
                    sp.dma_start(xt[:, half], x[bass.ds(b * L + half * GT, GT), :]
                                 .rearrange("(t p) c -> p t c", p=P)).then_inc(x_in[half], 16)
                    sp.dma_start(md[:, half], mod[bass.ds(b, 1)].rearrange("a p n -> (a p) n")) \
                      .then_inc(md_in[half], 16)

                load(0, 0)
                load(0, 1)
                load_split_weight(sp, w, wqkv, slice(0, 3 * C), w_in)
                sp.dma_start(bqk[:], b_qkv[0:2 * C].rearrange("(m p) -> p m", p=P),
                             allow_slow_non_contiguous=True).then_inc(w_in, 16)
                sp.dma_start(bv[:], b_qkv[2 * C:3 * C].rearrange("(a n) -> a n", a=1)
                             .broadcast_to([P, C])).then_inc(w_in, 16)

                def body(b, half, last):
                    g = 2 * b + half
                    if not last:
                        wait_alone(sp, xn_ready, g + 1, passed)
                        sp.wait_ge(lo_ready, NK * (g + 1))
                        load(b + 1, half)
                    for m in range(QKM):
                        sp.wait_ge(qk_lo[m % QR], (QKM // QR) * g + m // QR + 1)
                        for name, r0, r1 in (("q", 0, C), ("k", C, 2 * C)):
                            a, z = max(r0, m * P), min(r1, (m + 1) * P)
                            if a < z:
                                dst = q_s if name == "q" else k_s
                                sp.dma_start(
                                    dst[:, bass.ds(b * C + a - r0, z - a), half * GT:(half + 1) * GT]
                                    .rearrange("s f t -> f s t"),
                                    raw(qko[a - m * P:z - m * P, m % QR])).then_inc(qk_out[m % QR], 16)
                    for t in range(SUB):
                        sp.wait_ge(v_lo[t % VR], (SUB // VR) * g + t // VR + 1)
                        for s in range(2):
                            sp.dma_start(
                                v_s[s, bass.ds(b * H, H), half * GT + t * P:half * GT + (t + 1) * P, :]
                                .rearrange("h t d -> t h d"),
                                raw(vo[:, t % VR, s]).rearrange("p (h d) -> p h d", h=H)) \
                              .then_inc(v_out[t % VR], 16)

                groups(nc.sync, body)
                for m in range(QR):
                    sp.wait_ge(qk_out[m], 16 * out_count(m, 2 * B))
                for t in range(VR):
                    sp.wait_ge(v_out[t], 32 * (SUB // VR) * 2 * B)

            @block.gpsimd
            def _(pool):
                make_identity(nc, pool, ident, zeroed, ident_made)

                def normalise(g, half):
                    if not (isinstance(g, int) and g < 2):
                        pool.wait_ge(t_ready, NK * (g - 1))
                    wait_alone(pool, rstd_ready, g + 1, passed)
                    for t in range(SUB):
                        for a, z, o in ((0, C, 0), (FULL * P, C, C)):
                            i = pool.tensor_scalar(xn[:, half, t, o:o + z - a], xt[:, half, t, a:z],
                                                   rstd[:, half, t:t + 1], shift[:, half, t:t + 1],
                                                   ALU.mult, ALU.add)
                    i.then_inc(xn_ready, 1)

                def lows(g, half):
                    for c in range(NK):
                        pool.wait_ge(hi_ready, NK * g + c + 1)
                        pool.wait_ge(full_ready, NK * g + c + 1)
                        pool.tensor_tensor(ht[:, half, NK + c, :], hf[:, c, :], raw(ht[:, half, c, :]), ALU.subtract) \
                            .then_inc(lo_ready, 1)

                normalise(0, 0)
                lows(0, 0)
                normalise(1, 1)

                def body(b, half, last):
                    g = 2 * b + half
                    if not (last and half == 1):
                        lows(g + 1, 1 - half)
                    if not last:
                        normalise(g + 2, half)
                    for t in range(SUB):
                        pool.wait_ge(v_hi, SUB * g + t + 1)
                        pool.tensor_tensor(vo[:, t % VR, 1], vf[:, t % VR], vo[:, t % VR, 0].bitcast(F32),
                                           ALU.subtract).then_inc(v_lo[t % VR], 1)

                groups(nc.gpsimd, body)

            @block.vector
            def _(dve):
                def link(ins, n):
                    ins.then_inc(dve_link, 1)
                    dve.wait_ge(dve_link, n)

                LINKS = 7

                def row_stats(g, b, half, t):
                    if t == 0:
                        dve.wait_ge(x_in[half], 16 * b + 16)
                    for a in range(2):
                        i = dve.bn_stats(stats[:, t, a], xt[:, half, t, a * HALF:(a + 1) * HALF])
                    if t == SUB - 1:
                        link(i, LINKS * g + 1)

                def statistics(g, half):
                    n = LINKS * g
                    if not (isinstance(g, int) and g < 2):
                        wait_alone(dve, xn_ready, g - 1, passed)
                    for t in range(SUB):
                        i = dve.bn_aggr(mv[:, half, t], stats[:, t].rearrange("p a s -> p (a s)"))
                    link(i, n + 2)
                    ve, std, r0, r2, cor = (small[:, k] for k in range(5))
                    dve.tensor_scalar(ve, mv[:, half, :, 1], LN_EPS, None, ALU.add).then_inc(var_ready, 1)
                    dve.wait_ge(std_ready, g + 1)
                    link(dve.reciprocal(r0, std), n + 3)
                    link(dve.tensor_tensor(r2, r0, r0, ALU.mult), n + 4)
                    link(dve.tensor_tensor(r2, r2, ve, ALU.mult), n + 5)
                    link(dve.tensor_scalar(cor, r2, -0.5, 1.5, ALU.mult, ALU.add), n + 6)
                    link(dve.tensor_tensor(rstd[:, half], r0, cor, ALU.mult), n + 7)
                    dve.scalar_tensor_tensor(shift[:, half], mv[:, half, :, 0], -1.0, rstd[:, half],
                                             ALU.mult, ALU.mult).then_inc(rstd_ready, 1)

                def fulls(g, b, half):
                    for c in range(NK):
                        dve.wait_ge(hi_ready, NK * g + c + 1)
                        if c == 0:
                            dve.wait_ge(md_in[half], 16 * b + 16)
                        if not (isinstance(g, int) and g == 0):
                            dve.wait_ge(lo_ready, NK * (g - 1) + c + 1)
                        dve.tensor_scalar(hf[:, c, :], pt[:, c_slot(half, c), :], md[:, half, NK + c:NK + c + 1],
                                          md[:, half, c:c + 1], ALU.mult, ALU.add).then_inc(full_ready, 1)

                for t in range(SUB):
                    row_stats(0, 0, 0, t)
                statistics(0, 0)
                fulls(0, 0, 0)
                for t in range(SUB):
                    row_stats(1, 0, 1, t)
                statistics(1, 1)
                dve.wait_ge(w_in, 16 * 6)

                def body(b, half, last):
                    g = 2 * b + half
                    if not (last and half == 1):
                        fulls(g + 1, b + half, 1 - half)
                    for m in range(QKM):
                        dve.wait_ge(qk_hi, QKM * g + m + 1)
                        dve.scalar_tensor_tensor(qko[:, m % QR, 1], pqk[:, m % 3], bqk[:, m:m + 1],
                                                 qko[:, m % QR, 0].bitcast(F32), ALU.add, ALU.subtract) \
                           .then_inc(qk_lo[m % QR], 1)
                        if not last and m < SUB:
                            row_stats(g + 2, b + 1, half, m)
                        if not last and m == SUB:
                            statistics(g + 2, half)
                    for t in range(SUB):
                        dve.wait_ge(v_lo[t % VR], (SUB // VR) * g + t // VR)
                        for a in range(2):
                            dve.wait_ge(v_ready, 2 * SUB * g + 2 * t + a + 1)
                            dve.tensor_tensor(vf[:, t % VR, a * HALF:(a + 1) * HALF], pv[:, a, 0:HALF],
                                              bv[:, a * HALF:(a + 1) * HALF], ALU.add) \
                               .then_inc(v_full[a], 1)

                groups(nc.vector, body)

            @block.scalar
            def _(act):
                def root(g):
                    act.wait_ge(var_ready, g + 1)
                    act.activation(small[:, 1], small[:, 0], ACT.Sqrt).then_inc(std_ready, 1)

                def his(g, b, half):
                    for c in range(NK):
                        act.wait_ge(t_ready, NK * g + c + 1)
                        if c == 0:
                            act.wait_ge(md_in[half], 16 * b + 16)
                            if not (isinstance(g, int) and g < 2):
                                act.wait_ge(v_ready, 2 * SUB * (g - 1))
                        act.activation(ht[:, half, c, :], pt[:, c_slot(half, c), :], ACT.Identity,
                                       bias=md[:, half, c:c + 1], scale=md[:, half, NK + c:NK + c + 1]) \
                           .then_inc(hi_ready, 1)

                root(0)
                his(0, 0, 0)
                root(1)
                act.wait_ge(w_in, 16 * 6)

                def body(b, half, last):
                    g = 2 * b + half
                    if not (last and half == 1):
                        his(g + 1, b + half, 1 - half)
                    for m in range(QKM):
                        act.wait_ge(qk_ready, QKM * g + m + 1)
                        act.wait_ge(qk_out[m % QR], 16 * (out_count(m % QR, 1) * g + m // QR
                                                          + (1 if SPLIT % QR == m % QR and m > SPLIT else 0)))
                        act.activation(qko[:, m % QR, 0], pqk[:, m % 3], ACT.Identity,
                                       bias=bqk[:, m:m + 1]).then_inc(qk_hi, 1)
                        if not last and m == SUB:
                            root(g + 2)
                    for t in range(SUB):
                        for a in range(2):
                            act.wait_ge(v_full[a], SUB * g + t + 1)
                        act.wait_ge(v_out[t % VR], 32 * ((SUB // VR) * g + t // VR))
                        act.activation(vo[:, t % VR, 0], vf[:, t % VR], ACT.Copy).then_inc(v_hi, 1)

                groups(nc.scalar, body)

            @block.tensor
            def _(pe):
                pe.wait_ge(ident_made, 1)

                def transposes(g, half):
                    pe.wait_ge(xn_ready, g + 1)
                    for c in range(NK):
                        if not (isinstance(g, int) and g == 0 and c < 2):
                            pe.wait_ge(hi_ready, NK * g + c - 1)
                            pe.wait_ge(full_ready, NK * g + c - 1)
                        for t in range(SUB):
                            i = pe.transpose(pt[:, c_slot(half, c), t * P:(t + 1) * P],
                                             xn[:, half, t, c * P:(c + 1) * P], ident[:])
                        i.then_inc(t_ready, 1)

                transposes(0, 0)
                pe.wait_ge(w_in, 16 * 6)

                def body(b, half, last):
                    g = 2 * b + half
                    if not (last and half == 1):
                        transposes(g + 1, 1 - half)
                    pe.wait_ge(hi_ready, NK * (g + 1))
                    pe.wait_ge(lo_ready, NK * (g + 1))
                    for m in range(QKM):
                        pe.wait_ge(qk_lo[m % QR], (QKM // QR) * g + m // QR)
                        for n, (a, k) in enumerate(PASSES):
                            i = pe.matmul(pqk[:, m % 3], w[:, k, m * P:(m + 1) * P], ht[:, half, a, :],
                                          start=(n == 0), stop=(n == len(PASSES) - 1))
                        i.then_inc(qk_ready, 1)
                    for t in range(SUB):
                        for h in range(2):
                            pe.wait_ge(v_full[h], SUB * g + t)
                            for n, (a, k) in enumerate(PASSES):
                                i = pe.matmul(pv[:, h, 0:HALF], ht[:, half, a, t * P:(t + 1) * P],
                                              w[:, k, 2 * C + h * HALF:2 * C + (h + 1) * HALF],
                                              start=(n == 0), stop=(n == len(PASSES) - 1))
                            i.then_inc(v_ready, 1)

                groups(nc.tensor, body)


def stage_attention(nc, q_s, k_s, v_s, o_t, sums):
    KT = L // P
    LH = L // GT
    STEPS = LH * KT
    AHEAD = 4
    SLOTS = 4
    RING = 8
    SROWS, MROWS = 3 * D, 3 * D + 2
    ONES = 64
    VW = ONES + 1
    SCALE = float(D) ** -0.5
    MAX_STEP = (0, 3, 4, 6, 7, 9, 10, 12)
    TURN_STEP = STEPS - 1
    JOBS = KT + 1
    dve_lo = lambda s: s % 4 == 3
    NDVE = STEPS // 4
    NPOOL = STEPS - NDVE
    LOADS = 8
    with ExitStack() as ctx:
        sb = lambda n, s, d=F32: ctx.enter_context(nc.sbuf_tensor("a_" + n, s, d))
        ps = lambda n, s: ctx.enter_context(nc.psum_tensor("a_psum_" + n, s, F32))
        sem = stage_semaphores(nc, ctx, "a_")
        ident = sb("ident", [P, P])
        qs = sb("qs", [P, SLOTS, L], F32R)
        ks = sb("ks", [P, SLOTS, L], F32R)
        vh = sb("vh", [P, SLOTS, KT, VW], F32R)
        vl = sb("vl", [P, SLOTS, KT, VW], F32R)
        pf = sb("pf", [P, RING, GT])
        ph = sb("ph", [P, RING, GT], F32R)
        pl = sb("pl", [P, RING, GT], F32R)
        mx = sb("mx", [P, 2, KT])
        mxt = sb("mxt", [KT, 2, 2, P], F32R)
        ob = sb("ob", [VW, LH, GT])
        p_s = ps("s", [P, 2, L])
        p_t = ps("t", [P, 2, GT])
        p_o = ps("o", [P, LH, GT])

        zeroed, ident_made, set_up = sem("zeroed"), sem("ident_made"), sem("set_up")
        loaded = [sem(f"loaded{i}") for i in range(SLOTS)]
        max_in = [sem(f"max_in{i}") for i in range(SLOTS)]
        s_ready = sem("s_ready")
        s_free = [sem(f"s_free{i}") for i in range(2)]
        mxt_hi = sem("mxt_hi")
        t_ready = sem("t_ready")
        exp_done = [sem(f"exp_done{i}") for i in range(2)]
        hi_ready, lo_pool, lo_dve = sem("hi_ready"), sem("lo_pool"), sem("lo_dve")
        p_free = sem("p_free")
        o_copied = [sem(f"o_copied{i}") for i in range(LH)]
        o_out = [sem(f"o_out{i}") for i in range(LH)]

        def heads(eng, body):
            n = NHEAD // SLOTS
            with eng.Fori(0, n - 1) as i:
                for u in range(SLOTS):
                    body(SLOTS * i + u, u, i, False)
            for u in range(SLOTS):
                body(SLOTS * (n - 1) + u, u, n - 1, True)

        def bank(u, job):
            return (JOBS * u + job) % 2

        def bank_uses(u, i, job):
            return JOBS * SLOTS // 2 * i + (JOBS * u + job) // 2

        def lo_counts(n_heads, s):
            d = sum(dve_lo(x) for x in range(s + 1))
            return NPOOL * n_heads + s + 1 - d, NDVE * n_heads + d

        with nc.Block() as block:
            @block.sync
            def _(sp):
                def load(hd, u):
                    for t, tile in ((q_s, qs), (k_s, ks)):
                        for r, s in enumerate((0, 1, 0) if t is q_s else (0, 0, 1)):
                            sp.dma_start(raw(tile[r * D:(r + 1) * D, u]),
                                         t[s, bass.ds(hd * D, D), :]).then_inc(loaded[u], 16)
                    for s, tile in enumerate((vh, vl)):
                        sp.dma_start(raw(tile[:, u, :, 0:D]),
                                     v_s[s, bass.ds(hd, 1)].rearrange("a (t p) d -> p (a t) d", p=P)) \
                          .then_inc(loaded[u], 16)

                def put_max(u, i):
                    sp.wait_ge(s_free[bank(u, KT)], bank_uses(u, i, KT) + 1)
                    for s in range(2):
                        sp.dma_start(raw(qs[SROWS + s:SROWS + s + 1, u]).rearrange("o (t c) -> o t c", c=P),
                                     raw(mxt[:, u % 2, s])).then_inc(max_in[u], 16)

                sp.wait_ge(set_up, 4)
                for hd in range(SLOTS - 1):
                    load(hd, hd)
                put_max(0, 0)

                def body(hd, u, i, last):
                    if not (last and u > 0):
                        sp.wait_ge(p_free, RING + STEPS * hd)
                        load(hd + SLOTS - 1, (u + SLOTS - 1) % SLOTS)
                    if not (last and u == SLOTS - 1):
                        put_max((u + 1) % SLOTS, i + (u + 1) // SLOTS)
                    for lh in range(LH):
                        sp.wait_ge(o_copied[lh], hd + 1)
                        sp.dma_start(o_t[bass.ds(hd * D, D), lh * GT:(lh + 1) * GT], ob[0:D, lh]) \
                          .then_inc(o_out[lh], 16)
                        sp.dma_start(sums[bass.ds(hd, 1), lh * GT:(lh + 1) * GT], ob[ONES:VW, lh]) \
                          .then_inc(o_out[lh], 16)

                heads(nc.sync, body)
                for lh in range(LH):
                    sp.wait_ge(o_out[lh], 32 * NHEAD)

            @block.gpsimd
            def _(pool):
                make_identity(nc, pool, ident, zeroed, ident_made)
                pool.wait_ge(ident_made, 1)
                pool.memset(raw(ks[:]), 1.0).then_inc(set_up, 1)

                def body(hd, u, i, last):
                    for s in range(STEPS):
                        if not dve_lo(s):
                            pool.wait_ge(hi_ready, STEPS * hd + s + 1)
                            pool.tensor_tensor(pl[:, s % RING], pf[:, s % RING], raw(ph[:, s % RING]),
                                               ALU.subtract).then_inc(lo_pool, 1)

                heads(nc.gpsimd, body)

            @block.vector
            def _(dve):
                dve.memset(raw(qs[:]), 1.0).then_inc(set_up, 1)
                dve.memset(raw(vl[:]), 0.0).then_inc(set_up, 1)
                dve.memset(raw(vh[:]), 1.0).then_inc(set_up, 1)

                def max_tile(hd, u, t):
                    dve.wait_ge(s_ready, JOBS * hd + t + 1)
                    dve.tensor_reduce(mx[:, u % 2, t:t + 1], p_s[:, bank(u, t)], AX.X, ALU.max) \
                       .then_inc(s_free[bank(u, t)], 1)

                def turn_lo(hd, u):
                    dve.wait_ge(mxt_hi, hd + 1)
                    dve.scalar_tensor_tensor(mxt[:, u % 2, 1], p_s[0:KT, bank(u, KT), 0:P], -1.0,
                                             raw(mxt[:, u % 2, 0]), ALU.mult, ALU.subtract) \
                       .then_inc(s_free[bank(u, KT)], 1)

                def finish(hd, u, lh):
                    dve.wait_ge(p_free, RING + STEPS * hd + KT * (lh + 1))
                    dve.wait_ge(o_out[lh], 32 * hd)
                    dve.tensor_copy(ob[:, lh], p_o[0:VW, lh]).then_inc(o_copied[lh], 1)

                for hd in range(2):
                    for t in range(KT):
                        max_tile(hd, hd, t)
                    if hd == 0:
                        turn_lo(0, 0)

                def body(hd, u, i, last):
                    for s in range(STEPS):
                        if s in MAX_STEP and not (last and u >= SLOTS - 2):
                            max_tile(hd + 2, (u + 2) % SLOTS, MAX_STEP.index(s))
                        if s == 2 and not (last and u == SLOTS - 1):
                            turn_lo(hd + 1, (u + 1) % SLOTS)
                        e = s + 2
                        if dve_lo(e):
                            dve.wait_ge(hi_ready, STEPS * hd + e + 1)
                            dve.tensor_tensor(pl[:, e % RING], pf[:, e % RING], raw(ph[:, e % RING]),
                                              ALU.subtract).then_inc(lo_dve, 1)
                        if s == KT + 1:
                            finish(hd, u, 0)
                    finish(hd, u, 1)

                heads(nc.vector, body)

            @block.scalar
            def _(act):
                def turn_hi(hd, u, puts):
                    act.wait_ge(s_ready, JOBS * (hd + 1))
                    if puts is not None:
                        act.wait_ge(max_in[(u + 2) % SLOTS], 32 * puts)
                    act.activation(mxt[:, u % 2, 0], p_s[0:KT, bank(u, KT), 0:P], ACT.Copy, scale=-1.0) \
                       .then_inc(mxt_hi, 1)

                def exp(hd, s):
                    act.wait_ge(t_ready, STEPS * hd + s + 1)
                    act.wait_ge(p_free, STEPS * hd + s + 1)
                    act.activation(pf[:, s % RING], p_t[:, s % 2], ACT.Exp, scale=SCALE) \
                       .then_inc(exp_done[s % 2], 1)

                def high(hd, s):
                    act.wait_ge(exp_done[s % 2], (STEPS // 2) * hd + s // 2 + 1)
                    act.activation(ph[:, s % RING], pf[:, s % RING], ACT.Copy).then_inc(hi_ready, 1)

                turn_hi(0, 0, None)
                exp(0, 0)

                def body(hd, u, i, last):
                    for s in range(STEPS):
                        if s < STEPS - 1:
                            exp(hd, s + 1)
                        elif not (last and u == SLOTS - 1):
                            exp(hd + 1, 0)
                        high(hd, s)
                        if s == 3 and not (last and u == SLOTS - 1):
                            turn_hi(hd + 1, (u + 1) % SLOTS, i if u == 0 else i + 1)

                heads(nc.scalar, body)

            @block.tensor
            def _(pe):
                pe.sem_inc(p_free, RING)
                pe.wait_ge(ident_made, 1)

                def score_tile(u, i, t):
                    if t == 0:
                        pe.wait_ge(loaded[u], 16 * LOADS * (i + 1))
                    k = bank(u, t)
                    pe.wait_ge(s_free[k], bank_uses(u, i, t))
                    for h in range(L // 512):
                        m = pe.matmul(p_s[:, k, h * 512:(h + 1) * 512], qs[0:SROWS, u, t * P:(t + 1) * P],
                                      ks[0:SROWS, u, h * 512:(h + 1) * 512], start=True, stop=True)
                    m.then_inc(s_ready, 1)

                def turn(u, i):
                    k = bank(u, KT)
                    pe.wait_ge(s_free[1 - k], bank_uses(u, i, KT - 1) + 1)
                    pe.wait_ge(s_free[k], bank_uses(u, i, KT))
                    pe.transpose(p_s[0:KT, k, 0:P], mx[:, u % 2], ident[:]).then_inc(s_ready, 1)

                def scores(hd, u, i, s):
                    lh, t = divmod(s, KT)
                    if s == 0:
                        pe.wait_ge(max_in[u], 32 * (i + 1))
                    pe.wait_ge(exp_done[s % 2], (STEPS // 2) * hd + s // 2)
                    pe.matmul(p_t[:, s % 2], ks[0:MROWS, u, t * P:(t + 1) * P],
                              qs[0:MROWS, u, lh * GT:(lh + 1) * GT], start=True, stop=True) \
                      .then_inc(t_ready, 1)

                def values(hd, u, s):
                    lh, t = divmod(s, KT)
                    if t == 0:
                        pe.wait_ge(o_copied[lh], hd)
                    n_pool, n_dve = lo_counts(hd, s)
                    if dve_lo(s):
                        pe.wait_ge(lo_dve, n_dve)
                    else:
                        pe.wait_ge(lo_pool, n_pool)
                    out = p_o[0:VW, lh]
                    pe.matmul(out, vh[:, u, t], ph[:, s % RING], start=(t == 0), stop=False)
                    pe.matmul(out, vl[:, u, t], ph[:, s % RING], start=False, stop=False)
                    m = pe.matmul(out, vh[:, u, t], pl[:, s % RING], start=False, stop=(t == KT - 1))
                    m.then_inc(p_free, 1)

                for hd in range(2):
                    for t in range(KT):
                        score_tile(hd, 0, t)
                    turn(hd, 0)
                for s in range(AHEAD):
                    scores(0, 0, 0, s)

                def body(hd, u, i, last):
                    for s in range(STEPS):
                        if s + AHEAD < STEPS:
                            scores(hd, u, i, s + AHEAD)
                        elif not (last and u == SLOTS - 1):
                            scores(hd + 1, (u + 1) % SLOTS, i + (u == SLOTS - 1), s + AHEAD - STEPS)
                        values(hd, u, s)
                        if not (last and u >= SLOTS - 2):
                            nxt = ((u + 2) % SLOTS, i + (u + 2) // SLOTS)
                            if s in MAX_STEP:
                                score_tile(*nxt, MAX_STEP.index(s))
                            if s == TURN_STEP:
                                turn(*nxt)

                heads(nc.tensor, body)


def stage_proj(nc, o_t, sums, rsums, x, wproj, ada, mod, x2_s, h2_s):
    NK = FULL + 1
    NG = B * L // GT
    with ExitStack() as ctx:
        sb = lambda n, s, d=F32: ctx.enter_context(nc.sbuf_tensor("p_" + n, s, d))
        ps = lambda n, s: ctx.enter_context(nc.psum_tensor("p_psum_" + n, s, F32))
        sem = stage_semaphores(nc, ctx, "p_")
        passed = sem("passed")
        w = sb("w", [P, W_TILES, C], F32R)
        ident = sb("ident", [P, P])
        heads = sb("heads", [H, C])
        sel = sb("sel", [H, CPAD], F32R)
        rs_flat = sb("rs_flat", [P, NHEAD * L // P])
        rs_f = sb("rs_f", [H, L])
        rs = sb("rs", [H, 2, 2, GT], F32R)
        ot = sb("ot", [P, NK, GT])
        of = sb("of", [P, NK, GT])
        oh = sb("oh", [P, 2, A_TILES, GT], F32R)
        xt = sb("xt", [P, 2, SUB, C])
        gt = sb("gt", [P, 2, 3, C])
        md = sb("md", [P, 2, len(MOD) * NK])
        x2 = sb("x2", [P, 2, SUB, C])
        x2b = sb("x2b", [P, C])
        xn = sb("xn", [P, SUB, CPAD])
        stats = sb("stats", [P, SUB, 2, 6])
        mv = sb("mv", [P, SUB, 2])
        small = sb("small", [P, 5, SUB])
        rstd = sb("rstd", [P, SUB])
        shift = sb("shift", [P, SUB])
        hf = sb("hf", [P, 2, GT])
        ht = sb("ht", [P, A_TILES, GT], F32R)
        p_r = ps("r", [P, 2, GT])
        p_p = ps("p", [P, 2, 2, 512])
        p_t = ps("t", [P, 2, GT])

        w_in, zeroed, ident_made, set_up = sem("w_in"), sem("zeroed"), sem("ident_made"), sem("set_up")
        sums_in, rs_made, rs_out = sem("sums_in"), sem("rs_made"), sem("rs_out")
        rs_in, rs_hi, rs_lo = sem("rs_in"), sem("rs_hi"), sem("rs_lo")
        o_in, r_ready, of_ready, oh_ready, ol_ready = (
            sem("o_in"), sem("r_ready"), sem("of_ready"), sem("oh_ready"), sem("ol_ready"))
        x_in = [sem(f"x_in{i}") for i in range(2)]
        xb_ready, p_ready, gated, x2_ready = sem("xb_ready"), sem("p_ready"), sem("gated"), sem("x2_ready")
        link_done, var_ready, std_ready, rstd_ready = (
            sem("link_done"), sem("var_ready"), sem("std_ready"), sem("rstd_ready"))
        xn_ready, x2b_ready, x2b_out = sem("xn_ready"), sem("x2b_ready"), sem("x2b_out")
        t_ready, hi_ready, full_ready, lo_ready, h_out = (
            sem("t_ready"), sem("hi_ready"), sem("full_ready"), sem("lo_ready"), sem("h_out"))

        def groups(eng, body):
            with eng.Fori(0, B - 1) as b:
                body(2 * b, b, 0, 2)
                body(2 * b + 1, b, 1, 2)
            body(NG - 2, B - 1, 0, 1)
            body(NG - 1, B - 1, 1, 0)

        with nc.Block() as block:
            @block.sync
            def _(sp):
                flat = "h (a n) -> (h a) n"
                sp.dma_start(rs_flat[:], sums.rearrange(flat, n=NHEAD * L // P)).then_inc(sums_in, 16)

                def load_x(g, b, half):
                    sp.dma_start(xt[:, half], x[bass.ds(g * GT, GT), :].rearrange("(t p) c -> p t c", p=P)) \
                      .then_inc(x_in[half], 16)
                    sp.dma_start(gt[:, half, 0], ada[bass.ds(b, 1), GATE_MSA * C:(GATE_MSA + 1) * C]
                                 .broadcast_to([P, C])).then_inc(x_in[half], 16)
                    sp.dma_start(gt[:, half, 1:3], ada[bass.ds(b, 1), GB_PROJ * C:(GB_FC2 + 1) * C]
                                 .broadcast_to([P, 2 * C]).rearrange("p (s c) -> p s c", s=2)) \
                      .then_inc(x_in[half], 16)
                    sp.dma_start(md[:, half], mod[bass.ds(b, 1)].rearrange("a p n -> (a p) n")) \
                      .then_inc(x_in[half], 16)

                def load_o(g, b, half):
                    cols = slice(half * GT, (half + 1) * GT)
                    sp.dma_start(ot[:, 0:FULL], o_t[bass.ds(b * C, FULL * P), cols]
                                 .rearrange("(k p) n -> p k n", p=P)).then_inc(o_in, 16)
                    for r in range(2):
                        sp.dma_start(ot[r * REM:(r + 1) * REM, FULL], o_t[bass.ds(b * C + FULL * P, REM), cols]) \
                          .then_inc(o_in, 16)
                    sp.dma_start(rs_f[:, 0:GT], rsums[bass.ds(b * H, H), cols]).then_inc(o_in, 16)

                load_split_weight(sp, w, wproj, slice(0, C), w_in)
                load_x(0, 0, 0)
                load_x(1, 0, 1)
                sp.wait_ge(rs_made, 1)
                sp.dma_start(rsums.rearrange(flat, n=NHEAD * L // P), rs_flat[:]).then_inc(rs_out, 16)
                sp.wait_ge(rs_out, 16)
                load_o(0, 0, 0)
                sp.wait_ge(of_ready, NK)
                sp.wait_ge(rs_lo, 1)
                load_o(1, 0, 1)

                def body(g, b, half, more):
                    if more == 2:
                        sp.wait_ge(of_ready, NK * (g + 2))
                        sp.wait_ge(rs_lo, g + 2)
                        load_o(g + 2, b + 1, half)
                    for t in range(SUB):
                        sp.wait_ge(x2b_ready, SUB * g + t + 1)
                        sp.dma_start(x2_s[bass.ds(g * GT + t * P, P), :], x2b[:]).then_inc(x2b_out, 16)
                    if more == 2:
                        sp.wait_ge(lo_ready, NK * (g + 1) + 2)
                        sp.wait_ge(x2_ready, g + 1)
                        load_x(g + 2, b + 1, half)
                    sp.wait_ge(lo_ready, NK * (g + 1) + 2)
                    sp.dma_start(h2_s[bass.ds(g, 1)].rearrange("a p k n -> (a p) k n"), raw(ht[:])) \
                      .then_inc(h_out, 16)

                groups(nc.sync, body)
                sp.wait_ge(x2b_out, 16 * SUB * NG)
                sp.wait_ge(h_out, 16 * NG)

            @block.gpsimd
            def _(pool):
                make_identity(nc, pool, ident, zeroed, ident_made)
                pool.wait_ge(ident_made, 1)
                pool.memset(heads[:], 1.0).then_inc(set_up, 1)
                pool.wait_ge(set_up, 1)
                pool.affine_select(out=heads[:], in_=heads[:], compare_op=ALU.is_ge, fill=0.0, base=0,
                                   pattern=[[1, C]], channel_multiplier=-D).then_inc(set_up, 1)
                pool.wait_ge(set_up, 2)
                pool.affine_select(out=heads[:], in_=heads[:], compare_op=ALU.is_ge, fill=0.0, base=D - 1,
                                   pattern=[[-1, C]], channel_multiplier=D).then_inc(set_up, 1)

                def biased_x(g, b, half):
                    pool.wait_ge(x_in[half], 64 * (b + 1))
                    for t in range(SUB):
                        i = pool.tensor_tensor(xt[:, half, t], xt[:, half, t], gt[:, half, 1], ALU.add)
                    i.then_inc(xb_ready, 1)

                biased_x(0, 0, 0)
                biased_x(1, 0, 1)

                def body(g, b, half, more):
                    if not (isinstance(g, int) and g == 0):
                        pool.wait_ge(t_ready, NK * g)
                    wait_alone(pool, rstd_ready, g + 1, passed)
                    for t in range(SUB):
                        for a, z, o in ((0, C, 0), (FULL * P, C, C)):
                            i = pool.tensor_scalar(xn[:, t, o:o + z - a], x2[:, half, t, a:z],
                                                   rstd[:, t:t + 1], shift[:, t:t + 1], ALU.mult, ALU.add)
                    i.then_inc(xn_ready, 1)
                    for t in range(SUB):
                        pool.wait_ge(x2b_out, 16 * (SUB * g + t))
                        pool.tensor_tensor(x2b[:], x2[:, half, t], gt[:, half, 2], ALU.add).then_inc(x2b_ready, 1)
                    for c in range(NK):
                        pool.wait_ge(full_ready, NK * g + c + 3)
                        pool.tensor_tensor(ht[:, NK + c], hf[:, c_slot(half, c)], raw(ht[:, c]), ALU.subtract) \
                            .then_inc(lo_ready, 1)
                    if more == 2:
                        biased_x(g + 2, b + 1, half)

                groups(nc.gpsimd, body)

            @block.vector
            def _(dve):
                dve.sem_inc(lo_ready, 2)
                dve.wait_ge(sums_in, 16)
                dve.reciprocal(rs_flat[:], rs_flat[:]).then_inc(rs_made, 1)
                dve.wait_ge(set_up, 3)
                dve.tensor_copy(sel[:, 0:C], heads[:]).then_inc(set_up, 1)
                dve.tensor_copy(sel[:, C:CPAD], heads[:, FULL * P:C]).then_inc(set_up, 1)

                def operand(g, half, c):
                    if c == 0:
                        dve.wait_ge(rs_hi, g + 1)
                        dve.tensor_tensor(rs[:, half, 1], rs_f[:, 0:GT], raw(rs[:, half, 0]), ALU.subtract) \
                           .then_inc(rs_lo, 1)
                    dve.wait_ge(r_ready, NK * g + c + 1)
                    dve.tensor_tensor(of[:, c], ot[:, c], p_r[:, c_slot(half, c)], ALU.mult) \
                       .then_inc(of_ready, 1)

                def operand_lo(g, half, c):
                    dve.wait_ge(oh_ready, NK * g + c + 1)
                    dve.tensor_tensor(oh[:, half, NK + c], of[:, c], raw(oh[:, half, c]), ALU.subtract) \
                       .then_inc(ol_ready, 1)

                def gate(g, half, t, a):
                    if t == 0 and a == 0:
                        dve.wait_ge(xb_ready, g + 1)
                        if not (isinstance(g, int) and g < 2):
                            dve.wait_ge(x2b_ready, SUB * (g - 1))
                    dve.wait_ge(p_ready, 2 * (SUB * g + t) + a + 1)
                    cols = slice(a * HALF, (a + 1) * HALF)
                    dve.tensor_tensor(x2[:, half, t, cols], p_p[:, t % 2, a, 0:HALF], gt[:, half, 0, cols],
                                      ALU.mult).then_inc(gated, 1)

                def residual(g, half, t):
                    dve.wait_ge(gated, 2 * (SUB * g + t) + 2)
                    i = dve.tensor_tensor(x2[:, half, t], x2[:, half, t], xt[:, half, t], ALU.add)
                    if t == SUB - 1:
                        i.then_inc(x2_ready, 1)

                LINKS = 7

                def statistics(g, half):
                    def link(ins, n):
                        ins.then_inc(link_done, 1)
                        dve.wait_ge(link_done, LINKS * g + n)

                    dve.wait_ge(x2_ready, g + 1)
                    for t in range(SUB):
                        for a in range(2):
                            i = dve.bn_stats(stats[:, t, a], x2[:, half, t, a * HALF:(a + 1) * HALF])
                    i.then_inc(link_done, 1)
                    wait_alone(dve, link_done, LINKS * g + 1, passed)
                    for t in range(SUB):
                        i = dve.bn_aggr(mv[:, t], stats[:, t].rearrange("p a s -> p (a s)"))
                    link(i, 2)
                    ve, std, r0, r2, cor = (small[:, k] for k in range(5))
                    dve.tensor_scalar(ve, mv[:, :, 1], LN_EPS, None, ALU.add).then_inc(var_ready, 1)
                    dve.wait_ge(std_ready, g + 1)
                    link(dve.reciprocal(r0, std), 3)
                    link(dve.tensor_tensor(r2, r0, r0, ALU.mult), 4)
                    link(dve.tensor_tensor(r2, r2, ve, ALU.mult), 5)
                    link(dve.tensor_scalar(cor, r2, -0.5, 1.5, ALU.mult, ALU.add), 6)
                    if not (isinstance(g, int) and g == 0):
                        dve.wait_ge(xn_ready, g)
                    link(dve.tensor_tensor(rstd[:], r0, cor, ALU.mult), 7)
                    dve.scalar_tensor_tensor(shift[:], mv[:, :, 0], -1.0, rstd[:], ALU.mult, ALU.mult) \
                       .then_inc(rstd_ready, 1)

                for g in range(2):
                    for c in range(NK):
                        operand(g, g, c)
                        operand_lo(g, g, c)
                    if g == 0:
                        for t in range(SUB):
                            for a in range(2):
                                gate(0, 0, t, a)
                            residual(0, 0, t)

                def body(g, b, half, more):
                    statistics(g, half)
                    for t in range(SUB):
                        if more >= 1:
                            for a in range(2):
                                gate(g + 1, 1 - half, t, a)
                            residual(g + 1, 1 - half, t)
                        if more == 2:
                            operand(g + 2, half, t)
                            operand_lo(g + 2, half, t)
                    if more == 2:
                        operand(g + 2, half, NK - 1)
                        operand_lo(g + 2, half, NK - 1)
                    for c in range(NK):
                        dve.wait_ge(hi_ready, NK * g + c + 1)
                        dve.wait_ge(lo_ready, NK * g + c + 1)
                        k = 2 * NK + c
                        dve.tensor_scalar(hf[:, c_slot(half, c)], p_t[:, c_slot(half, c)],
                                          md[:, half, k + NK:k + NK + 1], md[:, half, k:k + 1],
                                          ALU.mult, ALU.add).then_inc(full_ready, 1)

                groups(nc.vector, body)

            @block.scalar
            def _(act):
                def operand_hi(g, half):
                    act.wait_ge(o_in, 64 * (g + 1))
                    if not (isinstance(g, int) and g < 2):
                        act.wait_ge(r_ready, NK * (g - 1))
                        act.wait_ge(p_ready, 2 * SUB * (g - 1))
                    act.activation(rs[:, half, 0], rs_f[:, 0:GT], ACT.Copy).then_inc(rs_hi, 1)
                    for c in range(NK):
                        act.wait_ge(of_ready, NK * g + c + 1)
                        act.activation(oh[:, half, c], of[:, c], ACT.Copy).then_inc(oh_ready, 1)

                operand_hi(0, 0)
                operand_hi(1, 1)

                def body(g, b, half, more):
                    act.wait_ge(var_ready, g + 1)
                    act.activation(small[:, 1], small[:, 0], ACT.Sqrt).then_inc(std_ready, 1)
                    if more == 2:
                        operand_hi(g + 2, half)
                    act.wait_ge(h_out, 16 * g)
                    for c in range(NK):
                        act.wait_ge(t_ready, NK * g + c + 1)
                        k = 2 * NK + c
                        act.activation(ht[:, c], p_t[:, c_slot(half, c)], ACT.Identity,
                                       bias=md[:, half, k:k + 1], scale=md[:, half, k + NK:k + NK + 1]) \
                           .then_inc(hi_ready, 1)

                groups(nc.scalar, body)

            @block.tensor
            def _(pe):
                def spread(g, half, c):
                    pe.wait_ge(rs_lo, g + 1)
                    if not (isinstance(g, int) and g == 0 and c < 2):
                        pe.wait_ge(of_ready, NK * g + c - 1)
                    for s in range(2):
                        i = pe.matmul(p_r[:, c_slot(half, c)], sel[:, c * P:(c + 1) * P], rs[:, half, s],
                                      start=(s == 0), stop=(s == 1))
                    i.then_inc(r_ready, 1)

                def project(g, half, t):
                    if t == 0:
                        pe.wait_ge(oh_ready, NK * (g + 1))
                        pe.wait_ge(ol_ready, NK * (g + 1))
                    for a in range(2):
                        if t >= 2 or not (isinstance(g, int) and g == 0):
                            pe.wait_ge(gated, 2 * (SUB * g + t - 2) + a + 1)
                        for n, (k, j) in enumerate(PASSES):
                            i = pe.matmul(p_p[:, t % 2, a, 0:HALF], oh[:, half, k, t * P:(t + 1) * P],
                                          w[:, j, a * HALF:(a + 1) * HALF],
                                          start=(n == 0), stop=(n == len(PASSES) - 1))
                        i.then_inc(p_ready, 1)

                pe.sem_inc(full_ready, 2)
                pe.wait_ge(ident_made, 1)
                pe.wait_ge(set_up, 5)
                for c in range(NK):
                    spread(0, 0, c)
                pe.wait_ge(w_in, 64)
                for t in range(SUB):
                    project(0, 0, t)
                for c in range(NK):
                    spread(1, 1, c)

                def body(g, b, half, more):
                    for t in range(SUB):
                        if more >= 1:
                            project(g + 1, 1 - half, t)
                        if more == 2:
                            spread(g + 2, half, t)
                    if more == 2:
                        spread(g + 2, half, NK - 1)
                    pe.wait_ge(xn_ready, g + 1)
                    for c in range(NK):
                        pe.wait_ge(full_ready, NK * g + c + 1)
                        for t in range(SUB):
                            i = pe.transpose(p_t[:, c_slot(half, c), t * P:(t + 1) * P],
                                             xn[:, t, c * P:(c + 1) * P], ident[:])
                        i.then_inc(t_ready, 1)

                groups(nc.tensor, body)


def stage_mlp(nc, h2_s, x2_s, w1_s, b1, w2_s, gates, x3_s):
    FT = FF // P
    GM = GT // 2
    NT = GM // P
    NG = B * L // GM
    RING = 3
    AHEAD = 2
    with ExitStack() as ctx:
        sb = lambda n, s, d=F32: ctx.enter_context(nc.sbuf_tensor("m_" + n, s, d))
        ps = lambda n, s: ctx.enter_context(nc.psum_tensor("m_psum_" + n, s, F32))
        sem = stage_semaphores(nc, ctx, "m_")
        w1 = sb("w1", [P, W_TILES, FF], F32R)
        w2 = sb("w2", [P, 2, FT, C], F32R)
        bias1 = sb("bias1", [P, FT])
        gt = sb("gt", [P, 2, C])
        ht = sb("ht", [P, 2, A_TILES, GM], F32R)
        af = sb("af", [P, RING, GM])
        ah = sb("ah", [P, RING, GM], F32R)
        al = sb("al", [P, RING, GM], F32R)
        xt = sb("xt", [P, NT, C])
        y = sb("y", [P, NT, C])
        p_h = ps("h", [P, RING, 512])
        p_y = ps("y", [P, NT, 2, 512])

        w1_in, w2_in = sem("w1_in"), sem("w2_in")
        ht_in = [sem(f"ht_in{i}") for i in range(2)]
        gt_in = [sem(f"gt_in{i}") for i in range(2)]
        x_in = [sem(f"x_in{i}") for i in range(NT)]
        h_ready, act_ready, hi_ready, lo_ready, used = (
            sem("h_ready"), sem("act_ready"), sem("hi_ready"), sem("lo_ready"), sem("used"))
        gated, summed = sem("gated"), sem("summed")
        y_out = [sem(f"y_out{i}") for i in range(NT)]

        def groups(eng, body):
            with eng.Fori(0, NG // 2 - 1) as j:
                body(2 * j, j, 0, False)
                body(2 * j + 1, j, 1, False)
            body(NG - 2, NG // 2 - 1, 0, False)
            body(NG - 1, NG // 2 - 1, 1, True)

        with nc.Block() as block:
            @block.sync
            def _(sp):
                def load_h(j, q):
                    sp.dma_start(raw(ht[:, q]), h2_s[bass.ds(j, 1), :, :, q * GM:(q + 1) * GM]
                                 .rearrange("a p k n -> (a p) k n")).then_inc(ht_in[q], 16)

                def load_gate(j, q):
                    sp.dma_start(gt[:, q], gates[bass.ds(j, 1), :].broadcast_to([P, C])).then_inc(gt_in[q], 16)

                def load_x(n, t):
                    sp.dma_start(xt[:, t], x2_s[bass.ds(n * GM + t * P, P), :]).then_inc(x_in[t], 16)

                sp.dma_start(bias1[:], b1.rearrange("(f p) -> p f", p=P),
                             allow_slow_non_contiguous=True).then_inc(w1_in, 16)
                load_h(0, 0)
                load_split_weight(sp, w1, w1_s, slice(0, FF), w1_in)
                for s in range(2):
                    sp.dma_start(raw(w2[:, s]), w2_s[s].rearrange("(f p) n -> p f n", p=P)).then_inc(w2_in, 16)
                load_h(0, 1)
                for q in range(2):
                    load_gate(0, q)
                for t in range(NT):
                    load_x(0, t)

                def body(n, j, q, last):
                    for t in range(NT):
                        sp.wait_ge(summed, NT * n + t + 1)
                        sp.dma_start(x3_s[bass.ds(n * GM + t * P, P), :], y[:, t]).then_inc(y_out[t], 16)
                        if not last:
                            load_x(n + 1, t)
                    if not (isinstance(n, int) and n >= NG - 2):
                        load_h(j + 1, q)
                        load_gate(j + 1, q)

                groups(nc.sync, body)
                for t in range(NT):
                    sp.wait_ge(y_out[t], 16 * NG)

            @block.scalar
            def _(act):
                act.wait_ge(w1_in, 80)

                def activate(n, f):
                    act.wait_ge(h_ready, FT * n + f + 1)
                    act.wait_ge(used, FT * n + f + 1)
                    act.activation(af[:, f % RING], p_h[:, f % RING, 0:GM], ACT.Gelu_apprx_tanh,
                                   bias=bias1[:, f:f + 1]).then_inc(act_ready, 1)

                def body(n, j, q, last):
                    for f in range(FT):
                        activate(n, f)

                groups(nc.scalar, body)

            @block.gpsimd
            def _(pool):
                def body(n, j, q, last):
                    for f in range(FT):
                        pool.wait_ge(hi_ready, FT * n + f + 1)
                        pool.tensor_tensor(al[:, f % RING], af[:, f % RING], raw(ah[:, f % RING]),
                                           ALU.subtract).then_inc(lo_ready, 1)

                groups(nc.gpsimd, body)

            @block.vector
            def _(dve):
                def high(n, f):
                    dve.wait_ge(act_ready, FT * n + f + 1)
                    dve.tensor_copy(ah[:, f % RING], af[:, f % RING]).then_inc(hi_ready, 1)

                for f in range(AHEAD):
                    high(0, f)

                def body(n, j, q, last):
                    for f in range(FT):
                        if f + AHEAD < FT:
                            high(n, f + AHEAD)
                        elif not last:
                            high(n + 1, f + AHEAD - FT)
                    dve.wait_ge(used, RING + FT * (n + 1))
                    dve.wait_ge(gt_in[q], 16 * (j + 1))
                    for t in range(NT):
                        dve.wait_ge(y_out[t], 16 * n)
                        for a in range(2):
                            cols = slice(a * HALF, (a + 1) * HALF)
                            dve.tensor_tensor(y[:, t, cols], p_y[:, t, a, 0:HALF], gt[:, q, cols],
                                              ALU.mult).then_inc(gated, 1)
                    for t in range(NT):
                        dve.wait_ge(x_in[t], 16 * (n + 1))
                        dve.wait_ge(gated, 2 * (NT * n + t) + 2)
                        dve.tensor_tensor(y[:, t], y[:, t], xt[:, t], ALU.add).then_inc(summed, 1)

                groups(nc.vector, body)

            @block.tensor
            def _(pe):
                pe.sem_inc(used, RING)

                def first(n, j, q, f):
                    if f == 0:
                        pe.wait_ge(ht_in[q], 16 * (j + 1))
                    if not (isinstance(n, int) and n == 0 and f < RING):
                        pe.wait_ge(act_ready, FT * n + f + 1 - RING)
                    for i, (a, k) in enumerate(PASSES):
                        m = pe.matmul(p_h[:, f % RING, 0:GM], w1[:, k, f * P:(f + 1) * P], ht[:, q, a],
                                      start=(i == 0), stop=(i == len(PASSES) - 1))
                    m.then_inc(h_ready, 1)

                def second(n, f):
                    pe.wait_ge(lo_ready, FT * n + f + 1)
                    for t in range(NT):
                        for a in range(2):
                            if f == 0:
                                pe.wait_ge(gated, 2 * NT * n)
                            for i, (part, s) in enumerate(((ah, 0), (al, 0), (ah, 1))):
                                m = pe.matmul(p_y[:, t, a, 0:HALF], part[:, f % RING, t * P:(t + 1) * P],
                                              w2[:, s, f, a * HALF:(a + 1) * HALF],
                                              start=(f == 0 and i == 0), stop=(f == FT - 1 and i == 2))
                    m.then_inc(used, 1)

                pe.wait_ge(w1_in, 80)
                for f in range(AHEAD):
                    first(0, 0, 0, f)
                pe.wait_ge(w2_in, 32)

                def body(n, j, q, last):
                    for f in range(FT):
                        if f + AHEAD < FT:
                            first(n, j, q, f + AHEAD)
                        elif not last:
                            first(n + 1, j + q, 1 - q, f + AHEAD - FT)
                        second(n, f)

                groups(nc.tensor, body)


def stage_rotate(nc, x3_s, u_s, rot_s, out):
    NK = FULL + 1
    NG = B * L // GT
    with ExitStack() as ctx:
        sb = lambda n, s, d=F32: ctx.enter_context(nc.sbuf_tensor("r_" + n, s, d))
        ps = lambda n, s: ctx.enter_context(nc.psum_tensor("r_psum_" + n, s, F32))
        sem = stage_semaphores(nc, ctx, "r_")
        ident = sb("ident", [P, P])
        u = sb("u", [P, NK, 2 * R], F32R)
        ro = sb("ro", [P, 2, 2, C], F32R)
        xt = sb("xt", [P, 2, SUB, CPAD])
        xh = sb("xh", [P, 2, NK, GT], F32R)
        xl = sb("xl", [P, 2, NK, GT], F32R)
        z = sb("z", [P, 2, 2, GT], F32R)
        y = sb("y", [P, 2, C])
        p_t = ps("t", [P, 2, GT])
        p_z = ps("z", [P, GT])
        p_y = ps("y", [P, 2, 2, 512])

        u_in, zeroed, ident_made = sem("u_in"), sem("zeroed"), sem("ident_made")
        x_in = [sem(f"x_in{i}") for i in range(2)]
        t_ready, hi_ready, lo_ready = sem("t_ready"), sem("hi_ready"), sem("lo_ready")
        z_ready, z_hi, z_lo = sem("z_ready"), sem("z_hi"), sem("z_lo")
        y_ready, summed = sem("y_ready"), sem("summed")
        y_out = [sem(f"y_out{i}") for i in range(2)]

        def groups(eng, body):
            with eng.Fori(0, B - 1) as b:
                body(2 * b, b, 0, False)
                body(2 * b + 1, b, 1, False)
            body(NG - 2, B - 1, 0, False)
            body(NG - 1, B - 1, 1, True)

        with nc.Block() as block:
            @block.sync
            def _(sp):
                def load(g, b, half):
                    rows = x3_s[bass.ds(g * GT, GT), :].rearrange("(t p) c -> p t c", p=P)
                    sp.dma_start(xt[:, half, :, 0:C], rows).then_inc(x_in[half], 16)
                    sp.dma_start(xt[:, half, :, C:CPAD], rows[:, :, FULL * P:C]).then_inc(x_in[half], 16)
                    for r in range(2):
                        sp.dma_start(raw(ro[r * R:(r + 1) * R, half]), rot_s[bass.ds(b, 1)]
                                     .rearrange("a s r c -> r (a s) c")).then_inc(x_in[half], 16)

                sp.dma_start(raw(u[:]), u_s).then_inc(u_in, 16)
                load(0, 0, 0)
                load(1, 0, 1)

                def body(g, b, half, last):
                    for t in range(SUB):
                        sp.wait_ge(summed, 2 * (SUB * g + t) + 6)
                        sp.dma_start(out[bass.ds(g * GT + t * P, P), :], y[:, t % 2]).then_inc(y_out[t % 2], 16)
                    if not (isinstance(g, int) and g >= NG - 2):
                        load(g + 2, b + 1, half)

                groups(nc.sync, body)
                for t in range(2):
                    sp.wait_ge(y_out[t], 16 * SUB // 2 * NG)

            @block.gpsimd
            def _(pool):
                make_identity(nc, pool, ident, zeroed, ident_made)

            @block.scalar
            def _(act):
                def highs(g, half):
                    for c in range(NK):
                        act.wait_ge(t_ready, NK * g + c + 1)
                        if c == 0 and not (isinstance(g, int) and g < 2):
                            act.wait_ge(z_ready, g - 1)
                        act.activation(xh[:, half, c], p_t[:, c_slot(half, c)], ACT.Copy).then_inc(hi_ready, 1)

                highs(0, 0)

                def body(g, b, half, last):
                    act.wait_ge(z_ready, g + 1)
                    act.wait_ge(y_ready, 2 * SUB * g)
                    act.activation(z[:, half, 0], p_z[:], ACT.Copy).then_inc(z_hi, 1)
                    if not last:
                        highs(g + 1, 1 - half)

                groups(nc.scalar, body)

            @block.vector
            def _(dve):
                def lows(g, half):
                    for c in range(NK):
                        dve.wait_ge(hi_ready, NK * g + c + 1)
                        dve.tensor_tensor(xl[:, half, c], p_t[:, c_slot(half, c)], raw(xh[:, half, c]),
                                          ALU.subtract).then_inc(lo_ready, 1)

                lows(0, 0)

                def body(g, b, half, last):
                    dve.wait_ge(z_hi, g + 1)
                    dve.tensor_tensor(z[:, half, 1], p_z[:], raw(z[:, half, 0]), ALU.subtract).then_inc(z_lo, 1)
                    if not last:
                        lows(g + 1, 1 - half)
                    for t in range(SUB):
                        dve.wait_ge(y_out[t % 2], 16 * (SUB // 2 * g + t // 2))
                        for a in range(2):
                            cols = slice(a * HALF, (a + 1) * HALF)
                            dve.wait_ge(y_ready, 2 * (SUB * g + t) + a + 1)
                            dve.tensor_tensor(y[:, t % 2, cols], p_y[:, t % 2, a, 0:HALF], xt[:, half, t, cols],
                                              ALU.add).then_inc(summed, 1)

                groups(nc.vector, body)

            @block.tensor
            def _(pe):
                def transposes(g, b, half):
                    pe.wait_ge(x_in[half], 64 * (b + 1))
                    for c in range(NK):
                        if c >= 2 or not (isinstance(g, int) and g == 0):
                            pe.wait_ge(lo_ready, NK * g + c - 1)
                        for t in range(SUB):
                            i = pe.transpose(p_t[:, c_slot(half, c), t * P:(t + 1) * P],
                                             xt[:, half, t, c * P:(c + 1) * P], ident[:])
                        i.then_inc(t_ready, 1)

                pe.sem_inc(summed, 4)
                pe.wait_ge(ident_made, 1)
                transposes(0, 0, 0)
                pe.wait_ge(u_in, 16)

                def body(g, b, half, last):
                    pe.wait_ge(lo_ready, NK * (g + 1))
                    pe.wait_ge(z_lo, g)
                    n = 0
                    for part in (xh, xl):
                        for c in range(NK):
                            i = pe.matmul(p_z[:], u[:, c], part[:, half, c], start=(n == 0),
                                          stop=(n == 2 * NK - 1))
                            n += 1
                    i.then_inc(z_ready, 1)
                    if not last:
                        transposes(g + 1, b + half, 1 - half)
                    pe.wait_ge(z_lo, g + 1)
                    for t in range(SUB):
                        for a in range(2):
                            pe.wait_ge(summed, 2 * (SUB * g + t) + a + 1)
                            for n, (s, r) in enumerate(((0, 0), (1, 0), (0, 1))):
                                i = pe.matmul(p_y[:, t % 2, a, 0:HALF], z[:, half, s, t * P:(t + 1) * P],
                                              ro[:, half, r, a * HALF:(a + 1) * HALF],
                                              start=(n == 0), stop=(n == 2))
                            i.then_inc(y_ready, 1)

                groups(nc.tensor, body)


def stage_condition(nc, sct, cond, w_ada, b_ada, b_proj, b_fc2, weights, ada, mod, gates):
    NT = 8
    WT = SEC * C // NT
    BLK = 2592
    RING = 2
    blocks = []
    for src, dst in weights:
        n = src.shape[0] * src.shape[1] // P
        s = src.rearrange("r n -> (r n)").rearrange("(p m) -> p m", p=P)
        d = dst.rearrange("s r n -> s (r n)").rearrange("s (p m) -> p s m", p=P)
        blocks += [(s[:, i:i + BLK], d[:, :, i:i + BLK]) for i in range(0, n, BLK)]
    on_pool = lambda j: j % 3 == 2
    with ExitStack() as ctx:
        sb = lambda n, s, d=F32: ctx.enter_context(nc.sbuf_tensor("c_" + n, s, d))
        ps = lambda n, s: ctx.enter_context(nc.psum_tensor("c_psum_" + n, s, F32))
        sem = stage_semaphores(nc, ctx, "c_")
        ident = sb("ident", [P, P])
        wa = sb("wa", [P, FULL + 1, SEC * C])
        ba = sb("ba", [B, SEC * C])
        bb = sb("bb", [B, 2, C])
        cs = sb("cs", [B, 2, C])
        av = sb("av", [B, 8 * C])
        am = sb("am", [B, len(MOD), CPAD])
        mt = sb("mt", [P, B, len(MOD) * (FULL + 1)])
        wf = sb("wf", [P, RING, BLK])
        ws = sb("ws", [P, RING, 2, BLK], F32R)
        p_c = ps("c", [P, FULL + 1, B])
        p_a = ps("a", [B, 4, 512])
        p_m = ps("m", [P, len(MOD) * (FULL + 1), B])
        zeroed, ident_made = sem("zeroed"), sem("ident_made")
        c_in, wa_in, b_in = sem("c_in"), sem("wa_in"), sem("b_in")
        silu_done, c_turned, sct_ready = sem("silu_done"), sem("c_turned"), sem("sct_ready")
        a_ready, a_summed, bias_gated, am_ready, m_turned, mt_ready = (
            sem("a_ready"), sem("a_summed"), sem("bias_gated"), sem("am_ready"), sem("m_turned"), sem("mt_ready"))
        out_done = sem("out_done")
        wf_in = [sem(f"wf_in{i}") for i in range(RING)]
        ws_out = [sem(f"ws_out{i}") for i in range(RING)]
        w_hi = sem("w_hi")
        w_lo = [sem(f"w_lo{i}") for i in range(2)]

        def lo_count(j, pool):
            return sum(on_pool(i) == pool for i in range(j + 1))

        def chunk_rows(k):
            return P if k < FULL else REM

        with nc.Block() as block:
            @block.sync
            def _(sp):
                sp.dma_start(cs[:, 0], cond).then_inc(c_in, 16)
                for j in range(RING):
                    sp.dma_start(wf[:, j], blocks[j][0]).then_inc(wf_in[j], 16)
                sp.dma_start(wa[:, 0:FULL], w_ada[0:FULL * P].rearrange("(k p) n -> p k n", p=P)).then_inc(wa_in, 16)
                sp.dma_start(wa[0:REM, FULL], w_ada[FULL * P:C]).then_inc(wa_in, 16)
                row = lambda v: v.rearrange("(a n) -> a n", a=1)
                sp.dma_start(ba[:], row(b_ada).broadcast_to([B, SEC * C])).then_inc(b_in, 16)
                sp.dma_start(bb[:, 0], row(b_proj).broadcast_to([B, C])).then_inc(b_in, 16)
                sp.dma_start(bb[:, 1], row(b_fc2).broadcast_to([B, C])).then_inc(b_in, 16)
                for j, (_, dst) in enumerate(blocks):
                    sp.wait_ge(w_lo[on_pool(j)], lo_count(j, on_pool(j)))
                    sp.dma_start(dst, raw(ws[:, j % RING])).then_inc(ws_out[j % RING], 16)
                    if j + RING < len(blocks):
                        sp.dma_start(wf[:, j % RING], blocks[j + RING][0]).then_inc(wf_in[j % RING], 16)
                sp.wait_ge(bias_gated, 2)
                sp.wait_ge(a_summed, NT)
                sp.dma_start(ada, av[:]).then_inc(out_done, 16)
                per = gates.shape[0] // B
                for i in range(per):
                    sp.dma_start(gates.rearrange("(b i) c -> b i c", i=per)[:, i],
                                 av[:, GATE_MLP * C:(GATE_MLP + 1) * C]).then_inc(out_done, 16)
                sp.wait_ge(mt_ready, 1)
                sp.dma_start(mod.rearrange("b p n -> p b n"), mt[:]).then_inc(out_done, 16)
                sp.wait_ge(out_done, 16 * (2 + per))
                for j in range(RING):
                    sp.wait_ge(ws_out[j], 16 * len(range(j, len(blocks), RING)))

            def low(eng, j):
                eng.wait_ge(w_hi, j + 1)
                eng.tensor_tensor(ws[:, j % RING, 1], wf[:, j % RING], raw(ws[:, j % RING, 0]), ALU.subtract) \
                   .then_inc(w_lo[on_pool(j)], 1)

            @block.gpsimd
            def _(pool):
                make_identity(nc, pool, ident, zeroed, ident_made)
                pool.wait_ge(ident_made, 1)
                for j in range(len(blocks)):
                    if on_pool(j):
                        low(pool, j)

            @block.scalar
            def _(act):
                act.wait_ge(c_in, 16)
                act.activation(cs[:, 1], cs[:, 0], ACT.Silu).then_inc(silu_done, 1)
                for j in range(len(blocks)):
                    act.wait_ge(wf_in[j % RING], 16 * (j // RING + 1))
                    act.wait_ge(ws_out[j % RING], 16 * (j // RING))
                    act.activation(ws[:, j % RING, 0], wf[:, j % RING], ACT.Copy).then_inc(w_hi, 1)

            @block.vector
            def _(dve):
                dve.wait_ge(c_turned, 1)
                dve.tensor_copy(sct[:, 0:FULL], p_c[:, 0:FULL]).then_inc(sct_ready, 1)
                dve.tensor_copy(sct[0:REM, FULL], p_c[0:REM, FULL]).then_inc(sct_ready, 1)
                todo = [j for j in range(len(blocks)) if not on_pool(j)]
                first = len(todo) // 2
                for j in todo[:first]:
                    low(dve, j)
                dve.wait_ge(b_in, 48)
                for n in range(NT):
                    dve.wait_ge(a_ready, n + 1)
                    dve.tensor_tensor(av[:, n * WT:(n + 1) * WT], p_a[:, n % 4, 0:WT], ba[:, n * WT:(n + 1) * WT],
                                      ALU.add).then_inc(a_summed, 1)
                dve.wait_ge(a_summed, NT)
                for i, g in enumerate((GATE_MSA, GATE_MLP)):
                    dve.tensor_tensor(av[:, (SEC + i) * C:(SEC + i + 1) * C], av[:, g * C:(g + 1) * C], bb[:, i],
                                      ALU.mult).then_inc(bias_gated, 1)
                for i, s in enumerate(MOD):
                    one = 1.0 if s in (SCALE_MSA, SCALE_MLP) else 0.0
                    for a, z, o in ((0, C, 0), (FULL * P, C, C)):
                        dve.tensor_scalar(am[:, i, o:o + z - a], av[:, s * C + a:s * C + z], one, None, ALU.add) \
                           .then_inc(am_ready, 1)
                dve.wait_ge(m_turned, 1)
                dve.tensor_copy(mt[:].rearrange("p b n -> p n b"), p_m[:]).then_inc(mt_ready, 1)
                for j in todo[first:]:
                    low(dve, j)

            @block.tensor
            def _(pe):
                pe.wait_ge(ident_made, 1)
                pe.wait_ge(silu_done, 1)
                for k in range(FULL + 1):
                    i = pe.transpose(p_c[0:chunk_rows(k), k], cs[:, 1, k * P:k * P + chunk_rows(k)], ident[0:B, 0:B])
                i.then_inc(c_turned, 1)
                pe.wait_ge(sct_ready, 2)
                pe.wait_ge(wa_in, 32)
                for n in range(NT):
                    if n >= 4:
                        pe.wait_ge(a_summed, n - 3)
                    for k in range(FULL + 1):
                        r = chunk_rows(k)
                        i = pe.matmul(p_a[:, n % 4, 0:WT], sct[0:r, k], wa[0:r, k, n * WT:(n + 1) * WT],
                                      start=(k == 0), stop=(k == FULL))
                    i.then_inc(a_ready, 1)
                pe.wait_ge(am_ready, 2 * len(MOD))
                for i in range(len(MOD)):
                    for k in range(FULL + 1):
                        m = pe.transpose(p_m[:, i * (FULL + 1) + k], am[:, i, k * P:(k + 1) * P], ident[0:B, 0:B])
                m.then_inc(m_turned, 1)


def stage_rotation(nc, sct, p_in, w_skew, b_skew, u_s, rot_s):
    SQUARINGS = 16
    TERMS = 4
    TR = NSKEW // 16
    TQ = 4
    with ExitStack() as ctx:
        sb = lambda n, s, d=F32: ctx.enter_context(nc.sbuf_tensor("e_" + n, s, d))
        ps = lambda n, s: ctx.enter_context(nc.psum_tensor("e_psum_" + n, s, F32))
        sem = stage_semaphores(nc, ctx, "e_")
        passed = sem("passed")
        ident = sb("ident", [P, P])
        wr = sb("wr", [TR, 16, C])
        wt = sb("wt", [P, FULL + 1, NSKEW])
        bs = sb("bs", [B, NSKEW])
        v = sb("v", [B, NSKEW])
        up = sb("up", [R, B, R])
        a2 = sb("a2", [R, B, R])
        sa = sb("sa", [R, B, 2, R])
        ex = sb("ex", [R, B, 2, R])
        ts = sb("ts", [R, B, 2, R])
        pp = sb("pp", [P, FULL + 1, R])
        m = sb("m", [R, 2 * R])
        row = sb("row", [R, 2 * R])
        ones = sb("ones", [R, R])
        neg = sb("neg", [R, R])
        upm = sb("upm", [R, R])
        col = sb("col", [R, 8])
        sg = sb("sg", [R, R])
        sq = sb("sq", [R, R])
        lst = sb("lst", [R, R])
        phi = sb("phi", [R, R])
        pt = sb("pt", [R, C])
        qt = sb("qt", [R, C])
        ut = sb("ut", [R, C])
        q = sb("q", [P, FULL + 1, R])
        us = sb("us", [P, FULL + 1, 2 * R], F32R)
        ro = sb("ro", [R, B, 2, C], F32R)
        p_w = ps("w", [P, 2, 512])
        p_v = ps("v", [B, 512])
        p_b = ps("b", [R, 512])
        p_g = ps("g", [R, 512])
        p_s = ps("s", [R, B, 2, 2 * R])
        p_q = ps("q", [P, FULL + 1, R])

        zeroed, ident_made, masks = sem("zeroed"), sem("ident_made"), sem("masks")
        w_in, bs_in, pp_in = sem("w_in"), sem("bs_in"), sem("pp_in")
        w_turned, wt_ready, v_ready, v_done, up_in = (
            sem("w_turned"), sem("wt_ready"), sem("v_ready"), sem("v_done"), sem("up_in"))
        pe_done, dve_done, act_done = sem("pe_done"), sem("dve_done"), sem("act_done")
        row_ready, row_spread, step_done = sem("row_ready"), sem("row_spread"), sem("step_done")
        row2_ready, row2_spread, step2_done = sem("row2_ready"), sem("row2_spread"), sem("step2_done")
        sq_ready, ex_ready = sem("sq_ready"), sem("ex_ready")
        us_hi, us_lo, ro_ready, ro_hi, ro_lo, out_done = (
            sem("us_hi"), sem("us_lo"), sem("ro_ready"), sem("ro_hi"), sem("ro_lo"), sem("out_done"))
        NK = FULL + 1
        rows = lambda k: P if k < FULL else REM
        halves = ((0, HALF), (HALF, C))

        PE_STEPS = ("gram", "l_turned", "p_turned", "q_ready", "q_turned", "gram2", "fix", "top", "u_turned",
                    "a_turned") + tuple(f"taylor{i}" for i in range(1, TERMS))
        DVE_STEPS = ("m_ready", "diag", "diag_sum", "inv_std", "scaled", "lst", "pt", "qt", "q", "phi0", "phi",
                     "qt2", "m2_ready", "sign_diag", "signs", "ut", "a2", "sa", "y0") \
            + tuple(f"{x}{i}" for i in range(1, TERMS) for x in ("sum", "y"))
        pe_at = lambda name: PE_STEPS.index(name) + 1
        dve_at = lambda name: DVE_STEPS.index(name) + 1

        with nc.Block() as block:
            @block.sync
            def _(sp):
                sp.dma_start(wr[:], w_skew.rearrange("(t p) c -> p t c", p=TR)).then_inc(w_in, 16)
                sp.dma_start(pp[:, 0:FULL], p_in[0:FULL * P].rearrange("(k p) n -> p k n", p=P)).then_inc(pp_in, 16)
                sp.dma_start(pp[0:REM, FULL], p_in[FULL * P:C]).then_inc(pp_in, 16)
                sp.dma_start(bs[:], b_skew.rearrange("(a n) -> a n", a=1).broadcast_to([B, NSKEW])).then_inc(bs_in, 16)
                sp.wait_ge(masks, 6)
                sp.wait_ge(v_done, 4)
                off = 0
                for i in range(R - 1):
                    n = R - 1 - i
                    sp.dma_start(up[i:i + 1, :, i + 1:R], v[:, off:off + n], allow_slow_non_contiguous=True) \
                      .then_inc(up_in, 16)
                    off += n
                sp.wait_ge(us_lo, 2)
                sp.dma_start(u_s, raw(us[:])).then_inc(out_done, 16)
                sp.wait_ge(ro_lo, 2 * B)
                sp.dma_start(rot_s.rearrange("b s r c -> r b s c"), raw(ro[:])).then_inc(out_done, 16)
                sp.wait_ge(out_done, 32)

            @block.gpsimd
            def _(pool):
                make_identity(nc, pool, ident, zeroed, ident_made)
                pool.wait_ge(ident_made, 1)
                pool.memset(neg[:], -1.0).then_inc(masks, 1)
                pool.memset(sq[:], 1.0).then_inc(masks, 1)
                pool.wait_ge(masks, 2)
                pool.affine_select(out=neg[:], in_=neg[:], compare_op=ALU.is_ge, fill=0.0, base=-1,
                                   pattern=[[-1, R]], channel_multiplier=1).then_inc(masks, 1)
                pool.affine_select(out=sq[:], in_=sq[:], compare_op=ALU.is_ge, fill=0.0, base=-1,
                                   pattern=[[1, R]], channel_multiplier=-1).then_inc(masks, 1)
                pool.memset(ones[:], 1.0).then_inc(masks, 1)
                pool.memset(up[:], 0.0).then_inc(masks, 1)

            @block.scalar
            def _(act):
                n = 0
                for k in range(NK):
                    for h in range(16 // TQ):
                        act.wait_ge(w_turned, n + 1)
                        w = TR * TQ
                        act.activation(wt[0:rows(k), k, h * w:(h + 1) * w], p_w[0:rows(k), n % 2, 0:w], ACT.Copy) \
                           .then_inc(wt_ready, 1)
                        n += 1
                act.wait_ge(dve_done, dve_at("diag_sum"))
                act.activation(col[:, 1:2], col[:, 0:1], ACT.Sqrt).then_inc(act_done, 1)
                act.wait_ge(pe_done, pe_at("u_turned"))
                act.activation(us[:, 0:FULL, 0:R], p_q[:, 0:FULL], ACT.Copy).then_inc(us_hi, 1)
                act.activation(us[0:REM, FULL, 0:R], p_q[0:REM, FULL], ACT.Copy).then_inc(us_hi, 1)
                for b in range(B):
                    for h, (a, z) in enumerate(halves):
                        act.wait_ge(ro_ready, 2 * b + h + 1)
                        act.activation(ro[:, b, 0, a:z], p_w[0:R, h, 0:HALF], ACT.Copy).then_inc(ro_hi, 1)

            @block.vector
            def _(dve):
                dve.memset(raw(us[:]), 0.0).then_inc(us_lo, 1)
                at = [0]

                def step(ins, name):
                    assert DVE_STEPS[at[0]] == name
                    at[0] += 1
                    ins.then_inc(dve_done, 1)
                    dve.wait_ge(dve_done, at[0])

                dve.wait_ge(masks, 6)
                dve.wait_ge(ident_made, 1)
                dve.scalar_tensor_tensor(upm[:], ident[0:R, 0:R], 0.5, sq[:], ALU.mult, ALU.add).then_inc(masks, 1)
                dve.wait_ge(bs_in, 16)
                for h in range(4):
                    w = TR * TQ
                    dve.wait_ge(v_ready, h + 1)
                    dve.tensor_tensor(v[:, h * w:(h + 1) * w], p_v[:, 0:w], bs[:, h * w:(h + 1) * w], ALU.add) \
                       .then_inc(v_done, 1)
                dve.wait_ge(pe_done, pe_at("gram"))
                dve.tensor_copy(m[:, R:2 * R], ident[0:R, 0:R]).then_inc(masks, 1)
                dve.wait_ge(masks, 8)
                step(dve.tensor_copy(m[:, 0:R], p_g[:, 0:R]), "m_ready")

                with dve.Fori(0, R) as j:
                    c = bass.ds(j, 1)
                    dve.wait_ge(step_done, 3 * j)
                    dve.tensor_scalar(row[:], m[:], ident[0:R, c], None, ALU.mult).then_inc(row_ready, 1)
                    dve.wait_ge(row_spread, j + 1)
                    dve.reciprocal(col[:, 4:5], p_b[:, c]).then_inc(step_done, 1)
                    dve.wait_ge(step_done, 3 * j + 1)
                    dve.scalar_tensor_tensor(col[:, 5:6], m[:, c], col[:, 4:5], neg[:, c], ALU.mult, ALU.mult) \
                       .then_inc(step_done, 1)
                    dve.wait_ge(step_done, 3 * j + 2)
                    dve.scalar_tensor_tensor(m[:], p_b[:, 0:2 * R], col[:, 5:6], m[:], ALU.mult, ALU.add) \
                       .then_inc(step_done, 1)
                dve.wait_ge(step_done, 3 * R)
                step(dve.tensor_tensor(sq[:], m[:, 0:R], ident[0:R, 0:R], ALU.mult), "diag")
                step(dve.tensor_reduce(col[:, 0:1], sq[:], AX.X, ALU.add), "diag_sum")
                dve.wait_ge(act_done, 1)
                step(dve.reciprocal(col[:, 2:3], col[:, 1:2]), "inv_std")
                step(dve.tensor_scalar(sq[:], m[:, R:2 * R], col[:, 2:3], None, ALU.mult), "scaled")
                dve.wait_ge(pe_done, pe_at("l_turned"))
                step(dve.tensor_copy(lst[:], p_g[:, 0:R]), "lst")
                dve.wait_ge(pe_done, pe_at("p_turned"))
                dve.tensor_copy(pt[:, 0:512], p_w[0:R, 0]).then_inc(masks, 1)
                step(dve.tensor_copy(pt[:, 512:C], p_w[0:R, 1, 0:C - 512]), "pt")
                dve.wait_ge(pe_done, pe_at("q_ready"))
                dve.tensor_copy(qt[:, 0:HALF], p_w[0:R, 0, 0:HALF]).then_inc(masks, 1)
                step(dve.tensor_copy(qt[:, HALF:C], p_w[0:R, 1, 0:HALF]), "qt")
                dve.wait_ge(pe_done, pe_at("q_turned"))
                dve.tensor_copy(q[:, 0:FULL], p_q[:, 0:FULL]).then_inc(masks, 1)
                step(dve.tensor_copy(q[0:REM, FULL], p_q[0:REM, FULL]), "q")
                dve.wait_ge(pe_done, pe_at("gram2"))
                step(dve.tensor_tensor(phi[:], p_g[:, 0:R], ident[0:R, 0:R], ALU.subtract), "phi0")
                step(dve.tensor_tensor(phi[:], phi[:], upm[:], ALU.mult), "phi")
                dve.wait_ge(pe_done, pe_at("fix"))
                dve.tensor_tensor(qt[:, 0:HALF], qt[:, 0:HALF], p_w[0:R, 0, 0:HALF], ALU.subtract).then_inc(masks, 1)
                step(dve.tensor_tensor(qt[:, HALF:C], qt[:, HALF:C], p_w[0:R, 1, 0:HALF], ALU.subtract), "qt2")
                dve.wait_ge(pe_done, pe_at("top"))
                step(dve.tensor_copy(m[:, 0:R], p_g[:, 0:R]), "m2_ready")

                with dve.Fori(0, R) as j:
                    c = bass.ds(j, 1)
                    dve.wait_ge(step2_done, 6 * j)
                    dve.tensor_scalar(row[:], m[:], ident[0:R, c], None, ALU.mult).then_inc(row2_ready, 1)
                    dve.wait_ge(row2_spread, j + 1)
                    dve.tensor_scalar(col[:, 3:4], p_b[:, c], 0.0, -2.0, ALU.is_ge, ALU.mult).then_inc(step2_done, 1)
                    dve.wait_ge(step2_done, 6 * j + 1)
                    dve.tensor_scalar(sg[:, c], col[:, 3:4], 1.0, None, ALU.add).then_inc(step2_done, 1)
                    dve.wait_ge(step2_done, 6 * j + 2)
                    dve.tensor_tensor(col[:, 6:7], p_b[:, c], sg[:, c], ALU.subtract).then_inc(step2_done, 1)
                    dve.wait_ge(step2_done, 6 * j + 3)
                    dve.reciprocal(col[:, 4:5], col[:, 6:7]).then_inc(step2_done, 1)
                    dve.wait_ge(step2_done, 6 * j + 4)
                    dve.scalar_tensor_tensor(col[:, 5:6], m[:, c], col[:, 4:5], neg[:, c], ALU.mult, ALU.mult) \
                       .then_inc(step2_done, 1)
                    dve.wait_ge(step2_done, 6 * j + 5)
                    dve.scalar_tensor_tensor(m[:], p_b[:, 0:2 * R], col[:, 5:6], m[:], ALU.mult, ALU.add) \
                       .then_inc(step2_done, 1)
                dve.wait_ge(step2_done, 6 * R)
                step(dve.tensor_tensor(sq[:], sg[:], ident[0:R, 0:R], ALU.mult), "sign_diag")
                step(dve.tensor_reduce(col[:, 7:8], sq[:], AX.X, ALU.add), "signs")
                step(dve.tensor_scalar(ut[:], qt[:], col[:, 7:8], None, ALU.mult), "ut")

                dve.wait_ge(pe_done, pe_at("a_turned"))
                step(dve.tensor_tensor(a2[:], up[:], p_s[:, :, 0, 0:R], ALU.subtract), "a2")
                scale = 2.0 ** -SQUARINGS
                dve.tensor_scalar(sa[:, :, 1], a2[:], -scale, None, ALU.mult).then_inc(masks, 1)
                step(dve.tensor_scalar(sa[:, :, 0], a2[:], scale, None, ALU.mult), "sa")
                dve.wait_ge(masks, 13)
                step(dve.tensor_scalar(ex[:], sa[:], 1.0 / TERMS, None, ALU.mult), "y0")
                for i in range(1, TERMS):
                    dve.wait_ge(pe_done, pe_at(f"taylor{i}"))
                    step(dve.tensor_tensor(ts[:], p_s[:, :, :, 0:R], sa[:], ALU.add), f"sum{i}")
                    step(dve.tensor_scalar(ex[:], ts[:], 1.0 / (TERMS - i), None, ALU.mult), f"y{i}")
                with dve.Fori(0, SQUARINGS) as i:
                    dve.wait_ge(sq_ready, i + 1)
                    for s in range(2):
                        dve.scalar_tensor_tensor(ex[:, :, s], ex[:, :, s], 2.0, p_s[:, :, s, s * R:(s + 1) * R],
                                                 ALU.mult, ALU.add).then_inc(ex_ready, 1)
                dve.wait_ge(us_hi, 2)
                dve.tensor_tensor(us[:, 0:FULL, R:2 * R], p_q[:, 0:FULL], raw(us[:, 0:FULL, 0:R]), ALU.subtract) \
                   .then_inc(masks, 1)
                dve.tensor_tensor(us[0:REM, FULL, R:2 * R], p_q[0:REM, FULL], raw(us[0:REM, FULL, 0:R]),
                                  ALU.subtract).then_inc(us_lo, 1)
                for b in range(B):
                    for h, (a, z) in enumerate(halves):
                        dve.wait_ge(ro_hi, 2 * b + h + 1)
                        dve.tensor_tensor(ro[:, b, 1, a:z], p_w[0:R, h, 0:HALF], raw(ro[:, b, 0, a:z]),
                                          ALU.subtract).then_inc(ro_lo, 1)

            @block.tensor
            def _(pe):
                at = [0]

                def step(ins, name):
                    assert PE_STEPS[at[0]] == name
                    at[0] += 1
                    ins.then_inc(pe_done, 1)

                pe.wait_ge(ident_made, 1)
                pe.wait_ge(w_in, 16)
                n = 0
                for k in range(NK):
                    for h in range(16 // TQ):
                        if n >= 2:
                            pe.wait_ge(wt_ready, n - 1)
                        for t in range(TQ):
                            i = pe.transpose(p_w[0:rows(k), n % 2, t * TR:(t + 1) * TR],
                                             wr[:, h * TQ + t, k * P:k * P + rows(k)], ident[0:TR, 0:TR])
                        i.then_inc(w_turned, 1)
                        n += 1
                pe.wait_ge(wt_ready, NK * 16 // TQ)
                for h in range(16 // TQ):
                    w = TR * TQ
                    if h:
                        pe.wait_ge(v_done, h)
                    for k in range(NK):
                        i = pe.matmul(p_v[:, 0:w], sct[0:rows(k), k], wt[0:rows(k), k, h * w:(h + 1) * w],
                                      start=(k == 0), stop=(k == NK - 1))
                    i.then_inc(v_ready, 1)

                def gram(x, name):
                    for k in range(NK):
                        i = pe.matmul(p_g[:, 0:R], x[0:rows(k), k], x[0:rows(k), k], start=(k == 0), stop=(k == NK - 1))
                    step(i, name)

                def turn_rows(x, name):
                    for k in range(NK):
                        i = pe.transpose(p_q[0:rows(k), k], x[:, k * P:k * P + rows(k)], ident[0:R, 0:R])
                    step(i, name)

                pe.wait_ge(pp_in, 32)
                gram(pp, "gram")
                pe.wait_ge(dve_done, dve_at("m_ready"))
                pe.wait_ge(masks, 6)
                with pe.Fori(0, R) as j:
                    wait_alone(pe, row_ready, j + 1, passed)
                    pe.matmul(p_b[:, 0:2 * R], ones[:], row[:], start=True, stop=True).then_inc(row_spread, 1)
                pe.wait_ge(dve_done, dve_at("scaled"))
                step(pe.transpose(p_g[:, 0:R], sq[:], ident[0:R, 0:R]), "l_turned")
                for k in range(NK):
                    i = pe.transpose(p_w[0:R, k // 4, k % 4 * P:k % 4 * P + rows(k)], pp[0:rows(k), k],
                                     ident[0:rows(k), 0:rows(k)])
                step(i, "p_turned")
                pe.wait_ge(dve_done, dve_at("pt"))
                for h, (a, z) in enumerate(halves):
                    i = pe.matmul(p_w[0:R, h, 0:HALF], lst[:], pt[:, a:z], start=True, stop=True)
                step(i, "q_ready")
                pe.wait_ge(dve_done, dve_at("qt"))
                turn_rows(qt, "q_turned")
                pe.wait_ge(dve_done, dve_at("q"))
                gram(q, "gram2")
                pe.wait_ge(dve_done, dve_at("phi"))
                for h, (a, z) in enumerate(halves):
                    i = pe.matmul(p_w[0:R, h, 0:HALF], phi[:], qt[:, a:z], start=True, stop=True)
                step(i, "fix")
                pe.wait_ge(dve_done, dve_at("qt2"))
                step(pe.transpose(p_g[:, 0:R], qt[:, 0:R], ident[0:R, 0:R]), "top")
                pe.wait_ge(dve_done, dve_at("m2_ready"))
                with pe.Fori(0, R) as j:
                    wait_alone(pe, row2_ready, j + 1, passed)
                    pe.matmul(p_b[:, 0:2 * R], ones[:], row[:], start=True, stop=True).then_inc(row2_spread, 1)
                pe.wait_ge(dve_done, dve_at("ut"))
                turn_rows(ut, "u_turned")

                pe.wait_ge(up_in, 16 * (R - 1))
                for b in range(B):
                    i = pe.transpose(p_s[:, b, 0, 0:R], up[:, b], ident[0:R, 0:R])
                step(i, "a_turned")
                for t in range(1, TERMS):
                    pe.wait_ge(dve_done, dve_at("y0" if t == 1 else f"y{t - 1}"))
                    for b in range(B):
                        for s in range(2):
                            i = pe.matmul(p_s[:, b, s, 0:R], sa[:, b, 1 - s], ex[:, b, s], start=True, stop=True)
                    step(i, f"taylor{t}")
                pe.wait_ge(dve_done, dve_at(f"y{TERMS - 1}"))
                with pe.Fori(0, SQUARINGS) as n:
                    wait_alone(pe, ex_ready, 2 * n, passed)
                    for b in range(B):
                        for s in range(2):
                            i = pe.matmul(p_s[:, b, s], ex[:, b, 1 - s], ex[:, b].rearrange("p s n -> p (s n)"),
                                          start=True, stop=True)
                    i.then_inc(sq_ready, 1)
                pe.wait_ge(ex_ready, 2 * SQUARINGS)
                for b in range(B):
                    for h, (a, z) in enumerate(halves):
                        if b:
                            pe.wait_ge(ro_lo, 2 * (b - 1) + h + 1)
                        pe.matmul(p_w[0:R, h, 0:HALF], ex[:, b, 1], ut[:, a:z], start=True, stop=True) \
                          .then_inc(ro_ready, 1)


def build(nc, x, cond, w_qkv, b_qkv, w_proj, b_proj, w_fc1, b_fc1, w_fc2, b_fc2, w_ada, b_ada, p_in, w_skew, b_skew,
          out):
    scratch = lambda name, *shape: nc.dram_tensor(name, shape, F32, kind="Internal").ap()
    wqkv_s = scratch("wqkv_s", 2, C, 3 * C)
    wproj_s = scratch("wproj_s", 2, C, C)
    w1_s = scratch("w1_s", 2, C, FF)
    w2_s = scratch("w2_s", 2, FF, C)
    ada = scratch("ada", B, 8 * C)
    mod = scratch("mod", B, P, len(MOD) * (FULL + 1))
    gates = scratch("gates", B * L // GT, C)
    u_s = scratch("u_s", P, FULL + 1, 2 * R)
    rot_s = scratch("rot_s", B, 2, R, C)
    q_s = scratch("q_s", 2, NHEAD * D, L)
    k_s = scratch("k_s", 2, NHEAD * D, L)
    v_s = scratch("v_s", 2, NHEAD, L, D)
    o_t = scratch("o_t", NHEAD * D, L)
    sums = scratch("sums", NHEAD, L)
    rsums = scratch("rsums", NHEAD, L)
    x2_s = scratch("x2_s", B * L, C)
    h2_s = scratch("h2_s", B * L // GT, P, A_TILES, GT)
    x3_s = scratch("x3_s", B * L, C)
    x_rows = x.rearrange("b t c -> (b t) c")
    out_rows = out.rearrange("b t c -> (b t) c")
    weights = [(w_qkv, wqkv_s), (w_proj, wproj_s), (w_fc1, w1_s), (w_fc2, w2_s)]

    with nc.sbuf_tensor("sct", [P, FULL + 1, B], F32) as sct:
        stage_condition(nc, sct, cond, w_ada, b_ada, b_proj, b_fc2, weights, ada, mod, gates)
        stage_rotation(nc, sct, p_in, w_skew, b_skew, u_s, rot_s)
    stage_qkv(nc, x_rows, b_qkv, wqkv_s, mod, q_s, k_s, v_s)
    stage_attention(nc, q_s, k_s, v_s, o_t, sums)
    stage_proj(nc, o_t, sums, rsums, x_rows, wproj_s, ada, mod, x2_s, h2_s)
    stage_mlp(nc, h2_s, x2_s, w1_s, b_fc1, w2_s, gates, x3_s)
    stage_rotate(nc, x3_s, u_s, rot_s, out_rows)


_INS = ("x", "cond_1152", "L0_cond_W_qkv", "L0_cond_b_qkv", "L0_cond_W_proj", "L0_cond_b_proj", "L0_cond_W_fc1",
        "L0_cond_b_fc1", "L0_cond_W_fc2", "L0_cond_b_fc2", "L0_cond_W_ada", "L0_cond_b_ada", "L1_cond_P",
        "L1_cond_W", "L1_cond_b")
_OUTS = [((B, L, C), "float32")]


def kernel(**inputs):
    import numpy as _np
    import concourse.bacc as _bacc
    from concourse import mybir as _mybir
    from concourse.bass_utils import run_bass_kernel_spmd as _run

    nc = _bacc.Bacc("TRN2", target_bir_lowering=False, num_devices=1)
    arrays, args = {}, []
    for name in _INS:
        a = _np.ascontiguousarray(inputs[name])
        arrays[f"in_{name}_dram"] = a
        args.append(nc.dram_tensor(f"in_{name}_dram", a.shape, _mybir.dt.from_np(a.dtype), kind="ExternalInput").ap())
    for i, (shape, dtype) in enumerate(_OUTS):
        dt = _mybir.dt.from_np(_np.dtype(dtype))
        args.append(nc.dram_tensor(f"out_{i}_dram", shape, dt, kind="ExternalOutput").ap())
    build(nc, *args)
    r = _run(nc, [arrays], core_ids=[0])
    return r.results[0]["out_0_dram"]
```

```python
from contextlib import ExitStack

import concourse.bass as bass
from concourse import mybir

F32 = mybir.dt.float32
F32R = mybir.dt.float32r
ALU = mybir.AluOpType
ACT = mybir.ActivationFunctionType
AX = mybir.AxisListType

P = 128
B, L, C = 4, 1024, 576
H = 16
D = C // H
NHEAD = B * H
FF = 4 * C
R = 64
NSKEW = R * (R - 1) // 2
SEC = 6
LN_EPS = 1e-6
FULL = C // P
REM = C - FULL * P
CPAD = (FULL + 1) * P
GT = 512
SUB = GT // P
HALF = C // 2
SHIFT_MSA, SCALE_MSA, GATE_MSA, SHIFT_MLP, SCALE_MLP, GATE_MLP, GB_PROJ, GB_FC2 = range(8)
MOD = (SHIFT_MSA, SCALE_MSA, SHIFT_MLP, SCALE_MLP)

A_TILES = 2 * (FULL + 1)
W_TILES = 2 * FULL + 1
PASSES = [p for k in range(FULL) for p in ((k, k), (FULL + 1 + k, k), (k, FULL + k))]
PASSES += [(FULL, 2 * FULL), (2 * FULL + 1, 2 * FULL)]


def raw(ap):
    return ap.bitcast(F32)


def load_split_weight(eng, dst, src, cols, sem):
    for s in range(2):
        eng.dma_start(raw(dst[:, s * FULL:(s + 1) * FULL, :]),
                      src[s, 0:FULL * P, cols].rearrange("(k p) n -> p k n", p=P)).then_inc(sem, 16)
        eng.dma_start(raw(dst[s * REM:(s + 1) * REM, 2 * FULL, :]), src[s, FULL * P:C, cols]).then_inc(sem, 16)


def wait_alone(eng, sem, value, passed):
    eng.wait_ge(sem, value)
    eng.sem_inc(passed, 1)


def stage_semaphores(nc, ctx, prefix):
    made = []

    def sem(name):
        made.append(ctx.enter_context(nc.semaphore(prefix + name)))
        return made[-1]

    def zero():
        nums = sorted(s.num for s in made)
        starts = [n for n in nums if n - 1 not in nums]
        ends = [n for n in nums if n + 1 not in nums]
        nc.all_engine_barrier()
        for a, z in zip(starts, ends):
            nc.gpsimd.sem_clear(range(a, z + 1))
        nc.all_engine_barrier()

    ctx.callback(zero)
    return sem


def c_slot(half, c):
    return (half * (FULL + 1) + c) % 2


def make_identity(nc, pool, ident, zeroed, made):
    pool.memset(ident[:], 0.0).then_inc(zeroed, 1)
    pool.wait_ge(zeroed, 1)
    pool.affine_select(out=ident[:], in_=ident[:], compare_op=ALU.not_equal, fill=1.0, base=0,
                       pattern=[[-1, P]], channel_multiplier=1).then_inc(made, 1)


def stage_qkv(nc, x, b_qkv, wqkv, mod, q_s, k_s, v_s):
    QKM = 2 * C // P
    QR, VR = 3, 2
    with ExitStack() as ctx:
        sb = lambda n, s, d=F32: ctx.enter_context(nc.sbuf_tensor("q_" + n, s, d))
        ps = lambda n, s: ctx.enter_context(nc.psum_tensor("q_psum_" + n, s, F32))
        sem = stage_semaphores(nc, ctx, "q_")
        passed = sem("passed")
        w = sb("w", [P, W_TILES, 3 * C], F32R)
        bqk = sb("bqk", [P, QKM])
        bv = sb("bv", [P, C])
        ident = sb("ident", [P, P])
        xt = sb("xt", [P, 2, SUB, C])
        xn = sb("xn", [P, 2, SUB, CPAD])
        md = sb("md", [P, 2, len(MOD) * (FULL + 1)])
        stats = sb("stats", [P, SUB, 2, 6])
        mv = sb("mv", [P, 2, SUB, 2])
        small = sb("small", [P, 6, SUB])
        rstd = sb("rstd", [P, 2, SUB])
        shift = sb("shift", [P, 2, SUB])
        ht = sb("ht", [P, 2, A_TILES, GT], F32R)
        hf = sb("hf", [P, FULL + 1, GT])
        qko = sb("qko", [P, QR, 2, GT], F32R)
        vf = sb("vf", [P, VR, C])
        vo = sb("vo", [P, VR, 2, C], F32R)
        pt = ps("pt", [P, 2, GT])
        pqk = ps("pqk", [P, 3, 512])
        pv = ps("pv", [P, 2, 512])

        w_in, zeroed, ident_made = sem("w_in"), sem("zeroed"), sem("ident_made")
        x_in = [sem(f"x_in{i}") for i in range(2)]
        md_in = [sem(f"md_in{i}") for i in range(2)]
        dve_link, var_ready, std_ready, rstd_ready, xn_ready = (
            sem("dve_link"), sem("var_ready"), sem("std_ready"), sem("rstd_ready"), sem("xn_ready"))
        t_ready, hi_ready, full_ready, lo_ready = (
            sem("t_ready"), sem("hi_ready"), sem("full_ready"), sem("lo_ready"))
        qk_ready, qk_hi = sem("qk_ready"), sem("qk_hi")
        qk_lo = [sem(f"qk_lo{i}") for i in range(QR)]
        qk_out = [sem(f"qk_out{i}") for i in range(QR)]
        v_ready, v_hi = sem("v_ready"), sem("v_hi")
        v_full = [sem(f"v_full{i}") for i in range(2)]
        v_lo = [sem(f"v_lo{i}") for i in range(VR)]
        v_out = [sem(f"v_out{i}") for i in range(VR)]
        NK = FULL + 1

        def groups(eng, body):
            with eng.Fori(0, B - 1) as b:
                body(b, 0, False)
                body(b, 1, False)
            body(B - 1, 0, True)
            body(B - 1, 1, True)

        SPLIT = C // P

        def out_count(slot, g):
            return (QKM // QR + (1 if SPLIT % QR == slot else 0)) * g

        with nc.Block() as block:
            @block.sync
            def _(sp):
                def load(b, half):
                    sp.dma_start(xt[:, half], x[bass.ds(b * L + half * GT, GT), :]
                                 .rearrange("(t p) c -> p t c", p=P)).then_inc(x_in[half], 16)
                    sp.dma_start(md[:, half], mod[bass.ds(b, 1)].rearrange("a p n -> (a p) n")) \
                      .then_inc(md_in[half], 16)

                load(0, 0)
                load(0, 1)
                load_split_weight(sp, w, wqkv, slice(0, 3 * C), w_in)
                sp.dma_start(bqk[:], b_qkv[0:2 * C].rearrange("(m p) -> p m", p=P),
                             allow_slow_non_contiguous=True).then_inc(w_in, 16)
                sp.dma_start(bv[:], b_qkv[2 * C:3 * C].rearrange("(a n) -> a n", a=1)
                             .broadcast_to([P, C])).then_inc(w_in, 16)

                def body(b, half, last):
                    g = 2 * b + half
                    if not last:
                        wait_alone(sp, xn_ready, g + 1, passed)
                        sp.wait_ge(lo_ready, NK * (g + 1))
                        load(b + 1, half)
                    for m in range(QKM):
                        sp.wait_ge(qk_lo[m % QR], (QKM // QR) * g + m // QR + 1)
                        for name, r0, r1 in (("q", 0, C), ("k", C, 2 * C)):
                            a, z = max(r0, m * P), min(r1, (m + 1) * P)
                            if a < z:
                                dst = q_s if name == "q" else k_s
                                sp.dma_start(
                                    dst[:, bass.ds(b * C + a - r0, z - a), half * GT:(half + 1) * GT]
                                    .rearrange("s f t -> f s t"),
                                    raw(qko[a - m * P:z - m * P, m % QR])).then_inc(qk_out[m % QR], 16)
                    for t in range(SUB):
                        sp.wait_ge(v_lo[t % VR], (SUB // VR) * g + t // VR + 1)
                        for s in range(2):
                            sp.dma_start(
                                v_s[s, bass.ds(b * H, H), half * GT + t * P:half * GT + (t + 1) * P, :]
                                .rearrange("h t d -> t h d"),
                                raw(vo[:, t % VR, s]).rearrange("p (h d) -> p h d", h=H)) \
                              .then_inc(v_out[t % VR], 16)

                groups(nc.sync, body)
                for m in range(QR):
                    sp.wait_ge(qk_out[m], 16 * out_count(m, 2 * B))
                for t in range(VR):
                    sp.wait_ge(v_out[t], 32 * (SUB // VR) * 2 * B)

            @block.gpsimd
            def _(pool):
                make_identity(nc, pool, ident, zeroed, ident_made)

                def normalise(g, half):
                    if not (isinstance(g, int) and g < 2):
                        pool.wait_ge(t_ready, NK * (g - 1))
                    wait_alone(pool, rstd_ready, g + 1, passed)
                    for t in range(SUB):
                        for a, z, o in ((0, C, 0), (FULL * P, C, C)):
                            i = pool.tensor_scalar(xn[:, half, t, o:o + z - a], xt[:, half, t, a:z],
                                                   rstd[:, half, t:t + 1], shift[:, half, t:t + 1],
                                                   ALU.mult, ALU.add)
                    i.then_inc(xn_ready, 1)

                def lows(g, half):
                    for c in range(NK):
                        pool.wait_ge(hi_ready, NK * g + c + 1)
                        pool.wait_ge(full_ready, NK * g + c + 1)
                        pool.tensor_tensor(ht[:, half, NK + c, :], hf[:, c, :], raw(ht[:, half, c, :]), ALU.subtract) \
                            .then_inc(lo_ready, 1)

                normalise(0, 0)
                lows(0, 0)
                normalise(1, 1)

                def body(b, half, last):
                    g = 2 * b + half
                    if not (last and half == 1):
                        lows(g + 1, 1 - half)
                    if not last:
                        normalise(g + 2, half)
                    for t in range(SUB):
                        pool.wait_ge(v_hi, SUB * g + t + 1)
                        pool.tensor_tensor(vo[:, t % VR, 1], vf[:, t % VR], vo[:, t % VR, 0].bitcast(F32),
                                           ALU.subtract).then_inc(v_lo[t % VR], 1)

                groups(nc.gpsimd, body)

            @block.vector
            def _(dve):
                def link(ins, n):
                    ins.then_inc(dve_link, 1)
                    dve.wait_ge(dve_link, n)

                LINKS = 7

                def row_stats(g, b, half, t):
                    if t == 0:
                        dve.wait_ge(x_in[half], 16 * b + 16)
                    for a in range(2):
                        i = dve.bn_stats(stats[:, t, a], xt[:, half, t, a * HALF:(a + 1) * HALF])
                    if t == SUB - 1:
                        link(i, LINKS * g + 1)

                def statistics(g, half):
                    n = LINKS * g
                    if not (isinstance(g, int) and g < 2):
                        wait_alone(dve, xn_ready, g - 1, passed)
                    for t in range(SUB):
                        i = dve.bn_aggr(mv[:, half, t], stats[:, t].rearrange("p a s -> p (a s)"))
                    link(i, n + 2)
                    ve, std, r0, r2, cor = (small[:, k] for k in range(5))
                    dve.tensor_scalar(ve, mv[:, half, :, 1], LN_EPS, None, ALU.add).then_inc(var_ready, 1)
                    dve.wait_ge(std_ready, g + 1)
                    link(dve.reciprocal(r0, std), n + 3)
                    link(dve.tensor_tensor(r2, r0, r0, ALU.mult), n + 4)
                    link(dve.tensor_tensor(r2, r2, ve, ALU.mult), n + 5)
                    link(dve.tensor_scalar(cor, r2, -0.5, 1.5, ALU.mult, ALU.add), n + 6)
                    link(dve.tensor_tensor(rstd[:, half], r0, cor, ALU.mult), n + 7)
                    dve.scalar_tensor_tensor(shift[:, half], mv[:, half, :, 0], -1.0, rstd[:, half],
                                             ALU.mult, ALU.mult).then_inc(rstd_ready, 1)

                def fulls(g, b, half):
                    for c in range(NK):
                        dve.wait_ge(hi_ready, NK * g + c + 1)
                        if c == 0:
                            dve.wait_ge(md_in[half], 16 * b + 16)
                        if not (isinstance(g, int) and g == 0):
                            dve.wait_ge(lo_ready, NK * (g - 1) + c + 1)
                        dve.tensor_scalar(hf[:, c, :], pt[:, c_slot(half, c), :], md[:, half, NK + c:NK + c + 1],
                                          md[:, half, c:c + 1], ALU.mult, ALU.add).then_inc(full_ready, 1)

                for t in range(SUB):
                    row_stats(0, 0, 0, t)
                statistics(0, 0)
                fulls(0, 0, 0)
                for t in range(SUB):
                    row_stats(1, 0, 1, t)
                statistics(1, 1)
                dve.wait_ge(w_in, 16 * 6)

                def body(b, half, last):
                    g = 2 * b + half
                    if not (last and half == 1):
                        fulls(g + 1, b + half, 1 - half)
                    for m in range(QKM):
                        dve.wait_ge(qk_hi, QKM * g + m + 1)
                        dve.scalar_tensor_tensor(qko[:, m % QR, 1], pqk[:, m % 3], bqk[:, m:m + 1],
                                                 qko[:, m % QR, 0].bitcast(F32), ALU.add, ALU.subtract) \
                           .then_inc(qk_lo[m % QR], 1)
                        if not last and m < SUB:
                            row_stats(g + 2, b + 1, half, m)
                        if not last and m == SUB:
                            statistics(g + 2, half)
                    for t in range(SUB):
                        dve.wait_ge(v_lo[t % VR], (SUB // VR) * g + t // VR)
                        for a in range(2):
                            dve.wait_ge(v_ready, 2 * SUB * g + 2 * t + a + 1)
                            dve.tensor_tensor(vf[:, t % VR, a * HALF:(a + 1) * HALF], pv[:, a, 0:HALF],
                                              bv[:, a * HALF:(a + 1) * HALF], ALU.add) \
                               .then_inc(v_full[a], 1)

                groups(nc.vector, body)

            @block.scalar
            def _(act):
                def root(g):
                    act.wait_ge(var_ready, g + 1)
                    act.activation(small[:, 1], small[:, 0], ACT.Sqrt).then_inc(std_ready, 1)

                def his(g, b, half):
                    for c in range(NK):
                        act.wait_ge(t_ready, NK * g + c + 1)
                        if c == 0:
                            act.wait_ge(md_in[half], 16 * b + 16)
                            if not (isinstance(g, int) and g < 2):
                                act.wait_ge(v_ready, 2 * SUB * (g - 1))
                        act.activation(ht[:, half, c, :], pt[:, c_slot(half, c), :], ACT.Identity,
                                       bias=md[:, half, c:c + 1], scale=md[:, half, NK + c:NK + c + 1]) \
                           .then_inc(hi_ready, 1)

                root(0)
                his(0, 0, 0)
                root(1)
                act.wait_ge(w_in, 16 * 6)

                def body(b, half, last):
                    g = 2 * b + half
                    if not (last and half == 1):
                        his(g + 1, b + half, 1 - half)
                    for m in range(QKM):
                        act.wait_ge(qk_ready, QKM * g + m + 1)
                        act.wait_ge(qk_out[m % QR], 16 * (out_count(m % QR, 1) * g + m // QR
                                                          + (1 if SPLIT % QR == m % QR and m > SPLIT else 0)))
                        act.activation(qko[:, m % QR, 0], pqk[:, m % 3], ACT.Identity,
                                       bias=bqk[:, m:m + 1]).then_inc(qk_hi, 1)
                        if not last and m == SUB:
                            root(g + 2)
                    for t in range(SUB):
                        for a in range(2):
                            act.wait_ge(v_full[a], SUB * g + t + 1)
                        act.wait_ge(v_out[t % VR], 32 * ((SUB // VR) * g + t // VR))
                        act.activation(vo[:, t % VR, 0], vf[:, t % VR], ACT.Copy).then_inc(v_hi, 1)

                groups(nc.scalar, body)

            @block.tensor
            def _(pe):
                pe.wait_ge(ident_made, 1)

                def transposes(g, half):
                    pe.wait_ge(xn_ready, g + 1)
                    for c in range(NK):
                        if not (isinstance(g, int) and g == 0 and c < 2):
                            pe.wait_ge(hi_ready, NK * g + c - 1)
                            pe.wait_ge(full_ready, NK * g + c - 1)
                        for t in range(SUB):
                            i = pe.transpose(pt[:, c_slot(half, c), t * P:(t + 1) * P],
                                             xn[:, half, t, c * P:(c + 1) * P], ident[:])
                        i.then_inc(t_ready, 1)

                transposes(0, 0)
                pe.wait_ge(w_in, 16 * 6)

                def body(b, half, last):
                    g = 2 * b + half
                    if not (last and half == 1):
                        transposes(g + 1, 1 - half)
                    pe.wait_ge(hi_ready, NK * (g + 1))
                    pe.wait_ge(lo_ready, NK * (g + 1))
                    for m in range(QKM):
                        pe.wait_ge(qk_lo[m % QR], (QKM // QR) * g + m // QR)
                        for n, (a, k) in enumerate(PASSES):
                            i = pe.matmul(pqk[:, m % 3], w[:, k, m * P:(m + 1) * P], ht[:, half, a, :],
                                          start=(n == 0), stop=(n == len(PASSES) - 1))
                        i.then_inc(qk_ready, 1)
                    for t in range(SUB):
                        for h in range(2):
                            pe.wait_ge(v_full[h], SUB * g + t)
                            for n, (a, k) in enumerate(PASSES):
                                i = pe.matmul(pv[:, h, 0:HALF], ht[:, half, a, t * P:(t + 1) * P],
                                              w[:, k, 2 * C + h * HALF:2 * C + (h + 1) * HALF],
                                              start=(n == 0), stop=(n == len(PASSES) - 1))
                            i.then_inc(v_ready, 1)

                groups(nc.tensor, body)


def stage_attention(nc, q_s, k_s, v_s, o_t, sums):
    KT = L // P
    LH = L // GT
    STEPS = LH * KT
    AHEAD = 5
    SLOTS = 4
    RING = 8
    SROWS, MROWS = 3 * D, 3 * D + 2
    VLO = 64
    ONES = D
    VW = VLO + D
    SCALE = float(D) ** -0.5
    MAX_STEP = (1, 3, 5, 7, 9, 11, 13, 14)
    TURN_STEP = STEPS - 1
    JOBS = KT + 1
    dve_lo = lambda s: s % 4 == 3
    NDVE = STEPS // 4
    NPOOL = STEPS - NDVE
    LOADS = 8
    with ExitStack() as ctx:
        sb = lambda n, s, d=F32: ctx.enter_context(nc.sbuf_tensor("a_" + n, s, d))
        ps = lambda n, s: ctx.enter_context(nc.psum_tensor("a_psum_" + n, s, F32))
        sem = stage_semaphores(nc, ctx, "a_")
        ident = sb("ident", [P, P])
        qs = sb("qs", [P, SLOTS, L], F32R)
        ks = sb("ks", [P, SLOTS, L], F32R)
        vs = sb("vs", [P, SLOTS, KT, VW], F32R)
        pf = sb("pf", [P, RING, GT])
        ph = sb("ph", [P, RING, GT], F32R)
        pl = sb("pl", [P, RING, GT], F32R)
        mx = sb("mx", [P, 2, KT])
        mxt = sb("mxt", [KT, 2, 2, P], F32R)
        ob = sb("ob", [VLO, LH, GT])
        p_s = ps("s", [P, 2, L])
        p_t = ps("t", [P, 2, GT])
        p_o = ps("o", [P, LH, GT])

        zeroed, ident_made, set_up = sem("zeroed"), sem("ident_made"), sem("set_up")
        loaded = [sem(f"loaded{i}") for i in range(SLOTS)]
        max_in = [sem(f"max_in{i}") for i in range(SLOTS)]
        s_ready = sem("s_ready")
        s_free = [sem(f"s_free{i}") for i in range(2)]
        mxt_hi = sem("mxt_hi")
        t_ready = sem("t_ready")
        exp_done = [sem(f"exp_done{i}") for i in range(2)]
        hi_ready, lo_pool, lo_dve = sem("hi_ready"), sem("lo_pool"), sem("lo_dve")
        p_free = sem("p_free")
        hi_copied = sem("hi_copied")
        o_copied = [sem(f"o_copied{i}") for i in range(LH)]
        o_out = [sem(f"o_out{i}") for i in range(LH)]

        def heads(eng, body):
            n = NHEAD // SLOTS
            with eng.Fori(0, n - 1) as i:
                for u in range(SLOTS):
                    body(SLOTS * i + u, u, i, False)
            for u in range(SLOTS):
                body(SLOTS * (n - 1) + u, u, n - 1, True)

        def bank(u, job):
            return (JOBS * u + job) % 2

        def bank_uses(u, i, job):
            return JOBS * SLOTS // 2 * i + (JOBS * u + job) // 2

        def lo_counts(n_heads, s):
            d = sum(dve_lo(x) for x in range(s + 1))
            return NPOOL * n_heads + s + 1 - d, NDVE * n_heads + d

        with nc.Block() as block:
            @block.sync
            def _(sp):
                def load(hd, u):
                    for t, tile in ((q_s, qs), (k_s, ks)):
                        for r, s in enumerate((0, 1, 0) if t is q_s else (0, 0, 1)):
                            sp.dma_start(raw(tile[r * D:(r + 1) * D, u]),
                                         t[s, bass.ds(hd * D, D), :]).then_inc(loaded[u], 16)
                    for s, c in enumerate((0, VLO)):
                        sp.dma_start(raw(vs[:, u, :, c:c + D]),
                                     v_s[s, bass.ds(hd, 1)].rearrange("a (t p) d -> p (a t) d", p=P)) \
                          .then_inc(loaded[u], 16)

                def put_max(u, i):
                    sp.wait_ge(s_free[bank(u, KT)], bank_uses(u, i, KT) + 1)
                    for s in range(2):
                        sp.dma_start(raw(qs[SROWS + s:SROWS + s + 1, u]).rearrange("o (t c) -> o t c", c=P),
                                     raw(mxt[:, u % 2, s])).then_inc(max_in[u], 16)

                sp.wait_ge(set_up, 3)
                for hd in range(SLOTS - 1):
                    load(hd, hd)
                put_max(0, 0)

                def body(hd, u, i, last):
                    if not (last and u > 0):
                        sp.wait_ge(p_free, RING + STEPS * hd)
                        load(hd + SLOTS - 1, (u + SLOTS - 1) % SLOTS)
                    if not (last and u == SLOTS - 1):
                        put_max((u + 1) % SLOTS, i + (u + 1) // SLOTS)
                    for lh in range(LH):
                        sp.wait_ge(o_copied[lh], hd + 1)
                        sp.dma_start(o_t[bass.ds(hd * D, D), lh * GT:(lh + 1) * GT], ob[0:D, lh]) \
                          .then_inc(o_out[lh], 16)
                        sp.dma_start(sums[bass.ds(hd, 1), lh * GT:(lh + 1) * GT], ob[ONES:ONES + 1, lh]) \
                          .then_inc(o_out[lh], 16)

                heads(nc.sync, body)
                for lh in range(LH):
                    sp.wait_ge(o_out[lh], 32 * NHEAD)

            @block.gpsimd
            def _(pool):
                make_identity(nc, pool, ident, zeroed, ident_made)
                pool.wait_ge(ident_made, 1)
                pool.memset(raw(ks[:]), 1.0).then_inc(set_up, 1)

                def body(hd, u, i, last):
                    for s in range(STEPS):
                        if not dve_lo(s):
                            pool.wait_ge(hi_ready, STEPS * hd + s + 1)
                            pool.tensor_tensor(pl[:, s % RING], pf[:, s % RING], raw(ph[:, s % RING]),
                                               ALU.subtract).then_inc(lo_pool, 1)

                heads(nc.gpsimd, body)

            @block.vector
            def _(dve):
                dve.memset(raw(qs[:]), 1.0).then_inc(set_up, 1)
                dve.memset(raw(vs[:]), 1.0).then_inc(set_up, 1)

                def max_tile(hd, u, t):
                    dve.wait_ge(s_ready, JOBS * hd + t + 1)
                    dve.tensor_reduce(mx[:, u % 2, t:t + 1], p_s[:, bank(u, t)], AX.X, ALU.max) \
                       .then_inc(s_free[bank(u, t)], 1)

                def turn_lo(hd, u):
                    dve.wait_ge(mxt_hi, hd + 1)
                    dve.scalar_tensor_tensor(mxt[:, u % 2, 1], p_s[0:KT, bank(u, KT), 0:P], -1.0,
                                             raw(mxt[:, u % 2, 0]), ALU.mult, ALU.subtract) \
                       .then_inc(s_free[bank(u, KT)], 1)

                def finish(hd, u, lh):
                    dve.wait_ge(p_free, RING + STEPS * hd + KT * (lh + 1))
                    dve.wait_ge(o_out[lh], 32 * hd)
                    dve.tensor_copy(ob[:, lh], p_o[0:VLO, lh]).then_inc(hi_copied, 1)
                    dve.wait_ge(hi_copied, LH * hd + lh + 1)
                    dve.tensor_tensor(ob[0:D, lh], p_o[VLO:VW, lh], ob[0:D, lh], ALU.add).then_inc(o_copied[lh], 1)

                for hd in range(2):
                    for t in range(KT):
                        max_tile(hd, hd, t)
                    if hd == 0:
                        turn_lo(0, 0)

                def body(hd, u, i, last):
                    for s in range(STEPS):
                        if s in MAX_STEP and not (last and u >= SLOTS - 2):
                            max_tile(hd + 2, (u + 2) % SLOTS, MAX_STEP.index(s))
                        if s == 2 and not (last and u == SLOTS - 1):
                            turn_lo(hd + 1, (u + 1) % SLOTS)
                        e = s + 3
                        if dve_lo(e):
                            dve.wait_ge(hi_ready, STEPS * hd + e + 1)
                            dve.tensor_tensor(pl[:, e % RING], pf[:, e % RING], raw(ph[:, e % RING]),
                                              ALU.subtract).then_inc(lo_dve, 1)
                        if s == KT + 1:
                            finish(hd, u, 0)
                    finish(hd, u, 1)

                heads(nc.vector, body)

            @block.scalar
            def _(act):
                def turn_hi(hd, u, puts):
                    act.wait_ge(s_ready, JOBS * (hd + 1))
                    if puts is not None:
                        act.wait_ge(max_in[(u + 2) % SLOTS], 32 * puts)
                    act.activation(mxt[:, u % 2, 0], p_s[0:KT, bank(u, KT), 0:P], ACT.Copy, scale=-1.0) \
                       .then_inc(mxt_hi, 1)

                def exp(hd, s):
                    act.wait_ge(t_ready, STEPS * hd + s + 1)
                    act.wait_ge(p_free, STEPS * hd + s + 1)
                    act.activation(pf[:, s % RING], p_t[:, s % 2], ACT.Exp, scale=SCALE) \
                       .then_inc(exp_done[s % 2], 1)

                def high(hd, s):
                    act.wait_ge(exp_done[s % 2], (STEPS // 2) * hd + s // 2 + 1)
                    act.activation(ph[:, s % RING], pf[:, s % RING], ACT.Copy).then_inc(hi_ready, 1)

                turn_hi(0, 0, None)
                exp(0, 0)

                def body(hd, u, i, last):
                    for s in range(STEPS):
                        if s < STEPS - 1:
                            exp(hd, s + 1)
                        elif not (last and u == SLOTS - 1):
                            exp(hd + 1, 0)
                        high(hd, s)
                        if s == 3 and not (last and u == SLOTS - 1):
                            turn_hi(hd + 1, (u + 1) % SLOTS, i if u == 0 else i + 1)

                heads(nc.scalar, body)

            @block.tensor
            def _(pe):
                pe.sem_inc(p_free, RING)
                pe.wait_ge(ident_made, 1)

                def score_tile(u, i, t):
                    if t == 0:
                        pe.wait_ge(loaded[u], 16 * LOADS * (i + 1))
                    k = bank(u, t)
                    pe.wait_ge(s_free[k], bank_uses(u, i, t))
                    for h in range(L // 512):
                        m = pe.matmul(p_s[:, k, h * 512:(h + 1) * 512], qs[0:SROWS, u, t * P:(t + 1) * P],
                                      ks[0:SROWS, u, h * 512:(h + 1) * 512], start=True, stop=True)
                    m.then_inc(s_ready, 1)

                def turn(u, i):
                    k = bank(u, KT)
                    pe.wait_ge(s_free[1 - k], bank_uses(u, i, KT - 1) + 1)
                    pe.wait_ge(s_free[k], bank_uses(u, i, KT))
                    pe.transpose(p_s[0:KT, k, 0:P], mx[:, u % 2], ident[:]).then_inc(s_ready, 1)

                def scores(hd, u, i, s):
                    lh, t = divmod(s, KT)
                    if s == 0:
                        pe.wait_ge(max_in[u], 32 * (i + 1))
                    pe.wait_ge(exp_done[s % 2], (STEPS // 2) * hd + s // 2)
                    pe.matmul(p_t[:, s % 2], ks[0:MROWS, u, t * P:(t + 1) * P],
                              qs[0:MROWS, u, lh * GT:(lh + 1) * GT], start=True, stop=True) \
                      .then_inc(t_ready, 1)

                def values(hd, u, s):
                    lh, t = divmod(s, KT)
                    if t == 0:
                        pe.wait_ge(o_copied[lh], hd)
                    n_pool, n_dve = lo_counts(hd, s)
                    if dve_lo(s):
                        pe.wait_ge(lo_dve, n_dve)
                    else:
                        pe.wait_ge(lo_pool, n_pool)
                    out = p_o[0:VW, lh]
                    pe.matmul(out, vs[:, u, t], ph[:, s % RING], start=(t == 0), stop=False)
                    m = pe.matmul(out, vs[:, u, t], pl[:, s % RING], start=False, stop=(t == KT - 1))
                    m.then_inc(p_free, 1)

                for hd in range(2):
                    for t in range(KT):
                        score_tile(hd, 0, t)
                    turn(hd, 0)
                for s in range(AHEAD):
                    scores(0, 0, 0, s)

                def body(hd, u, i, last):
                    for s in range(STEPS):
                        if s + AHEAD < STEPS:
                            scores(hd, u, i, s + AHEAD)
                        elif not (last and u == SLOTS - 1):
                            scores(hd + 1, (u + 1) % SLOTS, i + (u == SLOTS - 1), s + AHEAD - STEPS)
                        values(hd, u, s)
                        if not (last and u >= SLOTS - 2):
                            nxt = ((u + 2) % SLOTS, i + (u + 2) // SLOTS)
                            if s in MAX_STEP:
                                score_tile(*nxt, MAX_STEP.index(s))
                            if s == TURN_STEP:
                                turn(*nxt)

                heads(nc.tensor, body)


def stage_proj(nc, o_t, sums, rsums, x, wproj, ada, mod, x2_s, h2_s):
    NK = FULL + 1
    NG = B * L // GT
    AFTER = ((), (0,), (1,), (2, 3, 4))
    with ExitStack() as ctx:
        sb = lambda n, s, d=F32: ctx.enter_context(nc.sbuf_tensor("p_" + n, s, d))
        ps = lambda n, s: ctx.enter_context(nc.psum_tensor("p_psum_" + n, s, F32))
        sem = stage_semaphores(nc, ctx, "p_")
        passed = sem("passed")
        w = sb("w", [P, W_TILES, C], F32R)
        ident = sb("ident", [P, P])
        heads = sb("heads", [H, C])
        sel = sb("sel", [H, CPAD], F32R)
        rs_flat = sb("rs_flat", [P, NHEAD * L // P])
        rs_f = sb("rs_f", [H, L])
        rs = sb("rs", [H, 2, 2, GT], F32R)
        ot = sb("ot", [P, NK, GT])
        of = sb("of", [P, NK, GT])
        oh = sb("oh", [P, 2, A_TILES, GT], F32R)
        xt = sb("xt", [P, 2, SUB, C])
        gt = sb("gt", [P, 2, 3, C])
        md = sb("md", [P, 2, len(MOD) * NK])
        x2 = sb("x2", [P, 2, SUB, C])
        xn = sb("xn", [P, SUB, CPAD])
        stats = sb("stats", [P, SUB, 2, 6])
        mv = sb("mv", [P, SUB, 2])
        small = sb("small", [P, 5, SUB])
        rstd = sb("rstd", [P, SUB])
        shift = sb("shift", [P, SUB])
        hf = sb("hf", [P, 2, GT])
        ht = sb("ht", [P, A_TILES, GT], F32R)
        p_r = ps("r", [P, 2, GT])
        p_p = ps("p", [P, 2, 2, 512])
        p_t = ps("t", [P, 2, GT])

        w_in, zeroed, ident_made, set_up = sem("w_in"), sem("zeroed"), sem("ident_made"), sem("set_up")
        sums_in, rs_made, rs_out = sem("sums_in"), sem("rs_made"), sem("rs_out")
        rs_in, rs_hi, rs_lo = sem("rs_in"), sem("rs_hi"), sem("rs_lo")
        o_in, r_ready, of_ready, oh_ready, ol_ready = (
            sem("o_in"), sem("r_ready"), sem("of_ready"), sem("oh_ready"), sem("ol_ready"))
        x_in = [sem(f"x_in{i}") for i in range(2)]
        md_in = [sem(f"md_in{i}") for i in range(2)]
        xb_ready, p_ready, gated, x2_ready = sem("xb_ready"), sem("p_ready"), sem("gated"), sem("x2_ready")
        link_done, var_ready, std_ready, rstd_ready = (
            sem("link_done"), sem("var_ready"), sem("std_ready"), sem("rstd_ready"))
        xn_ready, x2b_ready = sem("xn_ready"), sem("x2b_ready")
        x2b_out = [sem(f"x2b_out{i}") for i in range(2)]
        t_ready, hi_ready, full_ready, lo_ready = (
            sem("t_ready"), sem("hi_ready"), sem("full_ready"), sem("lo_ready"))
        h_out = [sem(f"h_out{c}") for c in range(NK)]

        def groups(eng, body):
            with eng.Fori(0, B - 1) as b:
                body(2 * b, b, 0, 2)
                body(2 * b + 1, b, 1, 2)
            body(NG - 2, B - 1, 0, 1)
            body(NG - 1, B - 1, 1, 0)

        with nc.Block() as block:
            @block.sync
            def _(sp):
                flat = "h (a n) -> (h a) n"
                sp.dma_start(rs_flat[:], sums.rearrange(flat, n=NHEAD * L // P)).then_inc(sums_in, 16)

                def load_x(g, b, half):
                    sp.dma_start(xt[:, half], x[bass.ds(g * GT, GT), :].rearrange("(t p) c -> p t c", p=P)) \
                      .then_inc(x_in[half], 16)
                    for i, s in enumerate((GATE_MSA, GB_PROJ)):
                        sp.dma_start(gt[:, half, i], ada[bass.ds(b, 1), s * C:(s + 1) * C].broadcast_to([P, C])) \
                          .then_inc(x_in[half], 16)

                def load_mod(b, half):
                    sp.dma_start(gt[:, half, 2], ada[bass.ds(b, 1), GB_FC2 * C:(GB_FC2 + 1) * C].broadcast_to([P, C])) \
                      .then_inc(md_in[half], 16)
                    sp.dma_start(md[:, half], mod[bass.ds(b, 1)].rearrange("a p n -> (a p) n")) \
                      .then_inc(md_in[half], 16)

                def load_o(g, b, half):
                    cols = slice(half * GT, (half + 1) * GT)
                    sp.dma_start(ot[:, 0:FULL], o_t[bass.ds(b * C, FULL * P), cols]
                                 .rearrange("(k p) n -> p k n", p=P)).then_inc(o_in, 16)
                    for r in range(2):
                        sp.dma_start(ot[r * REM:(r + 1) * REM, FULL], o_t[bass.ds(b * C + FULL * P, REM), cols]) \
                          .then_inc(o_in, 16)

                def load_rs(b, half):
                    sp.dma_start(rs_f[:, 0:GT], rsums[bass.ds(b * H, H), half * GT:(half + 1) * GT]).then_inc(o_in, 16)

                load_o(0, 0, 0)
                load_x(0, 0, 0)
                sp.wait_ge(rs_made, 1)
                sp.dma_start(rsums.rearrange(flat, n=NHEAD * L // P), rs_flat[:]).then_inc(rs_out, 16)
                load_split_weight(sp, w, wproj, slice(0, C), w_in)
                sp.wait_ge(rs_out, 16)
                load_rs(0, 0)
                load_mod(0, 0)
                sp.wait_ge(of_ready, NK)
                sp.wait_ge(rs_lo, 1)
                load_o(1, 0, 1)
                load_rs(0, 1)
                load_x(1, 0, 1)
                load_mod(0, 1)
                sp.wait_ge(of_ready, 2 * NK)
                sp.wait_ge(rs_lo, 2)
                load_o(2, 1, 0)
                load_rs(1, 0)

                def body(g, b, half, more):
                    if more >= 2:
                        sp.wait_ge(x2_ready, g + 1)
                        load_x(g + 2, b + 1, half)
                    sp.wait_ge(x2b_ready, g + 1)
                    sp.dma_start(x2_s[bass.ds(g * GT, GT), :].rearrange("(t p) c -> p t c", p=P), x2[:, half]) \
                      .then_inc(x2b_out[half], 16)
                    if more == 3:
                        sp.wait_ge(of_ready, NK * (g + 3))
                        sp.wait_ge(rs_lo, g + 3)
                        load_o(g + 3, b + 1 + half, 1 - half)
                        load_rs(b + 1 + half, 1 - half)
                    for c in range(NK):
                        sp.wait_ge(lo_ready, NK * g + c + 3)
                        sp.dma_start(h2_s[bass.ds(g, 1)].rearrange("a p (s k) n -> (a p) s k n", s=2)[:, :, c],
                                     raw(ht[:].rearrange("p (s k) n -> p s k n", s=2)[:, :, c])) \
                          .then_inc(h_out[c], 16)
                    if more >= 2:
                        load_mod(b + 1, half)

                with nc.sync.Fori(0, B - 2) as b:
                    body(2 * b, b, 0, 3)
                    body(2 * b + 1, b, 1, 3)
                for g in range(NG - 4, NG):
                    body(g, g // 2, g % 2, min(3, NG - 1 - g))
                for i in range(2):
                    sp.wait_ge(x2b_out[i], 16 * NG // 2)
                for c in range(NK):
                    sp.wait_ge(h_out[c], 16 * NG)

            @block.gpsimd
            def _(pool):
                make_identity(nc, pool, ident, zeroed, ident_made)
                pool.wait_ge(ident_made, 1)
                pool.memset(heads[:], 1.0).then_inc(set_up, 1)
                pool.wait_ge(set_up, 1)
                pool.affine_select(out=heads[:], in_=heads[:], compare_op=ALU.is_ge, fill=0.0, base=0,
                                   pattern=[[1, C]], channel_multiplier=-D).then_inc(set_up, 1)
                pool.wait_ge(set_up, 2)
                pool.affine_select(out=heads[:], in_=heads[:], compare_op=ALU.is_ge, fill=0.0, base=D - 1,
                                   pattern=[[-1, C]], channel_multiplier=D).then_inc(set_up, 1)

                def biased_x(g, b, half):
                    pool.wait_ge(x_in[half], 48 * (b + 1))
                    for t in range(SUB):
                        i = pool.tensor_tensor(xt[:, half, t], xt[:, half, t], gt[:, half, 1], ALU.add)
                    i.then_inc(xb_ready, 1)

                biased_x(0, 0, 0)
                biased_x(1, 0, 1)

                def body(g, b, half, more):
                    if not (isinstance(g, int) and g == 0):
                        pool.wait_ge(t_ready, NK * g)
                    wait_alone(pool, rstd_ready, g + 1, passed)
                    for t in range(SUB):
                        for a, z, o in ((0, C, 0), (FULL * P, C, C)):
                            i = pool.tensor_scalar(xn[:, t, o:o + z - a], x2[:, half, t, a:z],
                                                   rstd[:, t:t + 1], shift[:, t:t + 1], ALU.mult, ALU.add)
                    i.then_inc(xn_ready, 1)
                    pool.wait_ge(md_in[half], 32 * (b + 1))
                    pool.wait_ge(xn_ready, g + 1)
                    for t in range(SUB):
                        i = pool.tensor_tensor(x2[:, half, t], x2[:, half, t], gt[:, half, 2], ALU.add)
                    i.then_inc(x2b_ready, 1)
                    if more == 2:
                        biased_x(g + 2, b + 1, half)
                    for c in range(NK):
                        pool.wait_ge(full_ready, NK * g + c + 3)
                        pool.tensor_tensor(ht[:, NK + c], hf[:, c_slot(half, c)], raw(ht[:, c]), ALU.subtract) \
                            .then_inc(lo_ready, 1)

                groups(nc.gpsimd, body)

            @block.vector
            def _(dve):
                dve.sem_inc(lo_ready, 2)
                dve.wait_ge(sums_in, 16)
                dve.reciprocal(rs_flat[:], rs_flat[:]).then_inc(rs_made, 1)
                dve.wait_ge(set_up, 3)
                dve.tensor_copy(sel[:, 0:C], heads[:]).then_inc(set_up, 1)
                dve.tensor_copy(sel[:, C:CPAD], heads[:, FULL * P:C]).then_inc(set_up, 1)

                def operand(g, half, c):
                    if c == 0:
                        dve.wait_ge(rs_hi, g + 1)
                        dve.tensor_tensor(rs[:, half, 1], rs_f[:, 0:GT], raw(rs[:, half, 0]), ALU.subtract) \
                           .then_inc(rs_lo, 1)
                    dve.wait_ge(r_ready, NK * g + c + 1)
                    dve.tensor_tensor(of[:, c], ot[:, c], p_r[:, c_slot(half, c)], ALU.mult) \
                       .then_inc(of_ready, 1)

                def operand_lo(g, half, c):
                    dve.wait_ge(oh_ready, NK * g + c + 1)
                    dve.tensor_tensor(oh[:, half, NK + c], of[:, c], raw(oh[:, half, c]), ALU.subtract) \
                       .then_inc(ol_ready, 1)

                def gate(g, b, half, t, a):
                    if t == 0 and a == 0:
                        dve.wait_ge(xb_ready, g + 1)
                        if not (isinstance(g, int) and g < 2):
                            dve.wait_ge(x2b_out[half], 16 * b)
                    dve.wait_ge(p_ready, 2 * (SUB * g + t) + a + 1)
                    cols = slice(a * HALF, (a + 1) * HALF)
                    dve.tensor_tensor(x2[:, half, t, cols], p_p[:, t % 2, a, 0:HALF], gt[:, half, 0, cols],
                                      ALU.mult).then_inc(gated, 1)

                def residual(g, half, t):
                    dve.wait_ge(gated, 2 * (SUB * g + t) + 2)
                    i = dve.tensor_tensor(x2[:, half, t], x2[:, half, t], xt[:, half, t], ALU.add)
                    if t == SUB - 1:
                        i.then_inc(x2_ready, 1)

                LINKS = 7

                def statistics(g, half):
                    def link(ins, n):
                        ins.then_inc(link_done, 1)
                        dve.wait_ge(link_done, LINKS * g + n)

                    dve.wait_ge(x2_ready, g + 1)
                    for t in range(SUB):
                        for a in range(2):
                            i = dve.bn_stats(stats[:, t, a], x2[:, half, t, a * HALF:(a + 1) * HALF])
                    i.then_inc(link_done, 1)
                    wait_alone(dve, link_done, LINKS * g + 1, passed)
                    for t in range(SUB):
                        i = dve.bn_aggr(mv[:, t], stats[:, t].rearrange("p a s -> p (a s)"))
                    link(i, 2)
                    ve, std, r0, r2, cor = (small[:, k] for k in range(5))
                    dve.tensor_scalar(ve, mv[:, :, 1], LN_EPS, None, ALU.add).then_inc(var_ready, 1)
                    dve.wait_ge(std_ready, g + 1)
                    link(dve.reciprocal(r0, std), 3)
                    link(dve.tensor_tensor(r2, r0, r0, ALU.mult), 4)
                    link(dve.tensor_tensor(r2, r2, ve, ALU.mult), 5)
                    link(dve.tensor_scalar(cor, r2, -0.5, 1.5, ALU.mult, ALU.add), 6)
                    if not (isinstance(g, int) and g == 0):
                        dve.wait_ge(xn_ready, g)
                    link(dve.tensor_tensor(rstd[:], r0, cor, ALU.mult), 7)
                    dve.scalar_tensor_tensor(shift[:], mv[:, :, 0], -1.0, rstd[:], ALU.mult, ALU.mult) \
                       .then_inc(rstd_ready, 1)

                for g in range(2):
                    for c in range(NK):
                        operand(g, g, c)
                        operand_lo(g, g, c)
                    if g == 0:
                        for t in range(SUB):
                            for a in range(2):
                                gate(0, 0, 0, t, a)
                            residual(0, 0, t)

                def body(g, b, half, more):
                    statistics(g, half)
                    for t in range(SUB):
                        if more >= 1:
                            for a in range(2):
                                gate(g + 1, b + half, 1 - half, t, a)
                            residual(g + 1, 1 - half, t)
                        if more == 2:
                            for c in AFTER[t]:
                                operand(g + 2, half, c)
                                if c:
                                    operand_lo(g + 2, half, c - 1)
                    if more == 2:
                        operand_lo(g + 2, half, NK - 1)
                    for c in range(NK):
                        dve.wait_ge(hi_ready, NK * g + c + 1)
                        dve.wait_ge(lo_ready, NK * g + c + 1)
                        k = 2 * NK + c
                        dve.tensor_scalar(hf[:, c_slot(half, c)], p_t[:, c_slot(half, c)],
                                          md[:, half, k + NK:k + NK + 1], md[:, half, k:k + 1],
                                          ALU.mult, ALU.add).then_inc(full_ready, 1)

                groups(nc.vector, body)

            @block.scalar
            def _(act):
                def operand_hi(g, half):
                    act.wait_ge(o_in, 64 * (g + 1))
                    if not (isinstance(g, int) and g < 2):
                        act.wait_ge(r_ready, NK * (g - 1))
                        act.wait_ge(p_ready, 2 * SUB * (g - 1))
                    act.activation(rs[:, half, 0], rs_f[:, 0:GT], ACT.Copy).then_inc(rs_hi, 1)
                    for c in range(NK):
                        act.wait_ge(of_ready, NK * g + c + 1)
                        act.activation(oh[:, half, c], of[:, c], ACT.Copy).then_inc(oh_ready, 1)

                operand_hi(0, 0)
                operand_hi(1, 1)

                def body(g, b, half, more):
                    act.wait_ge(var_ready, g + 1)
                    act.activation(small[:, 1], small[:, 0], ACT.Sqrt).then_inc(std_ready, 1)
                    if more == 2:
                        operand_hi(g + 2, half)
                    act.wait_ge(md_in[half], 32 * (b + 1))
                    for c in range(NK):
                        act.wait_ge(h_out[c], 16 * g)
                        act.wait_ge(t_ready, NK * g + c + 1)
                        k = 2 * NK + c
                        act.activation(ht[:, c], p_t[:, c_slot(half, c)], ACT.Identity,
                                       bias=md[:, half, k:k + 1], scale=md[:, half, k + NK:k + NK + 1]) \
                           .then_inc(hi_ready, 1)

                groups(nc.scalar, body)

            @block.tensor
            def _(pe):
                def spread(g, half, c):
                    pe.wait_ge(rs_lo, g + 1)
                    if not (isinstance(g, int) and g == 0 and c < 2):
                        pe.wait_ge(of_ready, NK * g + c - 1)
                    for s in range(2):
                        i = pe.matmul(p_r[:, c_slot(half, c)], sel[:, c * P:(c + 1) * P], rs[:, half, s],
                                      start=(s == 0), stop=(s == 1))
                    i.then_inc(r_ready, 1)

                def project(g, half, t):
                    if t == 0:
                        pe.wait_ge(oh_ready, NK * (g + 1))
                        pe.wait_ge(ol_ready, NK * (g + 1))
                    for a in range(2):
                        if t >= 2 or not (isinstance(g, int) and g == 0):
                            pe.wait_ge(gated, 2 * (SUB * g + t - 2) + a + 1)
                        for n, (k, j) in enumerate(PASSES):
                            i = pe.matmul(p_p[:, t % 2, a, 0:HALF], oh[:, half, k, t * P:(t + 1) * P],
                                          w[:, j, a * HALF:(a + 1) * HALF],
                                          start=(n == 0), stop=(n == len(PASSES) - 1))
                        i.then_inc(p_ready, 1)

                pe.sem_inc(full_ready, 2)
                pe.wait_ge(ident_made, 1)
                pe.wait_ge(set_up, 5)
                for c in range(NK):
                    spread(0, 0, c)
                pe.wait_ge(w_in, 64)
                for t in range(SUB):
                    project(0, 0, t)
                for c in range(NK):
                    spread(1, 1, c)

                def body(g, b, half, more):
                    for t in range(SUB):
                        if more >= 1:
                            project(g + 1, 1 - half, t)
                        if more == 2:
                            for c in AFTER[t]:
                                spread(g + 2, half, c)
                    pe.wait_ge(xn_ready, g + 1)
                    for c in range(NK):
                        pe.wait_ge(full_ready, NK * g + c + 1)
                        for t in range(SUB):
                            i = pe.transpose(p_t[:, c_slot(half, c), t * P:(t + 1) * P],
                                             xn[:, t, c * P:(c + 1) * P], ident[:])
                        i.then_inc(t_ready, 1)

                groups(nc.tensor, body)


def stage_mlp(nc, h2_s, x2_s, w1_s, b1, w2_s, gates, x3_s):
    FT = FF // P
    GM = GT // 2
    NT = GM // P
    NG = B * L // GM
    RING = 3
    AHEAD = 2
    PARTS = 6
    PF = FT // PARTS
    with ExitStack() as ctx:
        sb = lambda n, s, d=F32: ctx.enter_context(nc.sbuf_tensor("m_" + n, s, d))
        ps = lambda n, s: ctx.enter_context(nc.psum_tensor("m_psum_" + n, s, F32))
        sem = stage_semaphores(nc, ctx, "m_")
        w1 = sb("w1", [P, W_TILES, FF], F32R)
        w2 = sb("w2", [P, 2, FT, C], F32R)
        bias1 = sb("bias1", [P, FT])
        gt = sb("gt", [P, 2, C])
        ht = sb("ht", [P, 2, A_TILES, GM], F32R)
        af = sb("af", [P, RING, GM])
        ah = sb("ah", [P, RING, GM], F32R)
        al = sb("al", [P, RING, GM], F32R)
        xt = sb("xt", [P, NT, C])
        y = sb("y", [P, NT, C])
        p_h = ps("h", [P, RING, 512])
        p_y = ps("y", [P, NT, 2, 512])

        bias_in = sem("bias_in")
        w1_in = [sem(f"w1_in{i}") for i in range(PARTS)]
        w2_in = [sem(f"w2_in{i}") for i in range(PARTS)]
        ht_in = [sem(f"ht_in{i}") for i in range(2)]
        gt_in = [sem(f"gt_in{i}") for i in range(2)]
        x_in = [sem(f"x_in{i}") for i in range(NT)]
        h_ready, act_ready, hi_ready, lo_ready, used = (
            sem("h_ready"), sem("act_ready"), sem("hi_ready"), sem("lo_ready"), sem("used"))
        gated, summed = sem("gated"), sem("summed")
        y_out = [sem(f"y_out{i}") for i in range(NT)]

        def groups(eng, body):
            with eng.Fori(0, NG // 2 - 1) as j:
                body(2 * j, j, 0, False)
                body(2 * j + 1, j, 1, False)
            body(NG - 2, NG // 2 - 1, 0, False)
            body(NG - 1, NG // 2 - 1, 1, True)

        with nc.Block() as block:
            @block.sync
            def _(sp):
                def load_h(j, q):
                    sp.dma_start(raw(ht[:, q]), h2_s[bass.ds(j, 1), :, :, q * GM:(q + 1) * GM]
                                 .rearrange("a p k n -> (a p) k n")).then_inc(ht_in[q], 16)

                def load_gate(j, q):
                    sp.dma_start(gt[:, q], gates[bass.ds(j, 1), :].broadcast_to([P, C])).then_inc(gt_in[q], 16)

                def load_x(n, t):
                    sp.dma_start(xt[:, t], x2_s[bass.ds(n * GM + t * P, P), :]).then_inc(x_in[t], 16)

                sp.dma_start(bias1[:], b1.rearrange("(f p) -> p f", p=P),
                             allow_slow_non_contiguous=True).then_inc(bias_in, 16)
                load_h(0, 0)
                for i in range(PARTS):
                    cols = slice(i * PF * P, (i + 1) * PF * P)
                    load_split_weight(sp, w1[:, :, cols], w1_s, cols, w1_in[i])
                    for s in range(2):
                        sp.dma_start(raw(w2[:, s, i * PF:(i + 1) * PF]),
                                     w2_s[s, cols].rearrange("(f p) n -> p f n", p=P)).then_inc(w2_in[i], 16)
                load_h(0, 1)
                for q in range(2):
                    load_gate(0, q)
                for t in range(NT):
                    load_x(0, t)

                def body(n, j, q, last):
                    for t in range(NT):
                        sp.wait_ge(summed, NT * n + t + 1)
                        sp.dma_start(x3_s[bass.ds(n * GM + t * P, P), :], y[:, t]).then_inc(y_out[t], 16)
                        if not last:
                            load_x(n + 1, t)
                    if not (isinstance(n, int) and n >= NG - 2):
                        load_h(j + 1, q)
                        load_gate(j + 1, q)

                groups(nc.sync, body)
                for t in range(NT):
                    sp.wait_ge(y_out[t], 16 * NG)

            @block.scalar
            def _(act):
                act.wait_ge(bias_in, 16)

                def activate(n, f):
                    act.wait_ge(h_ready, FT * n + f + 1)
                    act.wait_ge(used, FT * n + f + 1)
                    act.activation(af[:, f % RING], p_h[:, f % RING, 0:GM], ACT.Gelu_apprx_tanh,
                                   bias=bias1[:, f:f + 1]).then_inc(act_ready, 1)

                def body(n, j, q, last):
                    for f in range(FT):
                        activate(n, f)

                groups(nc.scalar, body)

            @block.gpsimd
            def _(pool):
                def body(n, j, q, last):
                    for f in range(FT):
                        pool.wait_ge(hi_ready, FT * n + f + 1)
                        pool.tensor_tensor(al[:, f % RING], af[:, f % RING], raw(ah[:, f % RING]),
                                           ALU.subtract).then_inc(lo_ready, 1)

                groups(nc.gpsimd, body)

            @block.vector
            def _(dve):
                def high(n, f):
                    dve.wait_ge(act_ready, FT * n + f + 1)
                    dve.tensor_copy(ah[:, f % RING], af[:, f % RING]).then_inc(hi_ready, 1)

                for f in range(AHEAD):
                    high(0, f)

                def body(n, j, q, last):
                    for f in range(FT):
                        if f + AHEAD < FT:
                            high(n, f + AHEAD)
                        elif not last:
                            high(n + 1, f + AHEAD - FT)
                    dve.wait_ge(used, RING + FT * (n + 1))
                    dve.wait_ge(gt_in[q], 16 * (j + 1))
                    for t in range(NT):
                        dve.wait_ge(y_out[t], 16 * n)
                        for a in range(2):
                            cols = slice(a * HALF, (a + 1) * HALF)
                            dve.tensor_tensor(y[:, t, cols], p_y[:, t, a, 0:HALF], gt[:, q, cols],
                                              ALU.mult).then_inc(gated, 1)
                    for t in range(NT):
                        dve.wait_ge(x_in[t], 16 * (n + 1))
                        dve.wait_ge(gated, 2 * (NT * n + t) + 2)
                        dve.tensor_tensor(y[:, t], y[:, t], xt[:, t], ALU.add).then_inc(summed, 1)

                groups(nc.vector, body)

            @block.tensor
            def _(pe):
                pe.sem_inc(used, RING)

                def first(n, j, q, f):
                    if f == 0:
                        pe.wait_ge(ht_in[q], 16 * (j + 1))
                    if q == 0 and f % PF == 0:
                        pe.wait_ge(w1_in[f // PF], 64)
                    if not (isinstance(n, int) and n == 0 and f < RING):
                        pe.wait_ge(act_ready, FT * n + f + 1 - RING)
                    for i, (a, k) in enumerate(PASSES):
                        m = pe.matmul(p_h[:, f % RING, 0:GM], w1[:, k, f * P:(f + 1) * P], ht[:, q, a],
                                      start=(i == 0), stop=(i == len(PASSES) - 1))
                    m.then_inc(h_ready, 1)

                def second(n, q, f):
                    pe.wait_ge(lo_ready, FT * n + f + 1)
                    if q == 0 and f % PF == 0:
                        pe.wait_ge(w2_in[f // PF], 32)
                    for t in range(NT):
                        for a in range(2):
                            if f == 0:
                                pe.wait_ge(gated, 2 * NT * n)
                            for i, (part, s) in enumerate(((ah, 0), (al, 0), (ah, 1))):
                                m = pe.matmul(p_y[:, t, a, 0:HALF], part[:, f % RING, t * P:(t + 1) * P],
                                              w2[:, s, f, a * HALF:(a + 1) * HALF],
                                              start=(f == 0 and i == 0), stop=(f == FT - 1 and i == 2))
                    m.then_inc(used, 1)

                for f in range(AHEAD):
                    first(0, 0, 0, f)

                def body(n, j, q, last):
                    for f in range(FT):
                        if f + AHEAD < FT:
                            first(n, j, q, f + AHEAD)
                        elif not last:
                            first(n + 1, j + q, 1 - q, f + AHEAD - FT)
                        second(n, q, f)

                groups(nc.tensor, body)


def stage_rotate(nc, x3_s, u_s, rot_s, out):
    NK = FULL + 1
    NG = B * L // GT
    with ExitStack() as ctx:
        sb = lambda n, s, d=F32: ctx.enter_context(nc.sbuf_tensor("r_" + n, s, d))
        ps = lambda n, s: ctx.enter_context(nc.psum_tensor("r_psum_" + n, s, F32))
        sem = stage_semaphores(nc, ctx, "r_")
        ident = sb("ident", [P, P])
        u = sb("u", [P, NK, 2 * R], F32R)
        ro = sb("ro", [P, B, 2, C], F32R)
        xt = sb("xt", [P, NG, SUB, CPAD])
        xh = sb("xh", [P, 2, NK, GT], F32R)
        xl = sb("xl", [P, 2, NK, GT], F32R)
        z = sb("z", [P, 2, 2, GT], F32R)
        y = sb("y", [P, SUB, C])
        p_t = ps("t", [P, 2, GT])
        p_z = ps("z", [P, GT])
        p_y = ps("y", [P, 2, 2, 512])

        u_in, zeroed, ident_made = sem("u_in"), sem("zeroed"), sem("ident_made")
        x_in = [sem(f"x_in{g}") for g in range(NG)]
        ro_in = [sem(f"ro_in{b}") for b in range(B)]
        t_ready, hi_ready, lo_ready = sem("t_ready"), sem("hi_ready"), sem("lo_ready")
        z_ready, z_hi, z_lo = sem("z_ready"), sem("z_hi"), sem("z_lo")
        y_ready, summed = sem("y_ready"), sem("summed")
        y_out = [sem(f"y_out{t}") for t in range(SUB)]

        def groups(body):
            for g in range(NG):
                body(g, g % 2, g == NG - 1)

        with nc.Block() as block:
            @block.sync
            def _(sp):
                sp.dma_start(raw(u[:]), u_s).then_inc(u_in, 16)
                for g in range(NG):
                    rows = x3_s[g * GT:(g + 1) * GT].rearrange("(t p) c -> p t c", p=P)
                    sp.dma_start(xt[:, g, :, 0:C], rows).then_inc(x_in[g], 16)
                    sp.dma_start(xt[:, g, :, C:CPAD], rows[:, :, FULL * P:C]).then_inc(x_in[g], 16)
                    if g % 2 == 0:
                        for r in range(2):
                            sp.dma_start(raw(ro[r * R:(r + 1) * R, g // 2]), rot_s[g // 2]
                                         .rearrange("s r c -> r s c")).then_inc(ro_in[g // 2], 16)

                def body(g, half, last):
                    for t in range(SUB):
                        sp.wait_ge(summed, 2 * (SUB * g + t + 1))
                        sp.dma_start(out[g * GT + t * P:g * GT + (t + 1) * P], y[:, t]).then_inc(y_out[t], 16)

                groups(body)
                for t in range(SUB):
                    sp.wait_ge(y_out[t], 16 * NG)

            @block.gpsimd
            def _(pool):
                make_identity(nc, pool, ident, zeroed, ident_made)

            @block.scalar
            def _(act):
                def highs(g, half):
                    for c in range(NK):
                        act.wait_ge(t_ready, NK * g + c + 1)
                        if c == 0 and g >= 2:
                            act.wait_ge(z_ready, g - 1)
                        act.activation(xh[:, half, c], p_t[:, c_slot(half, c)], ACT.Copy).then_inc(hi_ready, 1)

                highs(0, 0)

                def body(g, half, last):
                    act.wait_ge(z_ready, g + 1)
                    act.wait_ge(y_ready, 2 * SUB * g)
                    act.activation(z[:, half, 0], p_z[:], ACT.Copy).then_inc(z_hi, 1)
                    if not last:
                        highs(g + 1, 1 - half)

                groups(body)

            @block.vector
            def _(dve):
                def lows(g, half):
                    for c in range(NK):
                        dve.wait_ge(hi_ready, NK * g + c + 1)
                        dve.tensor_tensor(xl[:, half, c], p_t[:, c_slot(half, c)], raw(xh[:, half, c]),
                                          ALU.subtract).then_inc(lo_ready, 1)

                lows(0, 0)

                def body(g, half, last):
                    dve.wait_ge(z_hi, g + 1)
                    dve.tensor_tensor(z[:, half, 1], p_z[:], raw(z[:, half, 0]), ALU.subtract).then_inc(z_lo, 1)
                    if not last:
                        lows(g + 1, 1 - half)
                    for t in range(SUB):
                        dve.wait_ge(y_out[t], 16 * g)
                        for a in range(2):
                            cols = slice(a * HALF, (a + 1) * HALF)
                            dve.wait_ge(y_ready, 2 * (SUB * g + t) + a + 1)
                            dve.tensor_tensor(y[:, t, cols], p_y[:, t % 2, a, 0:HALF], xt[:, g, t, cols],
                                              ALU.add).then_inc(summed, 1)

                groups(body)

            @block.tensor
            def _(pe):
                def transposes(g, half):
                    pe.wait_ge(x_in[g], 32)
                    for c in range(NK):
                        if NK * g + c >= 2:
                            pe.wait_ge(lo_ready, NK * g + c - 1)
                        for t in range(SUB):
                            i = pe.transpose(p_t[:, c_slot(half, c), t * P:(t + 1) * P],
                                             xt[:, g, t, c * P:(c + 1) * P], ident[:])
                        i.then_inc(t_ready, 1)

                pe.wait_ge(ident_made, 1)
                transposes(0, 0)
                pe.wait_ge(u_in, 16)

                def body(g, half, last):
                    pe.wait_ge(lo_ready, NK * (g + 1))
                    pe.wait_ge(z_lo, g)
                    n = 0
                    for part in (xh, xl):
                        for c in range(NK):
                            i = pe.matmul(p_z[:], u[:, c], part[:, half, c], start=(n == 0),
                                          stop=(n == 2 * NK - 1))
                            n += 1
                    i.then_inc(z_ready, 1)
                    if not last:
                        transposes(g + 1, 1 - half)
                    pe.wait_ge(z_lo, g + 1)
                    pe.wait_ge(ro_in[g // 2], 32)
                    for t in range(SUB):
                        for a in range(2):
                            if SUB * g + t >= 2:
                                pe.wait_ge(summed, 2 * (SUB * g + t - 2) + a + 1)
                            for n, (s, r) in enumerate(((0, 0), (1, 0), (0, 1))):
                                i = pe.matmul(p_y[:, t % 2, a, 0:HALF], z[:, half, s, t * P:(t + 1) * P],
                                              ro[:, g // 2, r, a * HALF:(a + 1) * HALF],
                                              start=(n == 0), stop=(n == 2))
                            i.then_inc(y_ready, 1)

                groups(body)


def stage_prepare(nc, cond, w_ada, b_ada, b_proj, b_fc2, weights, p_in, w_skew, b_skew, ada, mod, gates, u_s, rot_s):
    NK = FULL + 1
    NT = 8
    WT = SEC * C // NT
    NV = 4
    TQ = 4
    TR = NSKEW // (NV * TQ)
    VT = TQ * TR
    A_RING = 3
    BLK = 1296
    RING = 3
    SQUARINGS = 16
    TERMS = 4
    PER = R // SQUARINGS
    blocks = []
    for src, dst in weights:
        n = src.shape[0] * src.shape[1] // P
        s = src.rearrange("r n -> (r n)").rearrange("(p m) -> p m", p=P)
        d = dst.rearrange("s r n -> s (r n)").rearrange("s (p m) -> p s m", p=P)
        blocks += [(s[:, i:i + BLK], d[:, :, i:i + BLK]) for i in range(0, n, BLK)]

    with ExitStack() as ctx:
        sb = lambda n, s, d=F32: ctx.enter_context(nc.sbuf_tensor("c_" + n, s, d))
        ps = lambda n, s: ctx.enter_context(nc.psum_tensor("c_psum_" + n, s, F32))
        sem = stage_semaphores(nc, ctx, "c_")
        ident = sb("ident", [P, P])
        sct = sb("sct", [P, NK, B])
        wa = sb("wa", [P, A_RING, NK, WT])
        bb = sb("bb", [B, 2, C])
        cs = sb("cs", [B, 2, C])
        av = sb("av", [B, 8 * C])
        am = sb("am", [B, len(MOD), CPAD])
        mt = sb("mt", [P, B, len(MOD) * NK])
        wf = sb("wf", [P, RING, BLK])
        ws = sb("ws", [P, RING, 2, BLK], F32R)
        wr = sb("wr", [TR, 2, TQ, C])
        wt = sb("wt", [P, 2, FULL, VT])
        wl = sb("wl", [REM + 1, NSKEW])
        v = sb("v", [B, NSKEW])
        up = sb("up", [R, B, R])
        a2 = sb("a2", [R, B, R])
        sa = sb("sa", [R, B, 2, R])
        ex = sb("ex", [R, B, 2, R])
        ts = sb("ts", [R, B, 2, R])
        pp = sb("pp", [P, NK, R])
        sel = sb("sel", [R, R, R])
        m = sb("m", [R, 2 * R])
        neg = sb("neg", [R, R])
        upm = sb("upm", [R, R])
        col = sb("col", [R, 8])
        zs = sb("zs", [R, R])
        sq = sb("sq", [R, R])
        lst = sb("lst", [R, R])
        phi = sb("phi", [R, R])
        pt = sb("pt", [R, C])
        qt = sb("qt", [R, C])
        ut = sb("ut", [R, C])
        q = sb("q", [P, NK, R])
        us = sb("us", [P, NK, 2 * R], F32R)
        ro = sb("ro", [R, 2, 2, C], F32R)
        p_w = ps("w", [P, 2, 512])
        p_v = ps("v", [P, 2, 512])
        p_b = ps("b", [R, 512])
        p_g = ps("g", [P, 512])
        p_s = ps("s", [R, B, 2, 2 * R])
        p_q = p_g[:, R:R + NK * R].rearrange("p (k n) -> p k n", n=R)
        p_m = p_v[:, 0, 0:len(MOD) * NK * B].rearrange("p (n b) -> p n b", b=B)
        p_c = p_v[:, 1, 0:NK * B].rearrange("p (k b) -> p k b", b=B)

        zeroed, ident_made, masks, set_up = sem("zeroed"), sem("ident_made"), sem("masks"), sem("set_up")
        c_in, b_in, pp_in, wl_in = sem("c_in"), sem("b_in"), sem("pp_in"), sem("wl_in")
        wr_in = [sem(f"wr_in{i}") for i in range(2)]
        wa_in = [sem(f"wa_in{i}") for i in range(A_RING)]
        silu_done, c_turned, sct_ready = sem("silu_done"), sem("c_turned"), sem("sct_ready")
        w_turned, wt_ready, v_ready, v_done, up_in = (
            sem("w_turned"), sem("wt_ready"), sem("v_ready"), sem("v_done"), sem("up_in"))
        bias_gated, am_ready, m_turned, mt_ready = (
            sem("bias_gated"), sem("am_ready"), sem("m_turned"), sem("mt_ready"))
        wf_in = [sem(f"wf_in{i}") for i in range(RING)]
        ws_out = [sem(f"ws_out{i}") for i in range(RING)]
        w_hi, w_lo = sem("w_hi"), sem("w_lo")
        pe_done, dve_done, act_done = sem("pe_done"), sem("dve_done"), sem("act_done")
        row_spread, row2_spread = sem("row_spread"), sem("row2_spread")
        step_done, step2_done = sem("step_done"), sem("step2_done")
        sq_ready, ex_ready = sem("sq_ready"), sem("ex_ready")
        us_hi, us_lo, ro_ready, ro_hi, ro_lo, out_done = (
            sem("us_hi"), sem("us_lo"), sem("ro_ready"), sem("ro_hi"), sem("ro_lo"), sem("out_done"))
        ro_out = [sem(f"ro_out{i}") for i in range(2)]
        rows = lambda k: P if k < FULL else REM
        halves = ((0, HALF), (HALF, C))

        PE_STEPS = ("gram", "p_turned", "l_turned", "q_ready", "q_turned", "gram2", "fix", "top", "a_turned") \
            + tuple(f"taylor{i}" for i in range(1, TERMS)) + ("u_turned",)
        DVE_STEPS = ("m_ready", "pt", "diag", "diag_sum", "inv_std", "scaled", "lst", "qt", "q", "phi0", "phi",
                     "qt2", "m2_ready", "a2", "sa", "y0") \
            + tuple(f"{x}{i}" for i in range(1, TERMS) for x in ("sum", "y")) + ("sign_diag", "signs", "flip", "ut")
        pe_at = lambda name: PE_STEPS.index(name) + 1
        dve_at = lambda name: DVE_STEPS.index(name) + 1

        V_ORDER = [("v", h) for h in range(NV)] + [("a", n) for n in range(NT)]
        bank = lambda kind, n: V_ORDER.index((kind, n))
        fill = []
        for h in range(NV + 1):
            fill += [("turn", h, k) for k in range(NK)] if h < NV else []
            fill += [("v", h - 1, k) for k in range(NK)] if h else []
        fill += [("a", n, k) for n in range(NT) for k in range(NK)]

        with nc.Block() as block:
            @block.sync
            def _(sp):
                sp.dma_start(pp[:, 0:FULL], p_in[0:FULL * P].rearrange("(k p) n -> p k n", p=P)).then_inc(pp_in, 16)
                sp.dma_start(pp[0:REM, FULL], p_in[FULL * P:C]).then_inc(pp_in, 16)
                for j in range(RING):
                    sp.dma_start(wf[:, j], blocks[j][0]).then_inc(wf_in[j], 16)
                for j, (_, dst) in enumerate(blocks):
                    sp.wait_ge(w_lo, j + 1)
                    sp.dma_start(dst, raw(ws[:, j % RING])).then_inc(ws_out[j % RING], 16)
                    if j + RING < len(blocks):
                        sp.dma_start(wf[:, j % RING], blocks[j + RING][0]).then_inc(wf_in[j % RING], 16)
                sp.wait_ge(bias_gated, 2)
                sp.wait_ge(v_done, NV + NT)
                sp.dma_start(ada, av[:]).then_inc(out_done, 16)
                per = gates.shape[0] // B
                for i in range(per):
                    sp.dma_start(gates.rearrange("(b i) c -> b i c", i=per)[:, i],
                                 av[:, GATE_MLP * C:(GATE_MLP + 1) * C]).then_inc(out_done, 16)
                sp.wait_ge(mt_ready, 1)
                sp.dma_start(mod.rearrange("b p n -> p b n"), mt[:]).then_inc(out_done, 16)
                sp.wait_ge(us_lo, 3)
                sp.dma_start(u_s, raw(us[:])).then_inc(out_done, 16)
                for b in range(B):
                    sp.wait_ge(ro_lo, 2 * (b + 1))
                    sp.dma_start(rot_s[b].rearrange("s r c -> r s c"), raw(ro[:, b % 2])).then_inc(ro_out[b % 2], 16)
                sp.wait_ge(out_done, 16 * (3 + per))
                for i in range(2):
                    sp.wait_ge(ro_out[i], 16 * B // 2)
                for j in range(RING):
                    sp.wait_ge(ws_out[j], 16 * len(range(j, len(blocks), RING)))

            @block.gpsimd
            def _(pool):
                make_identity(nc, pool, ident, zeroed, ident_made)
                pool.wait_ge(ident_made, 1)
                pool.memset(neg[:], -1.0).then_inc(masks, 1)
                pool.memset(sq[:], 1.0).then_inc(masks, 1)
                pool.wait_ge(masks, 2)
                pool.affine_select(out=neg[:], in_=neg[:], compare_op=ALU.is_ge, fill=0.0, base=-1,
                                   pattern=[[-1, R]], channel_multiplier=1).then_inc(masks, 1)
                pool.affine_select(out=sq[:], in_=sq[:], compare_op=ALU.is_ge, fill=0.0, base=-1,
                                   pattern=[[1, R]], channel_multiplier=-1).then_inc(masks, 1)
                pool.memset(up[:], 0.0).then_inc(masks, 1)

                def low(j):
                    pool.wait_ge(w_hi, j + 1)
                    pool.tensor_tensor(ws[:, j % RING, 1], wf[:, j % RING], raw(ws[:, j % RING, 0]), ALU.subtract) \
                        .then_inc(w_lo, 1)

                early = NV + NT
                for j in range(early):
                    low(j)
                pool.wait_ge(v_done, NV + NT)
                pool.wait_ge(b_in, 32)
                for i, g in enumerate((GATE_MSA, GATE_MLP)):
                    pool.tensor_tensor(av[:, (SEC + i) * C:(SEC + i + 1) * C], av[:, g * C:(g + 1) * C], bb[:, i],
                                       ALU.mult).then_inc(bias_gated, 1)
                for i, s in enumerate(MOD):
                    one = 1.0 if s in (SCALE_MSA, SCALE_MLP) else 0.0
                    for a, z, o in ((0, C, 0), (FULL * P, C, C)):
                        pool.tensor_scalar(am[:, i, o:o + z - a], av[:, s * C + a:s * C + z], one, None, ALU.add) \
                            .then_inc(am_ready, 1)
                for j in range(early, len(blocks)):
                    low(j)

            @block.scalar
            def _(act):
                def load_wr(h):
                    act.dma_start(wr[:, h % 2], w_skew[h * VT:(h + 1) * VT].rearrange("(t p) c -> p t c", p=TR)) \
                       .then_inc(wr_in[h % 2], 16)

                def load_wa(n):
                    cols = slice(n * WT, (n + 1) * WT)
                    s = n % A_RING
                    act.dma_start(wa[:, s, 0:FULL], w_ada[0:FULL * P, cols].rearrange("(k p) n -> p k n", p=P)) \
                       .then_inc(wa_in[s], 16)
                    act.dma_start(wa[0:REM, s, FULL], w_ada[FULL * P:C, cols]).then_inc(wa_in[s], 16)
                    act.dma_start(wa[REM:REM + 1, s, FULL], b_ada[cols].rearrange("(a n) -> a n", a=1)) \
                       .then_inc(wa_in[s], 16)

                def high(j):
                    act.wait_ge(wf_in[j % RING], 16 * (j // RING + 1))
                    act.wait_ge(ws_out[j % RING], 16 * (j // RING))
                    act.activation(ws[:, j % RING, 0], wf[:, j % RING], ACT.Copy).then_inc(w_hi, 1)

                row = lambda x: x.rearrange("(a n) -> a n", a=1)
                act.dma_start(cs[:, 0], cond).then_inc(c_in, 16)
                for h in range(2):
                    load_wr(h)
                act.dma_start(wl[REM:REM + 1], row(b_skew)).then_inc(wl_in, 16)
                for n in range(A_RING):
                    load_wa(n)
                act.dma_start(bb[:, 0], row(b_proj).broadcast_to([B, C])).then_inc(b_in, 16)
                act.dma_start(bb[:, 1], row(b_fc2).broadcast_to([B, C])).then_inc(b_in, 16)
                act.wait_ge(c_in, 16)
                act.activation(cs[:, 1], cs[:, 0], ACT.Silu).then_inc(silu_done, 1)
                turned, block_no = 0, 0
                for kind, n, k in fill:
                    if kind == "turn":
                        act.wait_ge(w_turned, turned + 1)
                        if n >= 2:
                            act.wait_ge(v_ready, n - 1)
                        dst = wt[:, n % 2, k] if k < FULL else wl[0:REM, n * VT:(n + 1) * VT]
                        act.activation(dst, p_w[0:rows(k), turned % 2, 0:VT], ACT.Copy).then_inc(wt_ready, 1)
                        turned += 1
                        if k == NK - 1 and n + 2 < NV:
                            load_wr(n + 2)
                    elif k == NK - 1:
                        i = bank(kind, n)
                        act.wait_ge(v_ready, i + 1)
                        dst, w = (v[:, n * VT:(n + 1) * VT], VT) if kind == "v" else (av[:, n * WT:(n + 1) * WT], WT)
                        act.activation(dst, p_v[0:B, i % 2, 0:w], ACT.Copy).then_inc(v_done, 1)
                        if kind == "a" and n + A_RING < NT:
                            load_wa(n + A_RING)
                        if kind == "a":
                            if n == 0:
                                act.wait_ge(masks, 5)
                                act.wait_ge(v_done, NV)
                            for r in range(n * R // NT, min((n + 1) * R // NT, R - 1)):
                                off = r * (R - 1) - r * (r - 1) // 2
                                act.dma_start(up[r:r + 1, :, r + 1:R], v[:, off:off + R - 1 - r],
                                              allow_slow_non_contiguous=True).then_inc(up_in, 16)
                        high(block_no)
                        block_no += 1
                act.wait_ge(dve_done, dve_at("diag_sum"))
                act.activation(col[:, 1:2], col[:, 0:1], ACT.Sqrt).then_inc(act_done, 1)
                for j in range(block_no, len(blocks) - 2):
                    high(j)
                act.wait_ge(m_turned, 1)
                act.activation(mt[:].rearrange("p b n -> p n b"), p_m, ACT.Copy).then_inc(mt_ready, 1)
                for j in range(len(blocks) - 2, len(blocks)):
                    high(j)
                act.wait_ge(pe_done, pe_at("u_turned"))
                act.wait_ge(us_lo, 1)
                act.activation(us[:, 0:FULL, 0:R], p_q[:, 0:FULL], ACT.Copy).then_inc(us_hi, 1)
                act.activation(us[0:REM, FULL, 0:R], p_q[0:REM, FULL], ACT.Copy).then_inc(us_hi, 1)
                for b in range(B):
                    if b >= 2:
                        act.wait_ge(ro_out[b % 2], 16 * (b // 2))
                    for h, (a, z) in enumerate(halves):
                        act.wait_ge(ro_ready, 2 * b + h + 1)
                        act.activation(ro[:, b % 2, 0, a:z], p_w[0:R, h, 0:HALF], ACT.Copy).then_inc(ro_hi, 1)

            @block.vector
            def _(dve):
                at = [0]

                def step(ins, name):
                    assert DVE_STEPS[at[0]] == name
                    at[0] += 1
                    ins.then_inc(dve_done, 1)
                    dve.wait_ge(dve_done, at[0])

                dve.memset(raw(us[:]), 0.0).then_inc(us_lo, 1)
                dve.memset(sct[:, FULL], 1.0).then_inc(set_up, 1)
                dve.wait_ge(ident_made, 1)
                dve.tensor_copy(sel[:], ident[0:R, 0:R].rearrange("p (j o) -> p j o", o=1).broadcast_to([R, R, R])) \
                   .then_inc(set_up, 1)
                dve.tensor_copy(m[:, R:2 * R], ident[0:R, 0:R]).then_inc(set_up, 1)
                dve.wait_ge(set_up, 3)
                dve.wait_ge(c_turned, 1)
                dve.tensor_copy(sct[:, 0:FULL], p_c[:, 0:FULL]).then_inc(sct_ready, 1)
                dve.tensor_copy(sct[0:REM, FULL], p_c[0:REM, FULL]).then_inc(sct_ready, 1)
                dve.wait_ge(masks, 5)
                dve.scalar_tensor_tensor(upm[:], ident[0:R, 0:R], 0.5, sq[:], ALU.mult, ALU.add).then_inc(set_up, 1)
                dve.wait_ge(set_up, 4)
                dve.wait_ge(pe_done, pe_at("gram"))
                step(dve.tensor_copy(m[:, 0:R], p_g[0:R, 0:R]), "m_ready")
                dve.wait_ge(pe_done, pe_at("p_turned"))
                dve.tensor_copy(pt[:, 0:512], p_w[0:R, 0]).then_inc(set_up, 1)
                step(dve.tensor_copy(pt[:, 512:C], p_w[0:R, 1, 0:C - 512]), "pt")

                for j in range(R):
                    dve.wait_ge(row_spread, j + 1)
                    dve.reciprocal(col[:, 4:5], p_b[:, j:j + 1]).then_inc(step_done, 1)
                    dve.wait_ge(step_done, 3 * j + 1)
                    dve.scalar_tensor_tensor(col[:, 5:6], m[:, j:j + 1], col[:, 4:5], neg[:, j:j + 1],
                                             ALU.mult, ALU.mult).then_inc(step_done, 1)
                    dve.wait_ge(step_done, 3 * j + 2)
                    dve.scalar_tensor_tensor(m[:, j + 1:R + j + 1], p_b[:, j + 1:R + j + 1], col[:, 5:6],
                                             m[:, j + 1:R + j + 1], ALU.mult, ALU.add).then_inc(step_done, 1)
                    dve.wait_ge(step_done, 3 * j + 3)
                step(dve.tensor_tensor(sq[:], m[:, 0:R], ident[0:R, 0:R], ALU.mult), "diag")
                step(dve.tensor_reduce(col[:, 0:1], sq[:], AX.X, ALU.add), "diag_sum")
                dve.wait_ge(act_done, 1)
                step(dve.reciprocal(col[:, 2:3], col[:, 1:2]), "inv_std")
                step(dve.tensor_scalar(sq[:], m[:, R:2 * R], col[:, 2:3], None, ALU.mult), "scaled")
                dve.wait_ge(pe_done, pe_at("l_turned"))
                step(dve.tensor_copy(lst[:], p_g[0:R, 0:R]), "lst")
                dve.wait_ge(pe_done, pe_at("q_ready"))
                dve.tensor_copy(qt[:, 0:HALF], p_w[0:R, 0, 0:HALF]).then_inc(set_up, 1)
                step(dve.tensor_copy(qt[:, HALF:C], p_w[0:R, 1, 0:HALF]), "qt")
                dve.wait_ge(pe_done, pe_at("q_turned"))
                dve.tensor_copy(q[:, 0:FULL], p_q[:, 0:FULL]).then_inc(set_up, 1)
                step(dve.tensor_copy(q[0:REM, FULL], p_q[0:REM, FULL]), "q")
                dve.wait_ge(pe_done, pe_at("gram2"))
                step(dve.tensor_tensor(phi[:], p_g[0:R, 0:R], ident[0:R, 0:R], ALU.subtract), "phi0")
                step(dve.tensor_tensor(phi[:], phi[:], upm[:], ALU.mult), "phi")
                dve.wait_ge(pe_done, pe_at("fix"))
                dve.tensor_tensor(qt[:, 0:HALF], qt[:, 0:HALF], p_w[0:R, 0, 0:HALF], ALU.subtract).then_inc(set_up, 1)
                step(dve.tensor_tensor(qt[:, HALF:C], qt[:, HALF:C], p_w[0:R, 1, 0:HALF], ALU.subtract), "qt2")
                dve.wait_ge(set_up, 8)
                dve.wait_ge(pe_done, pe_at("top"))
                step(dve.tensor_copy(m[:, 0:R], p_g[0:R, 0:R]), "m2_ready")

                dve.wait_ge(pe_done, pe_at("a_turned"))
                step(dve.tensor_tensor(a2[:], up[:], p_s[:, :, 0, 0:R], ALU.subtract), "a2")
                scale = 2.0 ** -SQUARINGS
                dve.tensor_scalar(sa[:, :, 1], a2[:], -scale, None, ALU.mult).then_inc(set_up, 1)
                step(dve.tensor_scalar(sa[:, :, 0], a2[:], scale, None, ALU.mult), "sa")
                dve.wait_ge(set_up, 9)
                step(dve.tensor_scalar(ex[:], sa[:], 1.0 / TERMS, None, ALU.mult), "y0")
                for i in range(1, TERMS):
                    dve.wait_ge(pe_done, pe_at(f"taylor{i}"))
                    step(dve.tensor_tensor(ts[:], p_s[:, :, :, 0:R], sa[:], ALU.add), f"sum{i}")
                    step(dve.tensor_scalar(ex[:], ts[:], 1.0 / (TERMS - i), None, ALU.mult), f"y{i}")

                for j in range(R):
                    dve.wait_ge(row2_spread, j + 1)
                    dve.tensor_scalar(zs[:, j:j + 1], p_b[:, j:j + 1], 0.0, 2.0, ALU.is_ge, ALU.mult) \
                       .then_inc(step2_done, 1)
                    dve.wait_ge(step2_done, 5 * j + 1)
                    dve.scalar_tensor_tensor(col[:, 6:7], zs[:, j:j + 1], -1.0, p_b[:, j:j + 1], ALU.add, ALU.add) \
                       .then_inc(step2_done, 1)
                    dve.wait_ge(step2_done, 5 * j + 2)
                    dve.reciprocal(col[:, 4:5], col[:, 6:7]).then_inc(step2_done, 1)
                    dve.wait_ge(step2_done, 5 * j + 3)
                    dve.scalar_tensor_tensor(col[:, 5:6], m[:, j:j + 1], col[:, 4:5], neg[:, j:j + 1],
                                             ALU.mult, ALU.mult).then_inc(step2_done, 1)
                    dve.wait_ge(step2_done, 5 * j + 4)
                    dve.scalar_tensor_tensor(m[:, 0:R], p_b[:, 0:R], col[:, 5:6], m[:, 0:R], ALU.mult, ALU.add) \
                       .then_inc(step2_done, 1)
                    if j % PER == PER - 1:
                        i = j // PER
                        dve.wait_ge(sq_ready, i + 1)
                        if i:
                            dve.wait_ge(ex_ready, 2 * i)
                        for s in range(2):
                            dve.scalar_tensor_tensor(ex[:, :, s], ex[:, :, s], 2.0, p_s[:, :, s, s * R:(s + 1) * R],
                                                     ALU.mult, ALU.add).then_inc(ex_ready, 1)
                    dve.wait_ge(step2_done, 5 * j + 5)
                step(dve.tensor_tensor(sq[:], zs[:], ident[0:R, 0:R], ALU.mult), "sign_diag")
                step(dve.tensor_reduce(col[:, 3:4], sq[:], AX.X, ALU.add), "signs")
                step(dve.tensor_scalar(col[:, 7:8], col[:, 3:4], -1.0, 1.0, ALU.mult, ALU.add), "flip")
                step(dve.tensor_scalar(ut[:], qt[:], col[:, 7:8], None, ALU.mult), "ut")
                dve.wait_ge(us_hi, 2)
                dve.tensor_tensor(us[:, 0:FULL, R:2 * R], p_q[:, 0:FULL], raw(us[:, 0:FULL, 0:R]), ALU.subtract) \
                   .then_inc(us_lo, 1)
                dve.tensor_tensor(us[0:REM, FULL, R:2 * R], p_q[0:REM, FULL], raw(us[0:REM, FULL, 0:R]),
                                  ALU.subtract).then_inc(us_lo, 1)
                for b in range(B):
                    for h, (a, z) in enumerate(halves):
                        dve.wait_ge(ro_hi, 2 * b + h + 1)
                        dve.tensor_tensor(ro[:, b % 2, 1, a:z], p_w[0:R, h, 0:HALF], raw(ro[:, b % 2, 0, a:z]),
                                          ALU.subtract).then_inc(ro_lo, 1)

            @block.tensor
            def _(pe):
                at = [0]

                def step(ins, name):
                    assert PE_STEPS[at[0]] == name
                    at[0] += 1
                    ins.then_inc(pe_done, 1)

                def gram(x, name):
                    for k in range(NK):
                        i = pe.matmul(p_g[0:R, 0:R], x[0:rows(k), k], x[0:rows(k), k], start=(k == 0),
                                      stop=(k == NK - 1))
                    step(i, name)

                def turn_rows(x, name):
                    for k in range(NK):
                        i = pe.transpose(p_q[0:rows(k), k], x[:, k * P:k * P + rows(k)], ident[0:R, 0:R])
                    step(i, name)

                turned = [0]

                def filling(kind, n, k):
                    if kind == "turn":
                        if k == 0:
                            pe.wait_ge(wr_in[n % 2], 16 * (n // 2 + 1))
                        if turned[0] >= 2:
                            pe.wait_ge(wt_ready, turned[0] - 1)
                        for t in range(TQ):
                            i = pe.transpose(p_w[0:rows(k), turned[0] % 2, t * TR:(t + 1) * TR],
                                             wr[:, n % 2, t, k * P:k * P + rows(k)], ident[0:TR, 0:TR])
                        i.then_inc(w_turned, 1)
                        turned[0] += 1
                        return
                    i = bank(kind, n)
                    if k == 0:
                        if kind == "v":
                            pe.wait_ge(wt_ready, NK * (n + 1))
                            pe.wait_ge(wl_in, 16)
                        else:
                            pe.wait_ge(wa_in[n % A_RING], 48 * (n // A_RING + 1))
                        if i >= 2:
                            pe.wait_ge(v_done, i - 1)
                    r = P if k < FULL else REM + 1
                    if kind == "a":
                        w, rhs = WT, wa[0:r, n % A_RING, k]
                    else:
                        w, rhs = VT, wt[:, n % 2, k] if k < FULL else wl[:, n * VT:(n + 1) * VT]
                    x = pe.matmul(p_v[0:B, i % 2, 0:w], sct[0:r, k], rhs, start=(k == 0), stop=(k == NK - 1))
                    if k == NK - 1:
                        x.then_inc(v_ready, 1)

                pe.wait_ge(ident_made, 1)
                pe.wait_ge(pp_in, 32)
                gram(pp, "gram")
                for k in range(NK):
                    i = pe.transpose(p_w[0:R, k // 4, k % 4 * P:k % 4 * P + rows(k)], pp[0:rows(k), k],
                                     ident[0:rows(k), 0:rows(k)])
                step(i, "p_turned")
                pe.wait_ge(silu_done, 1)
                for k in range(NK):
                    i = pe.transpose(p_c[0:rows(k), k], cs[:, 1, k * P:k * P + rows(k)], ident[0:B, 0:B])
                i.then_inc(c_turned, 1)
                pe.wait_ge(dve_done, dve_at("pt"))
                pe.wait_ge(sct_ready, 2)
                pe.wait_ge(set_up, 4)
                for j in range(R):
                    if j:
                        pe.wait_ge(step_done, 3 * j)
                    pe.matmul(p_b[:, 0:2 * R], sel[:, j], m[:], start=True, stop=True).then_inc(row_spread, 1)
                    for f in fill[j * len(fill) // R:(j + 1) * len(fill) // R]:
                        filling(*f)
                pe.wait_ge(dve_done, dve_at("scaled"))
                step(pe.transpose(p_g[0:R, 0:R], sq[:], ident[0:R, 0:R]), "l_turned")
                pe.wait_ge(dve_done, dve_at("lst"))
                for h, (a, z) in enumerate(halves):
                    i = pe.matmul(p_w[0:R, h, 0:HALF], lst[:], pt[:, a:z], start=True, stop=True)
                step(i, "q_ready")
                pe.wait_ge(dve_done, dve_at("qt"))
                turn_rows(qt, "q_turned")
                pe.wait_ge(dve_done, dve_at("q"))
                gram(q, "gram2")
                pe.wait_ge(dve_done, dve_at("phi"))
                for h, (a, z) in enumerate(halves):
                    i = pe.matmul(p_w[0:R, h, 0:HALF], phi[:], qt[:, a:z], start=True, stop=True)
                step(i, "fix")
                pe.wait_ge(dve_done, dve_at("qt2"))
                step(pe.transpose(p_g[0:R, 0:R], qt[:, 0:R], ident[0:R, 0:R]), "top")

                pe.wait_ge(up_in, 16 * (R - 1))
                for b in range(B):
                    i = pe.transpose(p_s[:, b, 0, 0:R], up[:, b], ident[0:R, 0:R])
                step(i, "a_turned")
                for t in range(1, TERMS):
                    pe.wait_ge(dve_done, dve_at("y0" if t == 1 else f"y{t - 1}"))
                    for b in range(B):
                        for s in range(2):
                            i = pe.matmul(p_s[:, b, s, 0:R], sa[:, b, 1 - s], ex[:, b, s], start=True, stop=True)
                    step(i, f"taylor{t}")
                pe.wait_ge(dve_done, dve_at(f"y{TERMS - 1}"))
                for j in range(R):
                    if j:
                        pe.wait_ge(step2_done, 5 * j)
                    pe.matmul(p_b[:, 0:2 * R], sel[:, j], m[:], start=True, stop=True).then_inc(row2_spread, 1)
                    if j % PER == 0 and j:
                        pe.wait_ge(ex_ready, 2 * (j // PER))
                    for b in range(j % PER * B // PER, (j % PER + 1) * B // PER):
                        for s in range(2):
                            i = pe.matmul(p_s[:, b, s], ex[:, b, 1 - s], ex[:, b].rearrange("p s n -> p (s n)"),
                                          start=True, stop=True)
                    if j % PER == PER - 1:
                        i.then_inc(sq_ready, 1)
                    if j == R // 2:
                        pe.wait_ge(am_ready, 2 * len(MOD))
                        for i in range(len(MOD)):
                            for k in range(NK):
                                t = pe.transpose(p_m[:, i * NK + k], am[:, i, k * P:(k + 1) * P], ident[0:B, 0:B])
                        t.then_inc(m_turned, 1)
                pe.wait_ge(dve_done, dve_at("ut"))
                turn_rows(ut, "u_turned")
                pe.wait_ge(ex_ready, 2 * SQUARINGS)
                for b in range(B):
                    for h, (a, z) in enumerate(halves):
                        if b:
                            pe.wait_ge(ro_lo, 2 * (b - 1) + h + 1)
                        pe.matmul(p_w[0:R, h, 0:HALF], ex[:, b, 1], ut[:, a:z], start=True, stop=True) \
                          .then_inc(ro_ready, 1)


def build(nc, x, cond, w_qkv, b_qkv, w_proj, b_proj, w_fc1, b_fc1, w_fc2, b_fc2, w_ada, b_ada, p_in, w_skew, b_skew,
          out):
    scratch = lambda name, *shape: nc.dram_tensor(name, shape, F32, kind="Internal").ap()
    wqkv_s = scratch("wqkv_s", 2, C, 3 * C)
    wproj_s = scratch("wproj_s", 2, C, C)
    w1_s = scratch("w1_s", 2, C, FF)
    w2_s = scratch("w2_s", 2, FF, C)
    ada = scratch("ada", B, 8 * C)
    mod = scratch("mod", B, P, len(MOD) * (FULL + 1))
    gates = scratch("gates", B * L // GT, C)
    u_s = scratch("u_s", P, FULL + 1, 2 * R)
    rot_s = scratch("rot_s", B, 2, R, C)
    q_s = scratch("q_s", 2, NHEAD * D, L)
    k_s = scratch("k_s", 2, NHEAD * D, L)
    v_s = scratch("v_s", 2, NHEAD, L, D)
    o_t = scratch("o_t", NHEAD * D, L)
    sums = scratch("sums", NHEAD, L)
    rsums = scratch("rsums", NHEAD, L)
    x2_s = scratch("x2_s", B * L, C)
    h2_s = scratch("h2_s", B * L // GT, P, A_TILES, GT)
    x3_s = scratch("x3_s", B * L, C)
    x_rows = x.rearrange("b t c -> (b t) c")
    out_rows = out.rearrange("b t c -> (b t) c")
    weights = [(w_qkv, wqkv_s), (w_proj, wproj_s), (w_fc1, w1_s), (w_fc2, w2_s)]

    stage_prepare(nc, cond, w_ada, b_ada, b_proj, b_fc2, weights, p_in, w_skew, b_skew, ada, mod, gates, u_s, rot_s)
    stage_qkv(nc, x_rows, b_qkv, wqkv_s, mod, q_s, k_s, v_s)
    stage_attention(nc, q_s, k_s, v_s, o_t, sums)
    stage_proj(nc, o_t, sums, rsums, x_rows, wproj_s, ada, mod, x2_s, h2_s)
    stage_mlp(nc, h2_s, x2_s, w1_s, b_fc1, w2_s, gates, x3_s)
    stage_rotate(nc, x3_s, u_s, rot_s, out_rows)


_INS = ("x", "cond_1152", "L0_cond_W_qkv", "L0_cond_b_qkv", "L0_cond_W_proj", "L0_cond_b_proj", "L0_cond_W_fc1",
        "L0_cond_b_fc1", "L0_cond_W_fc2", "L0_cond_b_fc2", "L0_cond_W_ada", "L0_cond_b_ada", "L1_cond_P",
        "L1_cond_W", "L1_cond_b")
_OUTS = [((B, L, C), "float32")]


def kernel(**inputs):
    import numpy as _np
    import concourse.bacc as _bacc
    from concourse import mybir as _mybir
    from concourse.bass_utils import run_bass_kernel_spmd as _run

    nc = _bacc.Bacc("TRN2", target_bir_lowering=False, num_devices=1)
    arrays, args = {}, []
    for name in _INS:
        a = _np.ascontiguousarray(inputs[name])
        arrays[f"in_{name}_dram"] = a
        args.append(nc.dram_tensor(f"in_{name}_dram", a.shape, _mybir.dt.from_np(a.dtype), kind="ExternalInput").ap())
    for i, (shape, dtype) in enumerate(_OUTS):
        dt = _mybir.dt.from_np(_np.dtype(dtype))
        args.append(nc.dram_tensor(f"out_{i}_dram", shape, dt, kind="ExternalOutput").ap())
    build(nc, *args)
    r = _run(nc, [arrays], core_ids=[0])
    return r.results[0]["out_0_dram"]
```

```python
from contextlib import ExitStack

import concourse.bass as bass
from concourse import mybir

F32 = mybir.dt.float32
F32R = mybir.dt.float32r
ALU = mybir.AluOpType
ACT = mybir.ActivationFunctionType
AX = mybir.AxisListType

P = 128
B, L, C = 4, 1024, 576
H = 16
D = C // H
NHEAD = B * H
FF = 4 * C
R = 64
NSKEW = R * (R - 1) // 2
SEC = 6
LN_EPS = 1e-6
FULL = C // P
REM = C - FULL * P
CPAD = (FULL + 1) * P
GT = 512
SUB = GT // P
HALF = C // 2
START = 1
SQUARINGS = 16
SHIFT_MSA, SCALE_MSA, GATE_MSA, SHIFT_MLP, SCALE_MLP, GATE_MLP, GB_PROJ, GB_FC2 = range(8)
MOD = (SHIFT_MSA, SCALE_MSA, SHIFT_MLP, SCALE_MLP)

A_TILES = 2 * (FULL + 1)
W_TILES = 2 * FULL + 1
PASSES = [p for k in range(FULL) for p in ((k, k), (FULL + 1 + k, k), (k, FULL + k))]
PASSES += [(FULL, 2 * FULL), (2 * FULL + 1, 2 * FULL)]


def raw(ap):
    return ap.bitcast(F32)


def load_split_weight(eng, dst, src, cols, sem):
    for s in range(2):
        eng.dma_start(raw(dst[:, s * FULL:(s + 1) * FULL, :]),
                      src[s, 0:FULL * P, cols].rearrange("(k p) n -> p k n", p=P)).then_inc(sem, 16)
        eng.dma_start(raw(dst[s * REM:(s + 1) * REM, 2 * FULL, :]), src[s, FULL * P:C, cols]).then_inc(sem, 16)


def wait_alone(eng, sem, value, passed):
    eng.wait_ge(sem, value)
    eng.sem_inc(passed, 1)


def stage_semaphores(nc, ctx, prefix, reused=False):
    made = []

    def sem(name):
        made.append(ctx.enter_context(nc.semaphore(prefix + name)))
        return made[-1]

    def zero():
        nums = sorted(s.num for s in made)
        starts = [n for n in nums if n - 1 not in nums]
        ends = [n for n in nums if n + 1 not in nums]
        for a, z in zip(starts, ends):
            nc.gpsimd.sem_clear(range(a, z + 1))
        nc.all_engine_barrier()

    if reused:
        ctx.callback(zero)
    return sem


def set_start(eng, sems):
    for s in sems:
        eng.sem_inc(s, START)


def c_slot(half, c):
    return (half * (FULL + 1) + c) % 2


def flat_split(src, dst):
    return (src.rearrange("r n -> (r n)").rearrange("(p m) -> p m", p=P),
            dst.rearrange("s r n -> s (r n)").rearrange("s (p m) -> p s m", p=P))


def chain_state(nc, ctx):
    sb = lambda n, s: ctx.enter_context(nc.sbuf_tensor("x_" + n, s, F32))
    return {"m": sb("m", [R, 2 * R]),
            "row": sb("row", [R, 2 * R]),
            "qt": sb("qt", [R, C]),
            "neg": sb("neg", [R, R]),
            "ex": sb("ex", [R, B, 2, R])}


def make_identity(nc, pool, ident, zeroed, made):
    pool.memset(ident[:], 0.0).then_inc(zeroed, 1)
    pool.wait_ge(zeroed, 1)
    pool.affine_select(out=ident[:], in_=ident[:], compare_op=ALU.not_equal, fill=1.0, base=0,
                       pattern=[[-1, P]], channel_multiplier=1).then_inc(made, 1)


def stage_qkv(nc, x, b_qkv, wqkv, mod, q_s, k_s, v_s, weights, state, u_s, rot_s):
    QKM = 2 * C // P
    QR, VR = 3, 2
    CHAIN_TILES = (5, 6, 7, 8)
    BLK = sum(src.shape[0] * src.shape[1] for src, _ in weights) // P // (QKM * 2 * B)
    flat = [flat_split(src, dst) for src, dst in weights]
    shares = [s.shape[1] // (2 * B * BLK) for s, _ in flat]
    plan = [(s, d, share, i) for (s, d), share in zip(flat, shares) for i in range(share)]
    assert len(plan) == QKM and all(s.shape[1] == share * 2 * B * BLK for s, _, share, _ in plan)
    with ExitStack() as ctx:
        sb = lambda n, s, d=F32: ctx.enter_context(nc.sbuf_tensor("q_" + n, s, d))
        ps = lambda n, s: ctx.enter_context(nc.psum_tensor("q_psum_" + n, s, F32))
        sem = stage_semaphores(nc, ctx, "q_", reused=True)
        passed = sem("passed")
        w = sb("w", [P, W_TILES, 3 * C], F32R)
        bqk = sb("bqk", [P, QKM])
        bv = sb("bv", [P, C])
        ident = sb("ident", [P, P])
        xt = sb("xt", [P, 2, SUB, C])
        xn = sb("xn", [P, 2, SUB, CPAD])
        md = sb("md", [P, 2, len(MOD) * (FULL + 1)])
        stats = sb("stats", [P, SUB, 2, 6])
        mv = sb("mv", [P, 2, SUB, 2])
        small = sb("small", [P, 6, SUB])
        rstd = sb("rstd", [P, 2, SUB])
        shift = sb("shift", [P, 2, SUB])
        ht = sb("ht", [P, 2, A_TILES, GT], F32R)
        hf = sb("hf", [P, FULL + 1, GT])
        qko = sb("qko", [P, QR, 2, GT], F32R)
        vf = sb("vf", [P, VR, C])
        vo = sb("vo", [P, VR, 2, C], F32R)
        pt = ps("pt", [P, 2, GT])
        pqk = ps("pqk", [P, 3, 512])
        pv = ps("pv", [P, 2, 512])
        wf = sb("wf", [P, 2, BLK])
        ws = sb("ws", [P, 2, 2, BLK], F32R)
        m, row, qt, neg, ex = (state[x] for x in ("m", "row", "qt", "neg", "ex"))
        ones = sb("ones", [R, R])
        zs = sb("zs", [R, R])
        sq = sb("sq", [R, R])
        col = sb("col", [R, 8])
        ut = sb("ut", [R, C])
        us = sb("us", [P, FULL + 1, 2 * R], F32R)
        ro = sb("ro", [R, 2, 2, C], F32R)
        p_x = ps("x", [R, 512])
        p_ee = p_x[:, 2 * R:2 * R + 6 * R].rearrange("p (s n) -> p s n", s=2)[:, :, 0:R]
        p_u = pt[:, 0, 0:(FULL + 1) * R].rearrange("p (k n) -> p k n", n=R)
        halves = ((0, HALF), (HALF, C))
        rows = lambda k: P if k < FULL else REM
        XL = 7
        PER = R // (2 * B)
        wf_in = [sem(f"wf_in{i}") for i in range(2)]
        ws_out = [sem(f"ws_out{i}") for i in range(2)]
        w_hi, w_lo = sem("w_hi"), sem("w_lo")
        x_ready, x_link, ones_made = sem("x_ready"), sem("x_link"), sem("ones_made")
        tail, u_turned, us_hi, us_lo = sem("tail"), sem("u_turned"), sem("us_hi"), sem("us_lo")
        ro_ready, ro_hi, ro_lo = sem("ro_ready"), sem("ro_hi"), sem("ro_lo")
        ro_out, u_out = [sem(f"ro_out{i}") for i in range(2)], sem("u_out")

        w_in, zeroed, ident_made = sem("w_in"), sem("zeroed"), sem("ident_made")
        x_in = [sem(f"x_in{i}") for i in range(2)]
        md_in = [sem(f"md_in{i}") for i in range(2)]
        dve_link, var_ready, std_ready, rstd_ready, xn_ready = (
            sem("dve_link"), sem("var_ready"), sem("std_ready"), sem("rstd_ready"), sem("xn_ready"))
        t_ready, hi_ready, full_ready, lo_ready = (
            sem("t_ready"), sem("hi_ready"), sem("full_ready"), sem("lo_ready"))
        qk_ready, qk_hi = sem("qk_ready"), sem("qk_hi")
        qk_lo = [sem(f"qk_lo{i}") for i in range(QR)]
        qk_out = [sem(f"qk_out{i}") for i in range(QR)]
        v_ready, v_hi = sem("v_ready"), sem("v_hi")
        v_full = [sem(f"v_full{i}") for i in range(2)]
        v_lo = [sem(f"v_lo{i}") for i in range(VR)]
        v_out = [sem(f"v_out{i}") for i in range(VR)]
        NK = FULL + 1

        def groups(eng, body):
            with eng.Fori(0, B - 1) as b:
                body(b, 0, False)
                body(b, 1, False)
            body(B - 1, 0, True)
            body(B - 1, 1, True)

        SPLIT = C // P

        def out_count(slot, g):
            return (QKM // QR + (1 if SPLIT % QR == slot else 0)) * g

        def block_slot(half, m):
            return (QKM * half + m) % 2

        def block_uses(b, half, m):
            return QKM * b + (QKM * half + m) // 2

        with nc.Block() as block:
            @block.sync
            def _(sp):
                def load(b, half):
                    sp.dma_start(xt[:, half], x[bass.ds(b * L + half * GT, GT), :]
                                 .rearrange("(t p) c -> p t c", p=P)).then_inc(x_in[half], 16)
                    sp.dma_start(md[:, half], mod[bass.ds(b, 1)].rearrange("a p n -> (a p) n")) \
                      .then_inc(md_in[half], 16)

                load(0, 0)
                load(0, 1)
                load_split_weight(sp, w, wqkv, slice(0, 3 * C), w_in)
                sp.dma_start(bqk[:], b_qkv[0:2 * C].rearrange("(m p) -> p m", p=P),
                             allow_slow_non_contiguous=True).then_inc(w_in, 16)
                sp.dma_start(bv[:], b_qkv[2 * C:3 * C].rearrange("(a n) -> a n", a=1)
                             .broadcast_to([P, C])).then_inc(w_in, 16)

                def load_block(g, half, m):
                    src, _, share, i = plan[m]
                    sp.dma_start(wf[:, block_slot(half, m)], src[:, bass.ds((share * g + i) * BLK, BLK)]) \
                      .then_inc(wf_in[block_slot(half, m)], 16)

                for m in range(2):
                    load_block(0, 0, m)

                def body(b, half, last):
                    g = 2 * b + half
                    if not last:
                        wait_alone(sp, xn_ready, g + 1, passed)
                        sp.wait_ge(lo_ready, NK * (g + 1))
                        load(b + 1, half)
                    for m in range(QKM):
                        sp.wait_ge(qk_lo[m % QR], START + (QKM // QR) * g + m // QR + 1)
                        for name, r0, r1 in (("q", 0, C), ("k", C, 2 * C)):
                            a, z = max(r0, m * P), min(r1, (m + 1) * P)
                            if a < z:
                                dst = q_s if name == "q" else k_s
                                sp.dma_start(
                                    dst[:, bass.ds(b * C + a - r0, z - a), half * GT:(half + 1) * GT]
                                    .rearrange("s f t -> f s t"),
                                    raw(qko[a - m * P:z - m * P, m % QR])).then_inc(qk_out[m % QR], 16)
                        _, dst, share, i = plan[m]
                        sp.wait_ge(w_lo, QKM * g + m + 1)
                        sp.dma_start(dst[:, :, bass.ds((share * g + i) * BLK, BLK)], raw(ws[:, block_slot(half, m)])) \
                          .then_inc(ws_out[block_slot(half, m)], 16)
                        if m + 2 < QKM:
                            load_block(g, half, m + 2)
                        elif not (last and half == 1):
                            load_block(g + 1, 1 - half, m + 2 - QKM)
                    for t in range(SUB):
                        sp.wait_ge(v_lo[t % VR], START + (SUB // VR) * g + t // VR + 1)
                        for s in range(2):
                            sp.dma_start(
                                v_s[s, bass.ds(b * H, H), half * GT + t * P:half * GT + (t + 1) * P, :]
                                .rearrange("h t d -> t h d"),
                                raw(vo[:, t % VR, s]).rearrange("p (h d) -> p h d", h=H)) \
                              .then_inc(v_out[t % VR], 16)

                groups(nc.sync, body)
                sp.wait_ge(us_lo, 3)
                sp.dma_start(u_s, raw(us[:])).then_inc(u_out, 16)
                for b in range(B):
                    sp.wait_ge(ro_lo, 2 * (b + 1))
                    sp.dma_start(rot_s[b].rearrange("s r c -> r s c"), raw(ro[:, b % 2])).then_inc(ro_out[b % 2], 16)
                sp.wait_ge(u_out, 16)
                for i in range(2):
                    sp.wait_ge(ro_out[i], 16 * B // 2)
                for i in range(2):
                    sp.wait_ge(ws_out[i], START + 16 * QKM * B)
                for m in range(QR):
                    sp.wait_ge(qk_out[m], START + 16 * out_count(m, 2 * B))
                for t in range(VR):
                    sp.wait_ge(v_out[t], START + 32 * (SUB // VR) * 2 * B)

            @block.gpsimd
            def _(pool):
                make_identity(nc, pool, ident, zeroed, ident_made)
                pool.memset(ones[:], 1.0).then_inc(ones_made, 1)

                def normalise(g, half):
                    if not (isinstance(g, int) and g < 2):
                        pool.wait_ge(t_ready, NK * (g - 1))
                    wait_alone(pool, rstd_ready, g + 1, passed)
                    for t in range(SUB):
                        for a, z, o in ((0, C, 0), (FULL * P, C, C)):
                            i = pool.tensor_scalar(xn[:, half, t, o:o + z - a], xt[:, half, t, a:z],
                                                   rstd[:, half, t:t + 1], shift[:, half, t:t + 1],
                                                   ALU.mult, ALU.add)
                    i.then_inc(xn_ready, 1)

                def lows(g, half):
                    for c in range(NK):
                        pool.wait_ge(hi_ready, NK * g + c + 1)
                        pool.wait_ge(full_ready, NK * g + c + 1)
                        pool.tensor_tensor(ht[:, half, NK + c, :], hf[:, c, :], raw(ht[:, half, c, :]), ALU.subtract) \
                            .then_inc(lo_ready, 1)

                normalise(0, 0)
                lows(0, 0)
                normalise(1, 1)

                def body(b, half, last):
                    g = 2 * b + half
                    if not (last and half == 1):
                        lows(g + 1, 1 - half)
                    if not last:
                        normalise(g + 2, half)
                    for t in range(SUB):
                        pool.wait_ge(v_hi, SUB * g + t + 1)
                        pool.tensor_tensor(vo[:, t % VR, 1], vf[:, t % VR], vo[:, t % VR, 0].bitcast(F32),
                                           ALU.subtract).then_inc(v_lo[t % VR], 1)

                groups(nc.gpsimd, body)

            @block.vector
            def _(dve):
                def link(ins, n):
                    ins.then_inc(dve_link, 1)
                    dve.wait_ge(dve_link, n)

                LINKS = 7

                def row_stats(g, b, half, t):
                    if t == 0:
                        dve.wait_ge(x_in[half], 16 * b + 16)
                    for a in range(2):
                        i = dve.bn_stats(stats[:, t, a], xt[:, half, t, a * HALF:(a + 1) * HALF])
                    if t == SUB - 1:
                        link(i, LINKS * g + 1)

                def statistics(g, half):
                    n = LINKS * g
                    if not (isinstance(g, int) and g < 2):
                        wait_alone(dve, xn_ready, g - 1, passed)
                    for t in range(SUB):
                        i = dve.bn_aggr(mv[:, half, t], stats[:, t].rearrange("p a s -> p (a s)"))
                    link(i, n + 2)
                    ve, std, r0, r2, cor = (small[:, k] for k in range(5))
                    dve.tensor_scalar(ve, mv[:, half, :, 1], LN_EPS, None, ALU.add).then_inc(var_ready, 1)
                    dve.wait_ge(std_ready, g + 1)
                    link(dve.reciprocal(r0, std), n + 3)
                    link(dve.tensor_tensor(r2, r0, r0, ALU.mult), n + 4)
                    link(dve.tensor_tensor(r2, r2, ve, ALU.mult), n + 5)
                    link(dve.tensor_scalar(cor, r2, -0.5, 1.5, ALU.mult, ALU.add), n + 6)
                    link(dve.tensor_tensor(rstd[:, half], r0, cor, ALU.mult), n + 7)
                    dve.scalar_tensor_tensor(shift[:, half], mv[:, half, :, 0], -1.0, rstd[:, half],
                                             ALU.mult, ALU.mult).then_inc(rstd_ready, 1)

                def fulls(g, b, half):
                    for c in range(NK):
                        dve.wait_ge(hi_ready, NK * g + c + 1)
                        if c == 0:
                            dve.wait_ge(md_in[half], 16 * b + 16)
                        if not (isinstance(g, int) and g == 0):
                            dve.wait_ge(lo_ready, NK * (g - 1) + c + 1)
                        dve.tensor_scalar(hf[:, c, :], pt[:, c_slot(half, c), :], md[:, half, NK + c:NK + c + 1],
                                          md[:, half, c:c + 1], ALU.mult, ALU.add).then_inc(full_ready, 1)

                def chain_step(g, i):
                    j = PER * g + i
                    c = bass.ds(j, 1)
                    n = XL * j

                    def step(ins, k):
                        ins.then_inc(x_link, 1)
                        dve.wait_ge(x_link, START + n + k)

                    dve.wait_ge(x_ready, j + 1)
                    step(dve.tensor_scalar(zs[:, c], p_x[:, c], 0.0, 2.0, ALU.is_ge, ALU.mult), 1)
                    step(dve.scalar_tensor_tensor(col[:, 6:7], zs[:, c], -1.0, p_x[:, c], ALU.add, ALU.add), 2)
                    step(dve.reciprocal(col[:, 4:5], col[:, 6:7]), 3)
                    step(dve.scalar_tensor_tensor(col[:, 5:6], m[:, c], col[:, 4:5], neg[:, c], ALU.mult,
                                                  ALU.mult), 4)
                    step(dve.scalar_tensor_tensor(m[:, 0:R], p_x[:, 0:R], col[:, 5:6], m[:, 0:R], ALU.mult,
                                                  ALU.add), 5)
                    dve.tensor_scalar(row[:], m[:], ident[0:R, bass.ds(j + 1, 1)], None, ALU.mult) \
                       .then_inc(x_link, 1)
                    dve.scalar_tensor_tensor(ex[:, i % B], ex[:, i % B], 2.0, p_ee, ALU.mult, ALU.add) \
                       .then_inc(x_link, 1)

                dve.memset(raw(us[:]), 0.0).then_inc(us_lo, 1)
                dve.wait_ge(ident_made, 1)
                for t in range(SUB):
                    row_stats(0, 0, 0, t)
                statistics(0, 0)
                fulls(0, 0, 0)
                for t in range(SUB):
                    row_stats(1, 0, 1, t)
                statistics(1, 1)
                dve.wait_ge(w_in, 16 * 6)

                def body(b, half, last):
                    g = 2 * b + half
                    if not (last and half == 1):
                        fulls(g + 1, b + half, 1 - half)
                    for m in range(QKM):
                        dve.wait_ge(qk_hi, QKM * g + m + 1)
                        dve.scalar_tensor_tensor(qko[:, m % QR, 1], pqk[:, m % 3], bqk[:, m:m + 1],
                                                 qko[:, m % QR, 0].bitcast(F32), ALU.add, ALU.subtract) \
                           .then_inc(qk_lo[m % QR], 1)
                        dve.wait_ge(w_hi, QKM * g + m + 1)
                        i = block_slot(half, m)
                        dve.tensor_tensor(ws[:, i, 1], wf[:, i], raw(ws[:, i, 0]), ALU.subtract).then_inc(w_lo, 1)
                        if not last and m < SUB:
                            row_stats(g + 2, b + 1, half, m)
                        if not last and m == SUB:
                            statistics(g + 2, half)
                        if m in CHAIN_TILES:
                            chain_step(g, CHAIN_TILES.index(m))
                    for t in range(SUB):
                        dve.wait_ge(v_lo[t % VR], START + (SUB // VR) * g + t // VR)
                        for a in range(2):
                            dve.wait_ge(v_ready, START + 2 * SUB * g + 2 * t + a + 1)
                            dve.tensor_tensor(vf[:, t % VR, a * HALF:(a + 1) * HALF], pv[:, a, 0:HALF],
                                              bv[:, a * HALF:(a + 1) * HALF], ALU.add) \
                               .then_inc(v_full[a], 1)
                        chain_step(g, len(CHAIN_TILES) + t)

                groups(nc.vector, body)

                def tail_step(ins, k):
                    ins.then_inc(tail, 1)
                    dve.wait_ge(tail, k)

                dve.wait_ge(x_link, START + XL * R)
                tail_step(dve.tensor_tensor(sq[:], zs[:], ident[0:R, 0:R], ALU.mult), 1)
                tail_step(dve.tensor_reduce(col[:, 3:4], sq[:], AX.X, ALU.add), 2)
                tail_step(dve.tensor_scalar(col[:, 7:8], col[:, 3:4], -1.0, 1.0, ALU.mult, ALU.add), 3)
                dve.tensor_scalar(ut[:], qt[:], col[:, 7:8], None, ALU.mult).then_inc(tail, 1)
                dve.wait_ge(us_hi, 2)
                dve.tensor_tensor(us[:, 0:FULL, R:2 * R], p_u[:, 0:FULL], raw(us[:, 0:FULL, 0:R]), ALU.subtract) \
                   .then_inc(us_lo, 1)
                dve.tensor_tensor(us[0:REM, FULL, R:2 * R], p_u[0:REM, FULL], raw(us[0:REM, FULL, 0:R]),
                                  ALU.subtract).then_inc(us_lo, 1)
                for b in range(B):
                    for h, (a, z) in enumerate(halves):
                        dve.wait_ge(ro_hi, 2 * b + h + 1)
                        dve.tensor_tensor(ro[:, b % 2, 1, a:z], pqk[0:R, h, 0:HALF], raw(ro[:, b % 2, 0, a:z]),
                                          ALU.subtract).then_inc(ro_lo, 1)

            @block.scalar
            def _(act):
                set_start(act, [x_link, v_ready] + qk_lo + v_full + v_lo + ws_out + qk_out + v_out)
                def root(g):
                    act.wait_ge(var_ready, g + 1)
                    act.activation(small[:, 1], small[:, 0], ACT.Sqrt).then_inc(std_ready, 1)

                def his(g, b, half):
                    for c in range(NK):
                        act.wait_ge(t_ready, NK * g + c + 1)
                        if c == 0:
                            act.wait_ge(md_in[half], 16 * b + 16)
                            if not (isinstance(g, int) and g < 2):
                                act.wait_ge(v_ready, START + 2 * SUB * (g - 1))
                        act.activation(ht[:, half, c, :], pt[:, c_slot(half, c), :], ACT.Identity,
                                       bias=md[:, half, c:c + 1], scale=md[:, half, NK + c:NK + c + 1]) \
                           .then_inc(hi_ready, 1)

                root(0)
                his(0, 0, 0)
                root(1)
                act.wait_ge(w_in, 16 * 6)

                def body(b, half, last):
                    g = 2 * b + half
                    if not (last and half == 1):
                        his(g + 1, b + half, 1 - half)
                    for m in range(QKM):
                        act.wait_ge(qk_ready, QKM * g + m + 1)
                        act.wait_ge(qk_out[m % QR], START + 16 * (out_count(m % QR, 1) * g + m // QR
                                                          + (1 if SPLIT % QR == m % QR and m > SPLIT else 0)))
                        act.activation(qko[:, m % QR, 0], pqk[:, m % 3], ACT.Identity,
                                       bias=bqk[:, m:m + 1]).then_inc(qk_hi, 1)
                        i, uses = block_slot(half, m), block_uses(b, half, m)
                        act.wait_ge(wf_in[i], 16 * (uses + 1))
                        act.wait_ge(ws_out[i], START + 16 * uses)
                        act.activation(ws[:, i, 0], wf[:, i], ACT.Copy).then_inc(w_hi, 1)
                        if not last and m == SUB:
                            root(g + 2)
                    for t in range(SUB):
                        for a in range(2):
                            act.wait_ge(v_full[a], START + SUB * g + t + 1)
                        act.wait_ge(v_out[t % VR], START + 32 * ((SUB // VR) * g + t // VR))
                        act.activation(vo[:, t % VR, 0], vf[:, t % VR], ACT.Copy).then_inc(v_hi, 1)

                groups(nc.scalar, body)
                act.wait_ge(u_turned, 1)
                act.wait_ge(us_lo, 1)
                act.activation(us[:, 0:FULL, 0:R], p_u[:, 0:FULL], ACT.Copy).then_inc(us_hi, 1)
                act.activation(us[0:REM, FULL, 0:R], p_u[0:REM, FULL], ACT.Copy).then_inc(us_hi, 1)
                for b in range(B):
                    if b >= 2:
                        act.wait_ge(ro_out[b % 2], 16 * (b // 2))
                    for h, (a, z) in enumerate(halves):
                        act.wait_ge(ro_ready, 2 * b + h + 1)
                        act.activation(ro[:, b % 2, 0, a:z], pqk[0:R, h, 0:HALF], ACT.Copy).then_inc(ro_hi, 1)

            @block.tensor
            def _(pe):
                pe.wait_ge(ident_made, 1)

                def transposes(g, half):
                    pe.wait_ge(xn_ready, g + 1)
                    for c in range(NK):
                        if not (isinstance(g, int) and g == 0 and c < 2):
                            pe.wait_ge(hi_ready, NK * g + c - 1)
                            pe.wait_ge(full_ready, NK * g + c - 1)
                        for t in range(SUB):
                            i = pe.transpose(pt[:, c_slot(half, c), t * P:(t + 1) * P],
                                             xn[:, half, t, c * P:(c + 1) * P], ident[:])
                        i.then_inc(t_ready, 1)

                def chain_step(g, i):
                    j = PER * g + i
                    wait_alone(pe, x_link, START + XL * j, passed)
                    pe.matmul(p_x[:, 0:2 * R], ones[:], row[:], start=True, stop=True)
                    for s in range(2):
                        x = pe.matmul(p_x[:, (1 + s) * 2 * R:(2 + s) * 2 * R], ex[:, i % B, 1 - s],
                                      ex[:, i % B].rearrange("p s n -> p (s n)"), start=True, stop=True)
                    x.then_inc(x_ready, 1)

                transposes(0, 0)
                pe.wait_ge(ones_made, 1)
                pe.wait_ge(w_in, 16 * 6)

                def body(b, half, last):
                    g = 2 * b + half
                    if not (last and half == 1):
                        transposes(g + 1, 1 - half)
                    pe.wait_ge(hi_ready, NK * (g + 1))
                    pe.wait_ge(lo_ready, NK * (g + 1))
                    for m in range(QKM):
                        pe.wait_ge(qk_lo[m % QR], START + (QKM // QR) * g + m // QR)
                        for n, (a, k) in enumerate(PASSES):
                            i = pe.matmul(pqk[:, m % 3], w[:, k, m * P:(m + 1) * P], ht[:, half, a, :],
                                          start=(n == 0), stop=(n == len(PASSES) - 1))
                        i.then_inc(qk_ready, 1)
                        if m in CHAIN_TILES:
                            chain_step(g, CHAIN_TILES.index(m))
                    for t in range(SUB):
                        for h in range(2):
                            pe.wait_ge(v_full[h], START + SUB * g + t)
                            for n, (a, k) in enumerate(PASSES):
                                i = pe.matmul(pv[:, h, 0:HALF], ht[:, half, a, t * P:(t + 1) * P],
                                              w[:, k, 2 * C + h * HALF:2 * C + (h + 1) * HALF],
                                              start=(n == 0), stop=(n == len(PASSES) - 1))
                            i.then_inc(v_ready, 1)
                        chain_step(g, len(CHAIN_TILES) + t)

                groups(nc.tensor, body)
                pe.wait_ge(tail, 4)
                for k in range(NK):
                    i = pe.transpose(p_u[0:rows(k), k], ut[:, k * P:k * P + rows(k)], ident[0:R, 0:R])
                i.then_inc(u_turned, 1)
                for i in range(QR):
                    pe.wait_ge(qk_lo[i], START + (QKM // QR) * 2 * B)
                for b in range(B):
                    for h, (a, z) in enumerate(halves):
                        if b:
                            pe.wait_ge(ro_lo, 2 * (b - 1) + h + 1)
                        pe.matmul(pqk[0:R, h, 0:HALF], ex[:, b, 1], ut[:, a:z], start=True, stop=True) \
                          .then_inc(ro_ready, 1)


def stage_attention(nc, q_s, k_s, v_s, o_t, sums):
    KT = L // P
    LH = L // GT
    STEPS = LH * KT
    AHEAD = 5
    SLOTS = 4
    RING = 8
    SROWS, MROWS = 3 * D, 3 * D + 2
    VLO = 64
    ONES = D
    VW = VLO + D
    SCALE = float(D) ** -0.5
    MAX_STEP = (1, 3, 5, 7, 9, 11, 13, 14)
    TURN_STEP = STEPS - 1
    JOBS = KT + 1
    dve_lo = lambda s: s % 4 == 3
    NDVE = STEPS // 4
    NPOOL = STEPS - NDVE
    LOADS = 8
    with ExitStack() as ctx:
        sb = lambda n, s, d=F32: ctx.enter_context(nc.sbuf_tensor("a_" + n, s, d))
        ps = lambda n, s: ctx.enter_context(nc.psum_tensor("a_psum_" + n, s, F32))
        sem = stage_semaphores(nc, ctx, "a_")
        ident = sb("ident", [P, P])
        qs = sb("qs", [P, SLOTS, L], F32R)
        ks = sb("ks", [P, SLOTS, L], F32R)
        vs = sb("vs", [P, SLOTS, KT, VW], F32R)
        pf = sb("pf", [P, RING, GT])
        ph = sb("ph", [P, RING, GT], F32R)
        pl = sb("pl", [P, RING, GT], F32R)
        mx = sb("mx", [P, 2, KT])
        mxt = sb("mxt", [KT, 2, 2, P], F32R)
        ob = sb("ob", [VLO, LH, GT])
        p_s = ps("s", [P, 2, L])
        p_t = ps("t", [P, 2, GT])
        p_o = ps("o", [P, LH, GT])

        zeroed, ident_made = sem("zeroed"), sem("ident_made")
        first_set_up, set_up = sem("first_set_up"), sem("set_up")
        loaded = [sem(f"loaded{i}") for i in range(SLOTS)]
        max_in = [sem(f"max_in{i}") for i in range(SLOTS)]
        s_ready = sem("s_ready")
        s_free = [sem(f"s_free{i}") for i in range(2)]
        mxt_hi = sem("mxt_hi")
        t_ready = sem("t_ready")
        exp_done = [sem(f"exp_done{i}") for i in range(2)]
        hi_ready, lo_pool, lo_dve = sem("hi_ready"), sem("lo_pool"), sem("lo_dve")
        p_free = sem("p_free")
        hi_copied = sem("hi_copied")
        o_copied = [sem(f"o_copied{i}") for i in range(LH)]
        o_out = [sem(f"o_out{i}") for i in range(LH)]

        def heads(eng, body):
            n = NHEAD // SLOTS
            with eng.Fori(0, n - 1) as i:
                for u in range(SLOTS):
                    body(SLOTS * i + u, u, i, False)
            for u in range(SLOTS):
                body(SLOTS * (n - 1) + u, u, n - 1, True)

        def bank(u, job):
            return (JOBS * u + job) % 2

        def bank_uses(u, i, job):
            return JOBS * SLOTS // 2 * i + (JOBS * u + job) // 2

        def lo_counts(n_heads, s):
            d = sum(dve_lo(x) for x in range(s + 1))
            return NPOOL * n_heads + s + 1 - d, NDVE * n_heads + d

        with nc.Block() as block:
            @block.sync
            def _(sp):
                def load(hd, u):
                    for t, tile in ((q_s, qs), (k_s, ks)):
                        for r, s in enumerate((0, 1, 0) if t is q_s else (0, 0, 1)):
                            sp.dma_start(raw(tile[r * D:(r + 1) * D, u]),
                                         t[s, bass.ds(hd * D, D), :]).then_inc(loaded[u], 16)
                    for s, c in enumerate((0, VLO)):
                        sp.dma_start(raw(vs[:, u, :, c:c + D]),
                                     v_s[s, bass.ds(hd, 1)].rearrange("a (t p) d -> p (a t) d", p=P)) \
                          .then_inc(loaded[u], 16)

                def put_max(u, i):
                    sp.wait_ge(s_free[bank(u, KT)], bank_uses(u, i, KT) + 1)
                    for s in range(2):
                        sp.dma_start(raw(qs[SROWS + s:SROWS + s + 1, u]).rearrange("o (t c) -> o t c", c=P),
                                     raw(mxt[:, u % 2, s])).then_inc(max_in[u], 16)

                sp.wait_ge(first_set_up, 3)
                load(0, 0)
                sp.wait_ge(set_up, 3)
                for hd in range(1, SLOTS - 1):
                    load(hd, hd)
                put_max(0, 0)

                def body(hd, u, i, last):
                    if not (last and u > 0):
                        sp.wait_ge(p_free, RING + STEPS * hd)
                        load(hd + SLOTS - 1, (u + SLOTS - 1) % SLOTS)
                    if not (last and u == SLOTS - 1):
                        put_max((u + 1) % SLOTS, i + (u + 1) // SLOTS)
                    for lh in range(LH):
                        sp.wait_ge(o_copied[lh], START + hd + 1)
                        sp.dma_start(o_t[bass.ds(hd * D, D), lh * GT:(lh + 1) * GT], ob[0:D, lh]) \
                          .then_inc(o_out[lh], 16)
                        sp.dma_start(sums[bass.ds(hd, 1), lh * GT:(lh + 1) * GT], ob[ONES:ONES + 1, lh]) \
                          .then_inc(o_out[lh], 16)

                heads(nc.sync, body)
                for lh in range(LH):
                    sp.wait_ge(o_out[lh], START + 32 * NHEAD)

            @block.gpsimd
            def _(pool):
                make_identity(nc, pool, ident, zeroed, ident_made)
                pool.wait_ge(ident_made, 1)
                pool.memset(raw(ks[:, 0]), 1.0).then_inc(first_set_up, 1)
                pool.memset(raw(ks[:, 1:SLOTS]), 1.0).then_inc(set_up, 1)

                def body(hd, u, i, last):
                    for s in range(STEPS):
                        if not dve_lo(s):
                            pool.wait_ge(hi_ready, STEPS * hd + s + 1)
                            pool.tensor_tensor(pl[:, s % RING], pf[:, s % RING], raw(ph[:, s % RING]),
                                               ALU.subtract).then_inc(lo_pool, 1)

                heads(nc.gpsimd, body)

            @block.vector
            def _(dve):
                dve.memset(raw(qs[:, 0]), 1.0).then_inc(first_set_up, 1)
                dve.memset(raw(vs[:, 0]), 1.0).then_inc(first_set_up, 1)
                dve.memset(raw(qs[:, 1:SLOTS]), 1.0).then_inc(set_up, 1)
                dve.memset(raw(vs[:, 1:SLOTS]), 1.0).then_inc(set_up, 1)

                def max_tile(hd, u, t):
                    dve.wait_ge(s_ready, JOBS * hd + t + 1)
                    dve.tensor_reduce(mx[:, u % 2, t:t + 1], p_s[:, bank(u, t)], AX.X, ALU.max) \
                       .then_inc(s_free[bank(u, t)], 1)

                def turn_lo(hd, u):
                    dve.wait_ge(mxt_hi, hd + 1)
                    dve.scalar_tensor_tensor(mxt[:, u % 2, 1], p_s[0:KT, bank(u, KT), 0:P], -1.0,
                                             raw(mxt[:, u % 2, 0]), ALU.mult, ALU.subtract) \
                       .then_inc(s_free[bank(u, KT)], 1)

                def finish(hd, u, lh):
                    dve.wait_ge(p_free, RING + STEPS * hd + KT * (lh + 1))
                    dve.wait_ge(o_out[lh], START + 32 * hd)
                    dve.tensor_copy(ob[:, lh], p_o[0:VLO, lh]).then_inc(hi_copied, 1)
                    dve.wait_ge(hi_copied, LH * hd + lh + 1)
                    dve.tensor_tensor(ob[0:D, lh], p_o[VLO:VW, lh], ob[0:D, lh], ALU.add).then_inc(o_copied[lh], 1)

                for hd in range(2):
                    for t in range(KT):
                        max_tile(hd, hd, t)
                    if hd == 0:
                        turn_lo(0, 0)

                def body(hd, u, i, last):
                    for s in range(STEPS):
                        if s in MAX_STEP and not (last and u >= SLOTS - 2):
                            max_tile(hd + 2, (u + 2) % SLOTS, MAX_STEP.index(s))
                        if s == 2 and not (last and u == SLOTS - 1):
                            turn_lo(hd + 1, (u + 1) % SLOTS)
                        e = s + 3
                        if dve_lo(e):
                            dve.wait_ge(hi_ready, STEPS * hd + e + 1)
                            dve.tensor_tensor(pl[:, e % RING], pf[:, e % RING], raw(ph[:, e % RING]),
                                              ALU.subtract).then_inc(lo_dve, 1)
                        if s == KT + 1:
                            finish(hd, u, 0)
                    finish(hd, u, 1)

                heads(nc.vector, body)

            @block.scalar
            def _(act):
                set_start(act, o_out + max_in + o_copied)
                def turn_hi(hd, u, puts):
                    act.wait_ge(s_ready, JOBS * (hd + 1))
                    if puts is not None:
                        act.wait_ge(max_in[(u + 2) % SLOTS], START + 32 * puts)
                    act.activation(mxt[:, u % 2, 0], p_s[0:KT, bank(u, KT), 0:P], ACT.Copy, scale=-1.0) \
                       .then_inc(mxt_hi, 1)

                def exp(hd, s):
                    act.wait_ge(t_ready, STEPS * hd + s + 1)
                    act.wait_ge(p_free, STEPS * hd + s + 1)
                    act.activation(pf[:, s % RING], p_t[:, s % 2], ACT.Exp, scale=SCALE) \
                       .then_inc(exp_done[s % 2], 1)

                def high(hd, s):
                    act.wait_ge(exp_done[s % 2], (STEPS // 2) * hd + s // 2 + 1)
                    act.activation(ph[:, s % RING], pf[:, s % RING], ACT.Copy).then_inc(hi_ready, 1)

                turn_hi(0, 0, None)
                exp(0, 0)

                def body(hd, u, i, last):
                    for s in range(STEPS):
                        if s < STEPS - 1:
                            exp(hd, s + 1)
                        elif not (last and u == SLOTS - 1):
                            exp(hd + 1, 0)
                        high(hd, s)
                        if s == 3 and not (last and u == SLOTS - 1):
                            turn_hi(hd + 1, (u + 1) % SLOTS, i if u == 0 else i + 1)

                heads(nc.scalar, body)

            @block.tensor
            def _(pe):
                pe.sem_inc(p_free, RING)
                pe.wait_ge(ident_made, 1)

                def score_tile(u, i, t):
                    if t == 0:
                        pe.wait_ge(loaded[u], 16 * LOADS * (i + 1))
                    k = bank(u, t)
                    pe.wait_ge(s_free[k], bank_uses(u, i, t))
                    for h in range(L // 512):
                        m = pe.matmul(p_s[:, k, h * 512:(h + 1) * 512], qs[0:SROWS, u, t * P:(t + 1) * P],
                                      ks[0:SROWS, u, h * 512:(h + 1) * 512], start=True, stop=True)
                    m.then_inc(s_ready, 1)

                def turn(u, i):
                    k = bank(u, KT)
                    pe.wait_ge(s_free[1 - k], bank_uses(u, i, KT - 1) + 1)
                    pe.wait_ge(s_free[k], bank_uses(u, i, KT))
                    pe.transpose(p_s[0:KT, k, 0:P], mx[:, u % 2], ident[:]).then_inc(s_ready, 1)

                def scores(hd, u, i, s):
                    lh, t = divmod(s, KT)
                    if s == 0:
                        pe.wait_ge(max_in[u], START + 32 * (i + 1))
                    pe.wait_ge(exp_done[s % 2], (STEPS // 2) * hd + s // 2)
                    pe.matmul(p_t[:, s % 2], ks[0:MROWS, u, t * P:(t + 1) * P],
                              qs[0:MROWS, u, lh * GT:(lh + 1) * GT], start=True, stop=True) \
                      .then_inc(t_ready, 1)

                def values(hd, u, s):
                    lh, t = divmod(s, KT)
                    if t == 0:
                        pe.wait_ge(o_copied[lh], START + hd)
                    n_pool, n_dve = lo_counts(hd, s)
                    if dve_lo(s):
                        pe.wait_ge(lo_dve, n_dve)
                    else:
                        pe.wait_ge(lo_pool, n_pool)
                    out = p_o[0:VW, lh]
                    pe.matmul(out, vs[:, u, t], ph[:, s % RING], start=(t == 0), stop=False)
                    m = pe.matmul(out, vs[:, u, t], pl[:, s % RING], start=False, stop=(t == KT - 1))
                    m.then_inc(p_free, 1)

                for hd in range(2):
                    for t in range(KT):
                        score_tile(hd, 0, t)
                    turn(hd, 0)
                for s in range(AHEAD):
                    scores(0, 0, 0, s)

                def body(hd, u, i, last):
                    for s in range(STEPS):
                        if s + AHEAD < STEPS:
                            scores(hd, u, i, s + AHEAD)
                        elif not (last and u == SLOTS - 1):
                            scores(hd + 1, (u + 1) % SLOTS, i + (u == SLOTS - 1), s + AHEAD - STEPS)
                        values(hd, u, s)
                        if not (last and u >= SLOTS - 2):
                            nxt = ((u + 2) % SLOTS, i + (u + 2) // SLOTS)
                            if s in MAX_STEP:
                                score_tile(*nxt, MAX_STEP.index(s))
                            if s == TURN_STEP:
                                turn(*nxt)

                heads(nc.tensor, body)


def stage_proj(nc, o_t, sums, rsums, x, wproj, ada, mod, x2_s, h2_s):
    NK = FULL + 1
    NG = B * L // GT
    ORDER = (("product", 0), ("product", 1), ("operand", 0), ("product", 2), ("operand", 1), ("turn", 0),
             ("turn", 1), ("product", 3), ("operand", 2), ("turn", 2), ("operand", 3), ("turn", 3),
             ("operand", 4), ("turn", 4))
    with ExitStack() as ctx:
        sb = lambda n, s, d=F32: ctx.enter_context(nc.sbuf_tensor("p_" + n, s, d))
        ps = lambda n, s: ctx.enter_context(nc.psum_tensor("p_psum_" + n, s, F32))
        sem = stage_semaphores(nc, ctx, "p_")
        passed = sem("passed")
        w = sb("w", [P, W_TILES, C], F32R)
        ident = sb("ident", [P, P])
        heads = sb("heads", [H, C])
        sel = sb("sel", [H, CPAD], F32R)
        rs_flat = sb("rs_flat", [P, NHEAD * L // P])
        rs_f = sb("rs_f", [H, L])
        rs = sb("rs", [H, 2, 2, GT], F32R)
        ot = sb("ot", [P, NK, GT])
        of = sb("of", [P, NK, GT])
        oh = sb("oh", [P, 2, A_TILES, GT], F32R)
        xt = sb("xt", [P, 2, SUB, C])
        gt = sb("gt", [P, 2, 3, C])
        md = sb("md", [P, 2, len(MOD) * NK])
        x2 = sb("x2", [P, 2, SUB, C])
        xn = sb("xn", [P, SUB, CPAD])
        stats = sb("stats", [P, SUB, 2, 6])
        mv = sb("mv", [P, SUB, 2])
        small = sb("small", [P, 5, SUB])
        rstd = sb("rstd", [P, SUB])
        shift = sb("shift", [P, SUB])
        hf = sb("hf", [P, 2, GT])
        ht = sb("ht", [P, A_TILES, GT], F32R)
        p_r = ps("r", [P, 2, GT])
        p_p = ps("p", [P, 2, 2, 512])
        p_t = ps("t", [P, 2, GT])

        w_in, zeroed, ident_made, set_up = sem("w_in"), sem("zeroed"), sem("ident_made"), sem("set_up")
        sums_in, rs_made, rs_out = sem("sums_in"), sem("rs_made"), sem("rs_out")
        rs_in, rs_hi, rs_lo = sem("rs_in"), sem("rs_hi"), sem("rs_lo")
        o_in, r_ready, of_ready, oh_ready, ol_ready = (
            sem("o_in"), sem("r_ready"), sem("of_ready"), sem("oh_ready"), sem("ol_ready"))
        x_in = [sem(f"x_in{i}") for i in range(2)]
        md_in = [sem(f"md_in{i}") for i in range(2)]
        xb_ready, p_ready, gated, x2_ready = sem("xb_ready"), sem("p_ready"), sem("gated"), sem("x2_ready")
        link_done, var_ready, std_ready, rstd_ready = (
            sem("link_done"), sem("var_ready"), sem("std_ready"), sem("rstd_ready"))
        xn_ready, x2b_ready = sem("xn_ready"), sem("x2b_ready")
        x2b_out = [sem(f"x2b_out{i}") for i in range(2)]
        t_ready, hi_ready, full_ready, lo_ready = (
            sem("t_ready"), sem("hi_ready"), sem("full_ready"), sem("lo_ready"))
        h_out = [sem(f"h_out{c}") for c in range(NK)]

        def groups(eng, body):
            with eng.Fori(0, B - 1) as b:
                body(2 * b, b, 0, 2)
                body(2 * b + 1, b, 1, 2)
            body(NG - 2, B - 1, 0, 1)
            body(NG - 1, B - 1, 1, 0)

        with nc.Block() as block:
            @block.sync
            def _(sp):
                flat = "h (a n) -> (h a) n"
                sp.dma_start(rs_flat[:], sums.rearrange(flat, n=NHEAD * L // P)).then_inc(sums_in, 16)

                def load_x(g, b, half):
                    sp.dma_start(xt[:, half], x[bass.ds(g * GT, GT), :].rearrange("(t p) c -> p t c", p=P)) \
                      .then_inc(x_in[half], 16)
                    for i, s in enumerate((GATE_MSA, GB_PROJ)):
                        sp.dma_start(gt[:, half, i], ada[bass.ds(b, 1), s * C:(s + 1) * C].broadcast_to([P, C])) \
                          .then_inc(x_in[half], 16)

                def load_mod(b, half):
                    sp.dma_start(gt[:, half, 2], ada[bass.ds(b, 1), GB_FC2 * C:(GB_FC2 + 1) * C].broadcast_to([P, C])) \
                      .then_inc(md_in[half], 16)
                    sp.dma_start(md[:, half], mod[bass.ds(b, 1)].rearrange("a p n -> (a p) n")) \
                      .then_inc(md_in[half], 16)

                def load_o(g, b, half):
                    cols = slice(half * GT, (half + 1) * GT)
                    sp.dma_start(ot[:, 0:FULL], o_t[bass.ds(b * C, FULL * P), cols]
                                 .rearrange("(k p) n -> p k n", p=P)).then_inc(o_in, 16)
                    for r in range(2):
                        sp.dma_start(ot[r * REM:(r + 1) * REM, FULL], o_t[bass.ds(b * C + FULL * P, REM), cols]) \
                          .then_inc(o_in, 16)

                def load_rs(b, half):
                    sp.dma_start(rs_f[:, 0:GT], rsums[bass.ds(b * H, H), half * GT:(half + 1) * GT]).then_inc(o_in, 16)

                load_o(0, 0, 0)
                load_x(0, 0, 0)
                sp.wait_ge(rs_made, 1)
                sp.dma_start(rsums.rearrange(flat, n=NHEAD * L // P), rs_flat[:]).then_inc(rs_out, 16)
                sp.wait_ge(rs_out, 16)
                load_rs(0, 0)
                load_split_weight(sp, w, wproj, slice(0, C), w_in)
                load_mod(0, 0)
                sp.wait_ge(of_ready, NK)
                sp.wait_ge(rs_lo, 1)
                load_o(1, 0, 1)
                load_rs(0, 1)
                load_x(1, 0, 1)
                load_mod(0, 1)
                sp.wait_ge(of_ready, 2 * NK)
                sp.wait_ge(rs_lo, 2)
                load_o(2, 1, 0)
                load_rs(1, 0)

                def body(g, b, half, more):
                    if more >= 2:
                        sp.wait_ge(x2_ready, g + 1)
                        load_x(g + 2, b + 1, half)
                    sp.wait_ge(x2b_ready, g + 1)
                    sp.dma_start(x2_s[bass.ds(g * GT, GT), :].rearrange("(t p) c -> p t c", p=P), x2[:, half]) \
                      .then_inc(x2b_out[half], 16)
                    if more == 3:
                        sp.wait_ge(of_ready, NK * (g + 3))
                        sp.wait_ge(rs_lo, g + 3)
                        load_o(g + 3, b + 1 + half, 1 - half)
                        load_rs(b + 1 + half, 1 - half)
                    for c in range(NK):
                        sp.wait_ge(lo_ready, NK * g + c + 3)
                        sp.dma_start(h2_s[bass.ds(g, 1)].rearrange("a p (s k) n -> (a p) s k n", s=2)[:, :, c],
                                     raw(ht[:].rearrange("p (s k) n -> p s k n", s=2)[:, :, c])) \
                          .then_inc(h_out[c], 16)
                    if more >= 2:
                        load_mod(b + 1, half)

                with nc.sync.Fori(0, B - 2) as b:
                    body(2 * b, b, 0, 3)
                    body(2 * b + 1, b, 1, 3)
                for g in range(NG - 4, NG):
                    body(g, g // 2, g % 2, min(3, NG - 1 - g))
                for i in range(2):
                    sp.wait_ge(x2b_out[i], START + 16 * NG // 2)
                for c in range(NK):
                    sp.wait_ge(h_out[c], START + 16 * NG)

            @block.gpsimd
            def _(pool):
                make_identity(nc, pool, ident, zeroed, ident_made)
                pool.wait_ge(ident_made, 1)
                pool.memset(heads[:], 1.0).then_inc(set_up, 1)
                pool.wait_ge(set_up, 1)
                pool.affine_select(out=heads[:], in_=heads[:], compare_op=ALU.is_ge, fill=0.0, base=0,
                                   pattern=[[1, C]], channel_multiplier=-D).then_inc(set_up, 1)
                pool.wait_ge(set_up, 2)
                pool.affine_select(out=heads[:], in_=heads[:], compare_op=ALU.is_ge, fill=0.0, base=D - 1,
                                   pattern=[[-1, C]], channel_multiplier=D).then_inc(set_up, 1)

                def biased_x(g, b, half):
                    pool.wait_ge(x_in[half], 48 * (b + 1))
                    for t in range(SUB):
                        i = pool.tensor_tensor(xt[:, half, t], xt[:, half, t], gt[:, half, 1], ALU.add)
                    i.then_inc(xb_ready, 1)

                biased_x(0, 0, 0)
                biased_x(1, 0, 1)

                def body(g, b, half, more):
                    if not (isinstance(g, int) and g == 0):
                        pool.wait_ge(t_ready, START + NK * g)
                    wait_alone(pool, rstd_ready, g + 1, passed)
                    for t in range(SUB):
                        for a, z, o in ((0, C, 0), (FULL * P, C, C)):
                            i = pool.tensor_scalar(xn[:, t, o:o + z - a], x2[:, half, t, a:z],
                                                   rstd[:, t:t + 1], shift[:, t:t + 1], ALU.mult, ALU.add)
                    i.then_inc(xn_ready, 1)
                    pool.wait_ge(md_in[half], 32 * (b + 1))
                    pool.wait_ge(xn_ready, START + g + 1)
                    for t in range(SUB):
                        i = pool.tensor_tensor(x2[:, half, t], x2[:, half, t], gt[:, half, 2], ALU.add)
                    i.then_inc(x2b_ready, 1)
                    for c in range(NK):
                        if c == 2 and more == 2:
                            biased_x(g + 2, b + 1, half)
                        pool.wait_ge(full_ready, NK * g + c + 3)
                        pool.tensor_tensor(ht[:, NK + c], hf[:, c_slot(half, c)], raw(ht[:, c]), ALU.subtract) \
                            .then_inc(lo_ready, 1)

                groups(nc.gpsimd, body)

            @block.vector
            def _(dve):
                dve.sem_inc(lo_ready, 2)
                dve.wait_ge(sums_in, 16)
                dve.reciprocal(rs_flat[:], rs_flat[:]).then_inc(rs_made, 1)
                dve.wait_ge(set_up, 3)
                dve.tensor_copy(sel[:, 0:C], heads[:]).then_inc(set_up, 1)
                dve.tensor_copy(sel[:, C:CPAD], heads[:, FULL * P:C]).then_inc(set_up, 1)

                def sums_lo(g, half):
                    dve.wait_ge(rs_hi, g + 1)
                    dve.tensor_tensor(rs[:, half, 1], rs_f[:, 0:GT], raw(rs[:, half, 0]), ALU.subtract) \
                       .then_inc(rs_lo, 1)

                def operand(g, half, c):
                    dve.wait_ge(r_ready, NK * g + c + 1)
                    dve.tensor_tensor(of[:, c], ot[:, c], p_r[:, c_slot(half, c)], ALU.mult) \
                       .then_inc(of_ready, 1)

                def operand_lo(g, half, c):
                    dve.wait_ge(oh_ready, NK * g + c + 1)
                    dve.tensor_tensor(oh[:, half, NK + c], of[:, c], raw(oh[:, half, c]), ALU.subtract) \
                       .then_inc(ol_ready, 1)

                def gate(g, b, half, t, a):
                    if t == 0 and a == 0:
                        dve.wait_ge(xb_ready, g + 1)
                        if not (isinstance(g, int) and g < 2):
                            dve.wait_ge(x2b_out[half], START + 16 * b)
                    dve.wait_ge(p_ready, 2 * (SUB * g + t) + a + 1)
                    cols = slice(a * HALF, (a + 1) * HALF)
                    dve.tensor_tensor(x2[:, half, t, cols], p_p[:, t % 2, a, 0:HALF], gt[:, half, 0, cols],
                                      ALU.mult).then_inc(gated, 1)

                def residual(g, half, t):
                    dve.wait_ge(gated, 2 * (SUB * g + t) + 2)
                    i = dve.tensor_tensor(x2[:, half, t], x2[:, half, t], xt[:, half, t], ALU.add)
                    if t == SUB - 1:
                        i.then_inc(x2_ready, 1)

                LINKS = 7

                def statistics(g, half):
                    def link(ins, n):
                        ins.then_inc(link_done, 1)
                        dve.wait_ge(link_done, LINKS * g + n)

                    dve.wait_ge(x2_ready, g + 1)
                    for t in range(SUB):
                        for a in range(2):
                            i = dve.bn_stats(stats[:, t, a], x2[:, half, t, a * HALF:(a + 1) * HALF])
                    i.then_inc(link_done, 1)
                    wait_alone(dve, link_done, LINKS * g + 1, passed)
                    for t in range(SUB):
                        i = dve.bn_aggr(mv[:, t], stats[:, t].rearrange("p a s -> p (a s)"))
                    link(i, 2)
                    ve, std, r0, r2, cor = (small[:, k] for k in range(5))
                    dve.tensor_scalar(ve, mv[:, :, 1], LN_EPS, None, ALU.add).then_inc(var_ready, 1)
                    dve.wait_ge(std_ready, g + 1)
                    link(dve.reciprocal(r0, std), 3)
                    link(dve.tensor_tensor(r2, r0, r0, ALU.mult), 4)
                    link(dve.tensor_tensor(r2, r2, ve, ALU.mult), 5)
                    link(dve.tensor_scalar(cor, r2, -0.5, 1.5, ALU.mult, ALU.add), 6)
                    if not (isinstance(g, int) and g == 0):
                        dve.wait_ge(xn_ready, START + g)
                    link(dve.tensor_tensor(rstd[:], r0, cor, ALU.mult), 7)
                    dve.scalar_tensor_tensor(shift[:], mv[:, :, 0], -1.0, rstd[:], ALU.mult, ALU.mult) \
                       .then_inc(rstd_ready, 1)

                for g in range(2):
                    sums_lo(g, g)
                    for c in range(NK):
                        operand(g, g, c)
                        if c:
                            operand_lo(g, g, c - 1)
                    operand_lo(g, g, NK - 1)
                    if g == 0:
                        for t in range(SUB):
                            for a in range(2):
                                gate(0, 0, 0, t, a)
                            residual(0, 0, t)

                def body(g, b, half, more):
                    statistics(g, half)
                    if more == 2:
                        sums_lo(g + 2, half)
                    for what, n in ORDER:
                        if what == "product" and more >= 1:
                            for a in range(2):
                                gate(g + 1, b + half, 1 - half, n, a)
                            residual(g + 1, 1 - half, n)
                        if what == "operand" and more == 2:
                            operand(g + 2, half, n)
                            if n:
                                operand_lo(g + 2, half, n - 1)
                        if what == "turn":
                            dve.wait_ge(hi_ready, NK * g + n + 1)
                            dve.wait_ge(lo_ready, NK * g + n + 1)
                            k = 2 * NK + n
                            dve.tensor_scalar(hf[:, c_slot(half, n)], p_t[:, c_slot(half, n)],
                                              md[:, half, k + NK:k + NK + 1], md[:, half, k:k + 1],
                                              ALU.mult, ALU.add).then_inc(full_ready, 1)
                    if more == 2:
                        operand_lo(g + 2, half, NK - 1)

                groups(nc.vector, body)

            @block.scalar
            def _(act):
                set_start(act, [t_ready, xn_ready] + x2b_out + h_out)
                def sums_hi(g, half):
                    act.wait_ge(o_in, 64 * (g + 1))
                    if not (isinstance(g, int) and g < 2):
                        act.wait_ge(r_ready, NK * (g - 1))
                    act.activation(rs[:, half, 0], rs_f[:, 0:GT], ACT.Copy).then_inc(rs_hi, 1)

                def operand_hi(g, half, c):
                    if c == 0 and not (isinstance(g, int) and g < 2):
                        act.wait_ge(p_ready, 2 * SUB * (g - 1))
                    act.wait_ge(of_ready, NK * g + c + 1)
                    act.activation(oh[:, half, c], of[:, c], ACT.Copy).then_inc(oh_ready, 1)

                for g in range(2):
                    sums_hi(g, g)
                    for c in range(NK):
                        operand_hi(g, g, c)

                def body(g, b, half, more):
                    act.wait_ge(var_ready, g + 1)
                    act.activation(small[:, 1], small[:, 0], ACT.Sqrt).then_inc(std_ready, 1)
                    if more == 2:
                        sums_hi(g + 2, half)
                    act.wait_ge(md_in[half], 32 * (b + 1))
                    for what, n in ORDER:
                        if what == "operand" and more == 2:
                            operand_hi(g + 2, half, n)
                        if what == "turn":
                            act.wait_ge(h_out[n], START + 16 * g)
                            act.wait_ge(t_ready, START + NK * g + n + 1)
                            k = 2 * NK + n
                            act.activation(ht[:, n], p_t[:, c_slot(half, n)], ACT.Identity,
                                           bias=md[:, half, k:k + 1], scale=md[:, half, k + NK:k + NK + 1]) \
                               .then_inc(hi_ready, 1)

                groups(nc.scalar, body)

            @block.tensor
            def _(pe):
                def spread(g, half, c):
                    pe.wait_ge(rs_lo, g + 1)
                    if not (isinstance(g, int) and g == 0 and c < 2):
                        pe.wait_ge(of_ready, NK * g + c - 1)
                    for s in range(2):
                        i = pe.matmul(p_r[:, c_slot(half, c)], sel[:, c * P:(c + 1) * P], rs[:, half, s],
                                      start=(s == 0), stop=(s == 1))
                    i.then_inc(r_ready, 1)

                def project(g, half, t):
                    if t == 0:
                        pe.wait_ge(oh_ready, NK * (g + 1))
                        pe.wait_ge(ol_ready, NK * (g + 1))
                    for a in range(2):
                        if t >= 2 or not (isinstance(g, int) and g == 0):
                            pe.wait_ge(gated, 2 * (SUB * g + t - 2) + a + 1)
                        for n, (k, j) in enumerate(PASSES):
                            i = pe.matmul(p_p[:, t % 2, a, 0:HALF], oh[:, half, k, t * P:(t + 1) * P],
                                          w[:, j, a * HALF:(a + 1) * HALF],
                                          start=(n == 0), stop=(n == len(PASSES) - 1))
                        i.then_inc(p_ready, 1)

                pe.sem_inc(full_ready, 2)
                pe.wait_ge(ident_made, 1)
                pe.wait_ge(set_up, 5)
                for c in range(NK):
                    spread(0, 0, c)
                pe.wait_ge(w_in, 64)
                for t in range(SUB):
                    project(0, 0, t)
                for c in range(NK):
                    spread(1, 1, c)

                def body(g, b, half, more):
                    for what, n in ORDER:
                        if what == "product" and more >= 1:
                            project(g + 1, 1 - half, n)
                        if what == "operand" and more == 2:
                            spread(g + 2, half, n)
                        if what == "turn":
                            if n == 0:
                                pe.wait_ge(xn_ready, START + g + 1)
                            pe.wait_ge(full_ready, NK * g + n + 1)
                            for t in range(SUB):
                                i = pe.transpose(p_t[:, c_slot(half, n), t * P:(t + 1) * P],
                                                 xn[:, t, n * P:(n + 1) * P], ident[:])
                            i.then_inc(t_ready, 1)

                groups(nc.tensor, body)


def stage_mlp(nc, h2_s, x2_s, w1_s, b1, w2_s, gates, x3_s):
    FT = FF // P
    GM = GT // 2
    NT = GM // P
    NG = B * L // GM
    RING = 3
    AHEAD = 2
    PARTS = 9
    PF = FT // PARTS
    with ExitStack() as ctx:
        sb = lambda n, s, d=F32: ctx.enter_context(nc.sbuf_tensor("m_" + n, s, d))
        ps = lambda n, s: ctx.enter_context(nc.psum_tensor("m_psum_" + n, s, F32))
        sem = stage_semaphores(nc, ctx, "m_")
        w1 = sb("w1", [P, W_TILES, FF], F32R)
        w2 = sb("w2", [P, 2, FT, C], F32R)
        bias1 = sb("bias1", [P, FT])
        gt = sb("gt", [P, 2, C])
        ht = sb("ht", [P, 2, A_TILES, GM], F32R)
        af = sb("af", [P, RING, GM])
        ah = sb("ah", [P, RING, GM], F32R)
        al = sb("al", [P, RING, GM], F32R)
        xt = sb("xt", [P, NT, C])
        y = sb("y", [P, NT, C])
        p_h = ps("h", [P, RING, 512])
        p_y = ps("y", [P, NT, 2, 512])

        bias_in = sem("bias_in")
        w1_in = [sem(f"w1_in{i}") for i in range(PARTS)]
        w2_in = [sem(f"w2_in{i}") for i in range(PARTS)]
        ht_in = [sem(f"ht_in{i}") for i in range(2)]
        gt_in = [sem(f"gt_in{i}") for i in range(2)]
        x_in = [sem(f"x_in{i}") for i in range(NT)]
        h_ready, act_ready, hi_ready, lo_ready, used = (
            sem("h_ready"), sem("act_ready"), sem("hi_ready"), sem("lo_ready"), sem("used"))
        gated, summed = sem("gated"), sem("summed")
        y_out = [sem(f"y_out{i}") for i in range(NT)]

        def groups(eng, body):
            with eng.Fori(0, NG // 2 - 1) as j:
                body(2 * j, j, 0, False)
                body(2 * j + 1, j, 1, False)
            body(NG - 2, NG // 2 - 1, 0, False)
            body(NG - 1, NG // 2 - 1, 1, True)

        with nc.Block() as block:
            @block.sync
            def _(sp):
                def load_h(j, q):
                    sp.dma_start(raw(ht[:, q]), h2_s[bass.ds(j, 1), :, :, q * GM:(q + 1) * GM]
                                 .rearrange("a p k n -> (a p) k n")).then_inc(ht_in[q], 16)

                def load_gate(j, q):
                    sp.dma_start(gt[:, q], gates[bass.ds(j, 1), :].broadcast_to([P, C])).then_inc(gt_in[q], 16)

                def load_x(n, t):
                    sp.dma_start(xt[:, t], x2_s[bass.ds(n * GM + t * P, P), :]).then_inc(x_in[t], 16)

                sp.dma_start(bias1[:], b1.rearrange("(f p) -> p f", p=P),
                             allow_slow_non_contiguous=True).then_inc(bias_in, 16)
                load_h(0, 0)
                for i in range(PARTS):
                    cols = slice(i * PF * P, (i + 1) * PF * P)
                    load_split_weight(sp, w1[:, :, cols], w1_s, cols, w1_in[i])
                    for s in range(2):
                        sp.dma_start(raw(w2[:, s, i * PF:(i + 1) * PF]),
                                     w2_s[s, cols].rearrange("(f p) n -> p f n", p=P)).then_inc(w2_in[i], 16)
                load_h(0, 1)
                for q in range(2):
                    load_gate(0, q)
                for t in range(NT):
                    load_x(0, t)

                def body(n, j, q, last):
                    for t in range(NT):
                        sp.wait_ge(summed, NT * n + t + 1)
                        sp.dma_start(x3_s[bass.ds(n * GM + t * P, P), :], y[:, t]).then_inc(y_out[t], 16)
                        if not last:
                            load_x(n + 1, t)
                    if not (isinstance(n, int) and n >= NG - 2):
                        load_h(j + 1, q)
                        load_gate(j + 1, q)

                groups(nc.sync, body)
                for t in range(NT):
                    sp.wait_ge(y_out[t], START + 16 * NG)

            @block.scalar
            def _(act):
                set_start(act, [act_ready, gated] + y_out)
                act.wait_ge(bias_in, 16)

                def activate(n, f):
                    act.wait_ge(h_ready, FT * n + f + 1)
                    act.wait_ge(used, FT * n + f + 1)
                    act.activation(af[:, f % RING], p_h[:, f % RING, 0:GM], ACT.Gelu_apprx_tanh,
                                   bias=bias1[:, f:f + 1]).then_inc(act_ready, 1)

                def body(n, j, q, last):
                    for f in range(FT):
                        activate(n, f)

                groups(nc.scalar, body)

            @block.gpsimd
            def _(pool):
                def body(n, j, q, last):
                    for f in range(FT):
                        pool.wait_ge(hi_ready, FT * n + f + 1)
                        pool.tensor_tensor(al[:, f % RING], af[:, f % RING], raw(ah[:, f % RING]),
                                           ALU.subtract).then_inc(lo_ready, 1)

                groups(nc.gpsimd, body)

            @block.vector
            def _(dve):
                def high(n, f):
                    dve.wait_ge(act_ready, START + FT * n + f + 1)
                    dve.tensor_copy(ah[:, f % RING], af[:, f % RING]).then_inc(hi_ready, 1)

                for f in range(AHEAD):
                    high(0, f)

                def body(n, j, q, last):
                    for f in range(FT):
                        if f + AHEAD < FT:
                            high(n, f + AHEAD)
                        elif not last:
                            high(n + 1, f + AHEAD - FT)
                    dve.wait_ge(used, RING + FT * (n + 1))
                    dve.wait_ge(gt_in[q], 16 * (j + 1))
                    for t in range(NT):
                        dve.wait_ge(y_out[t], START + 16 * n)
                        for a in range(2):
                            cols = slice(a * HALF, (a + 1) * HALF)
                            dve.tensor_tensor(y[:, t, cols], p_y[:, t, a, 0:HALF], gt[:, q, cols],
                                              ALU.mult).then_inc(gated, 1)
                    for t in range(NT):
                        dve.wait_ge(x_in[t], 16 * (n + 1))
                        dve.wait_ge(gated, START + 2 * (NT * n + t) + 2)
                        dve.tensor_tensor(y[:, t], y[:, t], xt[:, t], ALU.add).then_inc(summed, 1)

                groups(nc.vector, body)

            @block.tensor
            def _(pe):
                pe.sem_inc(used, RING)

                def first(n, j, q, f):
                    if f == 0:
                        pe.wait_ge(ht_in[q], 16 * (j + 1))
                    if q == 0 and f % PF == 0:
                        pe.wait_ge(w1_in[f // PF], 64)
                    if not (isinstance(n, int) and n == 0 and f < RING):
                        pe.wait_ge(act_ready, START + FT * n + f + 1 - RING)
                    for i, (a, k) in enumerate(PASSES):
                        m = pe.matmul(p_h[:, f % RING, 0:GM], w1[:, k, f * P:(f + 1) * P], ht[:, q, a],
                                      start=(i == 0), stop=(i == len(PASSES) - 1))
                    m.then_inc(h_ready, 1)

                def second(n, q, f):
                    pe.wait_ge(lo_ready, FT * n + f + 1)
                    if q == 0 and f % PF == 0:
                        pe.wait_ge(w2_in[f // PF], 32)
                    for t in range(NT):
                        for a in range(2):
                            if f == 0:
                                pe.wait_ge(gated, START + 2 * NT * n)
                            for i, (part, s) in enumerate(((ah, 0), (al, 0), (ah, 1))):
                                m = pe.matmul(p_y[:, t, a, 0:HALF], part[:, f % RING, t * P:(t + 1) * P],
                                              w2[:, s, f, a * HALF:(a + 1) * HALF],
                                              start=(f == 0 and i == 0), stop=(f == FT - 1 and i == 2))
                    m.then_inc(used, 1)

                for f in range(AHEAD):
                    first(0, 0, 0, f)

                def body(n, j, q, last):
                    for f in range(FT):
                        if f + AHEAD < FT:
                            first(n, j, q, f + AHEAD)
                        elif not last:
                            first(n + 1, j + q, 1 - q, f + AHEAD - FT)
                        second(n, q, f)

                groups(nc.tensor, body)


def stage_rotate(nc, x3_s, u_s, rot_s, out):
    NK = FULL + 1
    NG = B * L // GT
    with ExitStack() as ctx:
        sb = lambda n, s, d=F32: ctx.enter_context(nc.sbuf_tensor("r_" + n, s, d))
        ps = lambda n, s: ctx.enter_context(nc.psum_tensor("r_psum_" + n, s, F32))
        sem = stage_semaphores(nc, ctx, "r_")
        ident = sb("ident", [P, P])
        u = sb("u", [P, NK, 2 * R], F32R)
        ro = sb("ro", [P, B, 2, C], F32R)
        xt = sb("xt", [P, NG, SUB, CPAD])
        xh = sb("xh", [P, 2, NK, GT], F32R)
        xl = sb("xl", [P, 2, NK, GT], F32R)
        z = sb("z", [P, 2, 2, GT], F32R)
        y = sb("y", [P, SUB, C])
        p_t = ps("t", [P, 2, GT])
        p_z = ps("z", [P, GT])
        p_y = ps("y", [P, 2, 2, 512])

        u_in, zeroed, ident_made = sem("u_in"), sem("zeroed"), sem("ident_made")
        x_in = [sem(f"x_in{g}") for g in range(NG)]
        ro_in = [sem(f"ro_in{b}") for b in range(B)]
        t_ready, hi_ready, lo_ready = sem("t_ready"), sem("hi_ready"), sem("lo_ready")
        z_ready, z_hi, z_lo = sem("z_ready"), sem("z_hi"), sem("z_lo")
        y_ready, summed = sem("y_ready"), sem("summed")
        y_out = [sem(f"y_out{t}") for t in range(SUB)]

        def groups(body):
            for g in range(NG):
                body(g, g % 2, g == NG - 1)

        with nc.Block() as block:
            @block.sync
            def _(sp):
                sp.dma_start(raw(u[:]), u_s).then_inc(u_in, 16)
                for g in range(NG):
                    rows = x3_s[g * GT:(g + 1) * GT].rearrange("(t p) c -> p t c", p=P)
                    sp.dma_start(xt[:, g, :, 0:C], rows).then_inc(x_in[g], 16)
                    sp.dma_start(xt[:, g, :, C:CPAD], rows[:, :, FULL * P:C]).then_inc(x_in[g], 16)
                    if g % 2 == 0:
                        for r in range(2):
                            sp.dma_start(raw(ro[r * R:(r + 1) * R, g // 2]), rot_s[g // 2]
                                         .rearrange("s r c -> r s c")).then_inc(ro_in[g // 2], 16)

                def body(g, half, last):
                    for t in range(SUB):
                        sp.wait_ge(summed, 2 * (SUB * g + t + 1))
                        sp.dma_start(out[g * GT + t * P:g * GT + (t + 1) * P], y[:, t]).then_inc(y_out[t], 16)

                groups(body)
                for t in range(SUB):
                    sp.wait_ge(y_out[t], 16 * NG)

            @block.gpsimd
            def _(pool):
                make_identity(nc, pool, ident, zeroed, ident_made)

            @block.scalar
            def _(act):
                def highs(g, half):
                    for c in range(NK):
                        act.wait_ge(t_ready, NK * g + c + 1)
                        if c == 0 and g >= 2:
                            act.wait_ge(z_ready, g - 1)
                        act.activation(xh[:, half, c], p_t[:, c_slot(half, c)], ACT.Copy).then_inc(hi_ready, 1)

                highs(0, 0)

                def body(g, half, last):
                    act.wait_ge(z_ready, g + 1)
                    act.wait_ge(y_ready, 2 * SUB * g)
                    act.activation(z[:, half, 0], p_z[:], ACT.Copy).then_inc(z_hi, 1)
                    if not last:
                        highs(g + 1, 1 - half)

                groups(body)

            @block.vector
            def _(dve):
                def lows(g, half):
                    for c in range(NK):
                        dve.wait_ge(hi_ready, NK * g + c + 1)
                        dve.tensor_tensor(xl[:, half, c], p_t[:, c_slot(half, c)], raw(xh[:, half, c]),
                                          ALU.subtract).then_inc(lo_ready, 1)

                lows(0, 0)

                def body(g, half, last):
                    dve.wait_ge(z_hi, g + 1)
                    dve.tensor_tensor(z[:, half, 1], p_z[:], raw(z[:, half, 0]), ALU.subtract).then_inc(z_lo, 1)
                    if not last:
                        lows(g + 1, 1 - half)
                    for t in range(SUB):
                        dve.wait_ge(y_out[t], 16 * g)
                        for a in range(2):
                            cols = slice(a * HALF, (a + 1) * HALF)
                            dve.wait_ge(y_ready, 2 * (SUB * g + t) + a + 1)
                            dve.tensor_tensor(y[:, t, cols], p_y[:, t % 2, a, 0:HALF], xt[:, g, t, cols],
                                              ALU.add).then_inc(summed, 1)

                groups(body)

            @block.tensor
            def _(pe):
                def transposes(g, half):
                    pe.wait_ge(x_in[g], 32)
                    for c in range(NK):
                        if NK * g + c >= 2:
                            pe.wait_ge(lo_ready, NK * g + c - 1)
                        for t in range(SUB):
                            i = pe.transpose(p_t[:, c_slot(half, c), t * P:(t + 1) * P],
                                             xt[:, g, t, c * P:(c + 1) * P], ident[:])
                        i.then_inc(t_ready, 1)

                pe.wait_ge(ident_made, 1)
                transposes(0, 0)
                pe.wait_ge(u_in, 16)

                def body(g, half, last):
                    pe.wait_ge(lo_ready, NK * (g + 1))
                    pe.wait_ge(z_lo, g)
                    n = 0
                    for part in (xh, xl):
                        for c in range(NK):
                            i = pe.matmul(p_z[:], u[:, c], part[:, half, c], start=(n == 0),
                                          stop=(n == 2 * NK - 1))
                            n += 1
                    i.then_inc(z_ready, 1)
                    if not last:
                        transposes(g + 1, 1 - half)
                    pe.wait_ge(z_lo, g + 1)
                    pe.wait_ge(ro_in[g // 2], 32)
                    for t in range(SUB):
                        for a in range(2):
                            if SUB * g + t >= 2:
                                pe.wait_ge(summed, 2 * (SUB * g + t - 2) + a + 1)
                            for n, (s, r) in enumerate(((0, 0), (1, 0), (0, 1))):
                                i = pe.matmul(p_y[:, t % 2, a, 0:HALF], z[:, half, s, t * P:(t + 1) * P],
                                              ro[:, g // 2, r, a * HALF:(a + 1) * HALF],
                                              start=(n == 0), stop=(n == 2))
                            i.then_inc(y_ready, 1)

                groups(body)


def stage_prepare(nc, cond, w_ada, b_ada, b_proj, b_fc2, w_qkv, wqkv_s, p_in, w_skew, b_skew, ada, mod, gates, state):
    NK = FULL + 1
    NT = 8
    WT = SEC * C // NT
    NV = 4
    TQ = 4
    TR = NSKEW // (NV * TQ)
    VT = TQ * TR
    A_RING = 3
    BLK = 1296
    RING = 3
    TERMS = 4
    s, d = flat_split(w_qkv, wqkv_s)
    blocks = [(s[:, i:i + BLK], d[:, :, i:i + BLK]) for i in range(0, C * 3 * C // P, BLK)]

    with ExitStack() as ctx:
        sb = lambda n, s, d=F32: ctx.enter_context(nc.sbuf_tensor("c_" + n, s, d))
        ps = lambda n, s: ctx.enter_context(nc.psum_tensor("c_psum_" + n, s, F32))
        sem = stage_semaphores(nc, ctx, "c_", reused=True)
        ident = sb("ident", [P, P])
        sct = sb("sct", [P, NK, B])
        wa = sb("wa", [P, A_RING, NK, WT])
        bb = sb("bb", [B, 2, C])
        cs = sb("cs", [B, 2, C])
        av = sb("av", [B, 8 * C])
        am = sb("am", [B, len(MOD), CPAD])
        mt = sb("mt", [P, B, len(MOD) * NK])
        wf = sb("wf", [P, RING, BLK])
        ws = sb("ws", [P, RING, 2, BLK], F32R)
        wr = sb("wr", [TR, 2, TQ, C])
        wt = sb("wt", [P, 2, FULL, VT])
        wl = sb("wl", [REM + 1, NSKEW])
        v = sb("v", [B, NSKEW])
        up = sb("up", [R, B, R])
        a2 = sb("a2", [R, B, R])
        sa = sb("sa", [R, B, 2, R])
        ts = sb("ts", [R, B, 2, R])
        pp = sb("pp", [P, NK, R])
        sel = sb("sel", [R, R, R])
        m, row, qt, neg, ex = (state[x] for x in ("m", "row", "qt", "neg", "ex"))
        upm = sb("upm", [R, R])
        col = sb("col", [R, 8])
        sq = sb("sq", [R, R])
        lst = sb("lst", [R, R])
        phi = sb("phi", [R, R])
        pt = sb("pt", [R, C])
        q = sb("q", [P, NK, R])
        p_w = ps("w", [P, 2, 512])
        p_v = ps("v", [P, 2, 512])
        p_b = ps("b", [R, 512])
        p_g = ps("g", [P, 512])
        p_s = ps("s", [R, B, 2, 2 * R])
        p_q = p_g[:, R:R + NK * R].rearrange("p (k n) -> p k n", n=R)
        p_m = p_v[:, 0, 0:len(MOD) * NK * B].rearrange("p (n b) -> p n b", b=B)
        p_c = p_v[:, 1, 0:NK * B].rearrange("p (k b) -> p k b", b=B)

        zeroed, ident_made, masks, set_up = sem("zeroed"), sem("ident_made"), sem("masks"), sem("set_up")
        c_in, b_in, pp_in, wl_in = sem("c_in"), sem("b_in"), sem("pp_in"), sem("wl_in")
        wr_in = [sem(f"wr_in{i}") for i in range(2)]
        wa_in = [sem(f"wa_in{i}") for i in range(A_RING)]
        silu_done, c_turned, sct_ready = sem("silu_done"), sem("c_turned"), sem("sct_ready")
        w_turned, wt_ready, v_ready, v_done, up_in = (
            sem("w_turned"), sem("wt_ready"), sem("v_ready"), sem("v_done"), sem("up_in"))
        bias_gated, am_ready, m_turned, mt_ready = (
            sem("bias_gated"), sem("am_ready"), sem("m_turned"), sem("mt_ready"))
        wf_in = [sem(f"wf_in{i}") for i in range(RING)]
        ws_out = [sem(f"ws_out{i}") for i in range(RING)]
        w_hi, w_lo = sem("w_hi"), sem("w_lo")
        pe_done, dve_done, act_done = sem("pe_done"), sem("dve_done"), sem("act_done")
        row_spread, step_done, out_done = sem("row_spread"), sem("step_done"), sem("out_done")
        rows = lambda k: P if k < FULL else REM
        halves = ((0, HALF), (HALF, C))

        PE_STEPS = ("gram", "p_turned", "l_turned", "q_ready", "q_turned", "gram2", "fix", "top", "a_turned") \
            + tuple(f"taylor{i}" for i in range(1, TERMS))
        DVE_STEPS = ("m_ready", "pt", "diag", "diag_sum", "inv_std", "scaled", "lst", "qt", "q", "phi0", "phi",
                     "qt2", "m2_ready", "a2", "sa", "y0") \
            + tuple(f"{x}{i}" for i in range(1, TERMS) for x in ("sum", "y"))
        pe_at = lambda name: PE_STEPS.index(name) + 1
        dve_at = lambda name: DVE_STEPS.index(name) + 1

        V_ORDER = [("v", h) for h in range(NV)] + [("a", n) for n in range(NT)]
        bank = lambda kind, n: V_ORDER.index((kind, n))
        fill = []
        for h in range(NV + 1):
            fill += [("turn", h, k) for k in range(NK)] if h < NV else []
            fill += [("v", h - 1, k) for k in range(NK)] if h else []
        fill += [("a", n, k) for n in range(NT) for k in range(NK)]

        with nc.Block() as block:
            @block.sync
            def _(sp):
                sp.dma_start(pp[:, 0:FULL], p_in[0:FULL * P].rearrange("(k p) n -> p k n", p=P)).then_inc(pp_in, 16)
                sp.dma_start(pp[0:REM, FULL], p_in[FULL * P:C]).then_inc(pp_in, 16)
                for j in range(RING):
                    sp.dma_start(wf[:, j], blocks[j][0]).then_inc(wf_in[j], 16)
                for j, (_, dst) in enumerate(blocks):
                    sp.wait_ge(w_lo, j + 1)
                    sp.dma_start(dst, raw(ws[:, j % RING])).then_inc(ws_out[j % RING], 16)
                    if j + RING < len(blocks):
                        sp.dma_start(wf[:, j % RING], blocks[j + RING][0]).then_inc(wf_in[j % RING], 16)
                sp.wait_ge(bias_gated, 2)
                sp.wait_ge(v_done, NV + NT)
                sp.dma_start(ada, av[:]).then_inc(out_done, 16)
                per = gates.shape[0] // B
                for i in range(per):
                    sp.dma_start(gates.rearrange("(b i) c -> b i c", i=per)[:, i],
                                 av[:, GATE_MLP * C:(GATE_MLP + 1) * C]).then_inc(out_done, 16)
                sp.wait_ge(mt_ready, 1)
                sp.dma_start(mod.rearrange("b p n -> p b n"), mt[:]).then_inc(out_done, 16)
                sp.wait_ge(out_done, 16 * (2 + per))
                for j in range(RING):
                    sp.wait_ge(ws_out[j], 16 * len(range(j, len(blocks), RING)))

            @block.gpsimd
            def _(pool):
                make_identity(nc, pool, ident, zeroed, ident_made)
                pool.wait_ge(ident_made, 1)
                pool.memset(neg[:], -1.0).then_inc(masks, 1)
                pool.memset(sq[:], 1.0).then_inc(masks, 1)
                pool.wait_ge(masks, 2)
                pool.affine_select(out=neg[:], in_=neg[:], compare_op=ALU.is_ge, fill=0.0, base=-1,
                                   pattern=[[-1, R]], channel_multiplier=1).then_inc(masks, 1)
                pool.affine_select(out=sq[:], in_=sq[:], compare_op=ALU.is_ge, fill=0.0, base=-1,
                                   pattern=[[1, R]], channel_multiplier=-1).then_inc(masks, 1)
                pool.memset(up[:], 0.0).then_inc(masks, 1)

                def low(j):
                    pool.wait_ge(w_hi, j + 1)
                    pool.tensor_tensor(ws[:, j % RING, 1], wf[:, j % RING], raw(ws[:, j % RING, 0]), ALU.subtract) \
                        .then_inc(w_lo, 1)

                for j in range(len(blocks)):
                    low(j)
                pool.wait_ge(v_done, NV + NT)
                pool.wait_ge(b_in, 32)
                for i, g in enumerate((GATE_MSA, GATE_MLP)):
                    pool.tensor_tensor(av[:, (SEC + i) * C:(SEC + i + 1) * C], av[:, g * C:(g + 1) * C], bb[:, i],
                                       ALU.mult).then_inc(bias_gated, 1)
                for i, s in enumerate(MOD):
                    one = 1.0 if s in (SCALE_MSA, SCALE_MLP) else 0.0
                    for a, z, o in ((0, C, 0), (FULL * P, C, C)):
                        pool.tensor_scalar(am[:, i, o:o + z - a], av[:, s * C + a:s * C + z], one, None, ALU.add) \
                            .then_inc(am_ready, 1)

            @block.scalar
            def _(act):
                def load_wr(h):
                    act.dma_start(wr[:, h % 2], w_skew[h * VT:(h + 1) * VT].rearrange("(t p) c -> p t c", p=TR)) \
                       .then_inc(wr_in[h % 2], 16)

                def load_wa(n):
                    cols = slice(n * WT, (n + 1) * WT)
                    s = n % A_RING
                    act.dma_start(wa[:, s, 0:FULL], w_ada[0:FULL * P, cols].rearrange("(k p) n -> p k n", p=P)) \
                       .then_inc(wa_in[s], 16)
                    act.dma_start(wa[0:REM, s, FULL], w_ada[FULL * P:C, cols]).then_inc(wa_in[s], 16)
                    act.dma_start(wa[REM:REM + 1, s, FULL], b_ada[cols].rearrange("(a n) -> a n", a=1)) \
                       .then_inc(wa_in[s], 16)

                def high(j):
                    act.wait_ge(wf_in[j % RING], 16 * (j // RING + 1))
                    act.wait_ge(ws_out[j % RING], 16 * (j // RING))
                    act.activation(ws[:, j % RING, 0], wf[:, j % RING], ACT.Copy).then_inc(w_hi, 1)

                row = lambda x: x.rearrange("(a n) -> a n", a=1)
                act.dma_start(cs[:, 0], cond).then_inc(c_in, 16)
                for h in range(2):
                    load_wr(h)
                act.dma_start(wl[REM:REM + 1], row(b_skew)).then_inc(wl_in, 16)
                for n in range(A_RING):
                    load_wa(n)
                act.dma_start(bb[:, 0], row(b_proj).broadcast_to([B, C])).then_inc(b_in, 16)
                act.dma_start(bb[:, 1], row(b_fc2).broadcast_to([B, C])).then_inc(b_in, 16)
                act.wait_ge(c_in, 16)
                act.activation(cs[:, 1], cs[:, 0], ACT.Silu).then_inc(silu_done, 1)
                turned, block_no = 0, 0
                for kind, n, k in fill:
                    if kind == "turn":
                        act.wait_ge(w_turned, turned + 1)
                        if n >= 2:
                            act.wait_ge(v_ready, n - 1)
                        dst = wt[:, n % 2, k] if k < FULL else wl[0:REM, n * VT:(n + 1) * VT]
                        act.activation(dst, p_w[0:rows(k), turned % 2, 0:VT], ACT.Copy).then_inc(wt_ready, 1)
                        turned += 1
                        if k == NK - 1 and n + 2 < NV:
                            load_wr(n + 2)
                    elif k == NK - 1:
                        i = bank(kind, n)
                        act.wait_ge(v_ready, i + 1)
                        dst, w = (v[:, n * VT:(n + 1) * VT], VT) if kind == "v" else (av[:, n * WT:(n + 1) * WT], WT)
                        act.activation(dst, p_v[0:B, i % 2, 0:w], ACT.Copy).then_inc(v_done, 1)
                        if kind == "a" and n + A_RING < NT:
                            load_wa(n + A_RING)
                        if kind == "a":
                            if n == 0:
                                act.wait_ge(masks, 5)
                                act.wait_ge(v_done, NV)
                            for r in range(n * R // (NT - 1), min((n + 1) * R // (NT - 1), R - 1)):
                                off = r * (R - 1) - r * (r - 1) // 2
                                act.dma_start(up[r:r + 1, :, r + 1:R], v[:, off:off + R - 1 - r],
                                              allow_slow_non_contiguous=True).then_inc(up_in, 16)
                        if block_no < len(blocks):
                            high(block_no)
                            block_no += 1
                act.wait_ge(dve_done, dve_at("diag_sum"))
                act.activation(col[:, 1:2], col[:, 0:1], ACT.Sqrt).then_inc(act_done, 1)
                act.wait_ge(m_turned, 1)
                act.activation(mt[:].rearrange("p b n -> p n b"), p_m, ACT.Copy).then_inc(mt_ready, 1)

            @block.vector
            def _(dve):
                at = [0]

                def step(ins, name):
                    assert DVE_STEPS[at[0]] == name
                    at[0] += 1
                    ins.then_inc(dve_done, 1)
                    dve.wait_ge(dve_done, at[0])

                dve.memset(sct[:, FULL], 1.0).then_inc(set_up, 1)
                dve.wait_ge(ident_made, 1)
                dve.tensor_copy(sel[:], ident[0:R, 0:R].rearrange("p (j o) -> p j o", o=1).broadcast_to([R, R, R])) \
                   .then_inc(set_up, 1)
                dve.tensor_copy(m[:, R:2 * R], ident[0:R, 0:R]).then_inc(set_up, 1)
                dve.wait_ge(set_up, 3)
                dve.wait_ge(c_turned, 1)
                dve.tensor_copy(sct[:, 0:FULL], p_c[:, 0:FULL]).then_inc(sct_ready, 1)
                dve.tensor_copy(sct[0:REM, FULL], p_c[0:REM, FULL]).then_inc(sct_ready, 1)
                dve.wait_ge(masks, 5)
                dve.scalar_tensor_tensor(upm[:], ident[0:R, 0:R], 0.5, sq[:], ALU.mult, ALU.add).then_inc(set_up, 1)
                dve.wait_ge(set_up, 4)
                dve.wait_ge(pe_done, pe_at("gram"))
                step(dve.tensor_copy(m[:, 0:R], p_g[0:R, 0:R]), "m_ready")
                dve.wait_ge(pe_done, pe_at("p_turned"))
                dve.tensor_copy(pt[:, 0:512], p_w[0:R, 0]).then_inc(set_up, 1)
                step(dve.tensor_copy(pt[:, 512:C], p_w[0:R, 1, 0:C - 512]), "pt")

                for j in range(R):
                    dve.wait_ge(row_spread, j + 1)
                    dve.reciprocal(col[:, 4:5], p_b[:, j:j + 1]).then_inc(step_done, 1)
                    dve.wait_ge(step_done, 3 * j + 1)
                    dve.scalar_tensor_tensor(col[:, 5:6], m[:, j:j + 1], col[:, 4:5], neg[:, j:j + 1],
                                             ALU.mult, ALU.mult).then_inc(step_done, 1)
                    dve.wait_ge(step_done, 3 * j + 2)
                    dve.scalar_tensor_tensor(m[:, j + 1:R + j + 1], p_b[:, j + 1:R + j + 1], col[:, 5:6],
                                             m[:, j + 1:R + j + 1], ALU.mult, ALU.add).then_inc(step_done, 1)
                    dve.wait_ge(step_done, 3 * j + 3)
                step(dve.tensor_tensor(sq[:], m[:, 0:R], ident[0:R, 0:R], ALU.mult), "diag")
                step(dve.tensor_reduce(col[:, 0:1], sq[:], AX.X, ALU.add), "diag_sum")
                dve.wait_ge(act_done, 1)
                step(dve.reciprocal(col[:, 2:3], col[:, 1:2]), "inv_std")
                step(dve.tensor_scalar(sq[:], m[:, R:2 * R], col[:, 2:3], None, ALU.mult), "scaled")
                dve.wait_ge(pe_done, pe_at("l_turned"))
                step(dve.tensor_copy(lst[:], p_g[0:R, 0:R]), "lst")
                dve.wait_ge(pe_done, pe_at("q_ready"))
                dve.tensor_copy(qt[:, 0:HALF], p_w[0:R, 0, 0:HALF]).then_inc(set_up, 1)
                step(dve.tensor_copy(qt[:, HALF:C], p_w[0:R, 1, 0:HALF]), "qt")
                dve.wait_ge(pe_done, pe_at("q_turned"))
                dve.tensor_copy(q[:, 0:FULL], p_q[:, 0:FULL]).then_inc(set_up, 1)
                step(dve.tensor_copy(q[0:REM, FULL], p_q[0:REM, FULL]), "q")
                dve.wait_ge(pe_done, pe_at("gram2"))
                step(dve.tensor_tensor(phi[:], p_g[0:R, 0:R], ident[0:R, 0:R], ALU.subtract), "phi0")
                step(dve.tensor_tensor(phi[:], phi[:], upm[:], ALU.mult), "phi")
                dve.wait_ge(pe_done, pe_at("fix"))
                dve.tensor_tensor(qt[:, 0:HALF], qt[:, 0:HALF], p_w[0:R, 0, 0:HALF], ALU.subtract).then_inc(set_up, 1)
                step(dve.tensor_tensor(qt[:, HALF:C], qt[:, HALF:C], p_w[0:R, 1, 0:HALF], ALU.subtract), "qt2")
                dve.wait_ge(set_up, 8)
                dve.wait_ge(pe_done, pe_at("top"))
                step(dve.tensor_copy(m[:, 0:R], p_g[0:R, 0:R]), "m2_ready")
                dve.tensor_scalar(row[:], m[:], ident[0:R, 0:1], None, ALU.mult)

                dve.wait_ge(pe_done, pe_at("a_turned"))
                step(dve.tensor_tensor(a2[:], up[:], p_s[:, :, 0, 0:R], ALU.subtract), "a2")
                scale = 2.0 ** -SQUARINGS
                dve.tensor_scalar(sa[:, :, 1], a2[:], -scale, None, ALU.mult).then_inc(set_up, 1)
                step(dve.tensor_scalar(sa[:, :, 0], a2[:], scale, None, ALU.mult), "sa")
                dve.wait_ge(set_up, 9)
                step(dve.tensor_scalar(ex[:], sa[:], 1.0 / TERMS, None, ALU.mult), "y0")
                for i in range(1, TERMS):
                    dve.wait_ge(pe_done, pe_at(f"taylor{i}"))
                    step(dve.tensor_tensor(ts[:], p_s[:, :, :, 0:R], sa[:], ALU.add), f"sum{i}")
                    step(dve.tensor_scalar(ex[:], ts[:], 1.0 / (TERMS - i), None, ALU.mult), f"y{i}")

            @block.tensor
            def _(pe):
                at = [0]

                def step(ins, name):
                    assert PE_STEPS[at[0]] == name
                    at[0] += 1
                    ins.then_inc(pe_done, 1)

                def gram(x, name):
                    for k in range(NK):
                        i = pe.matmul(p_g[0:R, 0:R], x[0:rows(k), k], x[0:rows(k), k], start=(k == 0),
                                      stop=(k == NK - 1))
                    step(i, name)

                def turn_rows(x, name):
                    for k in range(NK):
                        i = pe.transpose(p_q[0:rows(k), k], x[:, k * P:k * P + rows(k)], ident[0:R, 0:R])
                    step(i, name)

                turned = [0]

                def filling(kind, n, k):
                    if kind == "turn":
                        if k == 0:
                            pe.wait_ge(wr_in[n % 2], 16 * (n // 2 + 1))
                        if turned[0] >= 2:
                            pe.wait_ge(wt_ready, turned[0] - 1)
                        for t in range(TQ):
                            i = pe.transpose(p_w[0:rows(k), turned[0] % 2, t * TR:(t + 1) * TR],
                                             wr[:, n % 2, t, k * P:k * P + rows(k)], ident[0:TR, 0:TR])
                        i.then_inc(w_turned, 1)
                        turned[0] += 1
                        return
                    i = bank(kind, n)
                    if k == 0:
                        if kind == "v":
                            pe.wait_ge(wt_ready, NK * (n + 1))
                            pe.wait_ge(wl_in, 16)
                        else:
                            pe.wait_ge(wa_in[n % A_RING], 48 * (n // A_RING + 1))
                        if i >= 2:
                            pe.wait_ge(v_done, i - 1)
                    r = P if k < FULL else REM + 1
                    if kind == "a":
                        w, rhs = WT, wa[0:r, n % A_RING, k]
                    else:
                        w, rhs = VT, wt[:, n % 2, k] if k < FULL else wl[:, n * VT:(n + 1) * VT]
                    x = pe.matmul(p_v[0:B, i % 2, 0:w], sct[0:r, k], rhs, start=(k == 0), stop=(k == NK - 1))
                    if k == NK - 1:
                        x.then_inc(v_ready, 1)

                pe.wait_ge(ident_made, 1)
                pe.wait_ge(pp_in, 32)
                gram(pp, "gram")
                for k in range(NK):
                    i = pe.transpose(p_w[0:R, k // 4, k % 4 * P:k % 4 * P + rows(k)], pp[0:rows(k), k],
                                     ident[0:rows(k), 0:rows(k)])
                step(i, "p_turned")
                pe.wait_ge(silu_done, 1)
                for k in range(NK):
                    i = pe.transpose(p_c[0:rows(k), k], cs[:, 1, k * P:k * P + rows(k)], ident[0:B, 0:B])
                i.then_inc(c_turned, 1)
                pe.wait_ge(dve_done, dve_at("pt"))
                pe.wait_ge(sct_ready, 2)
                pe.wait_ge(set_up, 4)
                for j in range(R):
                    if j:
                        pe.wait_ge(step_done, 3 * j)
                    pe.matmul(p_b[:, 0:2 * R], sel[:, j], m[:], start=True, stop=True).then_inc(row_spread, 1)
                    for f in fill[j * len(fill) // R:(j + 1) * len(fill) // R]:
                        filling(*f)
                pe.wait_ge(dve_done, dve_at("scaled"))
                step(pe.transpose(p_g[0:R, 0:R], sq[:], ident[0:R, 0:R]), "l_turned")
                pe.wait_ge(dve_done, dve_at("lst"))
                for h, (a, z) in enumerate(halves):
                    i = pe.matmul(p_w[0:R, h, 0:HALF], lst[:], pt[:, a:z], start=True, stop=True)
                step(i, "q_ready")
                pe.wait_ge(dve_done, dve_at("qt"))
                turn_rows(qt, "q_turned")
                pe.wait_ge(dve_done, dve_at("q"))
                gram(q, "gram2")
                pe.wait_ge(dve_done, dve_at("phi"))
                for h, (a, z) in enumerate(halves):
                    i = pe.matmul(p_w[0:R, h, 0:HALF], phi[:], qt[:, a:z], start=True, stop=True)
                step(i, "fix")
                pe.wait_ge(dve_done, dve_at("qt2"))
                step(pe.transpose(p_g[0:R, 0:R], qt[:, 0:R], ident[0:R, 0:R]), "top")

                pe.wait_ge(up_in, 16 * (R - 1))
                for b in range(B):
                    i = pe.transpose(p_s[:, b, 0, 0:R], up[:, b], ident[0:R, 0:R])
                step(i, "a_turned")
                for t in range(1, TERMS):
                    pe.wait_ge(dve_done, dve_at("y0" if t == 1 else f"y{t - 1}"))
                    for b in range(B):
                        for s in range(2):
                            i = pe.matmul(p_s[:, b, s, 0:R], sa[:, b, 1 - s], ex[:, b, s], start=True, stop=True)
                    step(i, f"taylor{t}")
                pe.wait_ge(am_ready, 2 * len(MOD))
                for i in range(len(MOD)):
                    for k in range(NK):
                        t = pe.transpose(p_m[:, i * NK + k], am[:, i, k * P:(k + 1) * P], ident[0:B, 0:B])
                t.then_inc(m_turned, 1)


def build(nc, x, cond, w_qkv, b_qkv, w_proj, b_proj, w_fc1, b_fc1, w_fc2, b_fc2, w_ada, b_ada, p_in, w_skew, b_skew,
          out):
    scratch = lambda name, *shape: nc.dram_tensor(name, shape, F32, kind="Internal").ap()
    wqkv_s = scratch("wqkv_s", 2, C, 3 * C)
    wproj_s = scratch("wproj_s", 2, C, C)
    w1_s = scratch("w1_s", 2, C, FF)
    w2_s = scratch("w2_s", 2, FF, C)
    ada = scratch("ada", B, 8 * C)
    mod = scratch("mod", B, P, len(MOD) * (FULL + 1))
    gates = scratch("gates", B * L // GT, C)
    u_s = scratch("u_s", P, FULL + 1, 2 * R)
    rot_s = scratch("rot_s", B, 2, R, C)
    q_s = scratch("q_s", 2, NHEAD * D, L)
    k_s = scratch("k_s", 2, NHEAD * D, L)
    v_s = scratch("v_s", 2, NHEAD, L, D)
    o_t = scratch("o_t", NHEAD * D, L)
    sums = scratch("sums", NHEAD, L)
    rsums = scratch("rsums", NHEAD, L)
    x2_s = scratch("x2_s", B * L, C)
    h2_s = scratch("h2_s", B * L // GT, P, A_TILES, GT)
    x3_s = scratch("x3_s", B * L, C)
    x_rows = x.rearrange("b t c -> (b t) c")
    out_rows = out.rearrange("b t c -> (b t) c")
    with ExitStack() as ctx:
        state = chain_state(nc, ctx)
        stage_prepare(nc, cond, w_ada, b_ada, b_proj, b_fc2, w_qkv, wqkv_s, p_in, w_skew, b_skew, ada, mod, gates,
                      state)
        stage_qkv(nc, x_rows, b_qkv, wqkv_s, mod, q_s, k_s, v_s,
                  [(w_proj, wproj_s), (w_fc1, w1_s), (w_fc2, w2_s)], state, u_s, rot_s)
    stage_attention(nc, q_s, k_s, v_s, o_t, sums)
    stage_proj(nc, o_t, sums, rsums, x_rows, wproj_s, ada, mod, x2_s, h2_s)
    stage_mlp(nc, h2_s, x2_s, w1_s, b_fc1, w2_s, gates, x3_s)
    stage_rotate(nc, x3_s, u_s, rot_s, out_rows)


_INS = ("x", "cond_1152", "L0_cond_W_qkv", "L0_cond_b_qkv", "L0_cond_W_proj", "L0_cond_b_proj", "L0_cond_W_fc1",
        "L0_cond_b_fc1", "L0_cond_W_fc2", "L0_cond_b_fc2", "L0_cond_W_ada", "L0_cond_b_ada", "L1_cond_P",
        "L1_cond_W", "L1_cond_b")
_OUTS = [((B, L, C), "float32")]


def kernel(**inputs):
    import numpy as _np
    import concourse.bacc as _bacc
    from concourse import mybir as _mybir
    from concourse.bass_utils import run_bass_kernel_spmd as _run

    nc = _bacc.Bacc("TRN2", target_bir_lowering=False, num_devices=1)
    arrays, args = {}, []
    for name in _INS:
        a = _np.ascontiguousarray(inputs[name])
        arrays[f"in_{name}_dram"] = a
        args.append(nc.dram_tensor(f"in_{name}_dram", a.shape, _mybir.dt.from_np(a.dtype), kind="ExternalInput").ap())
    for i, (shape, dtype) in enumerate(_OUTS):
        dt = _mybir.dt.from_np(_np.dtype(dtype))
        args.append(nc.dram_tensor(f"out_{i}_dram", shape, dt, kind="ExternalOutput").ap())
    build(nc, *args)
    r = _run(nc, [arrays], core_ids=[0])
    return r.results[0]["out_0_dram"]
```
